# Optimizing a Trainium2 kernel written in Bass

```python
import numpy as np
import jax
import jax.numpy as jnp

def _softmax(x, axis=-1):
    return jax.nn.softmax(x, axis=axis)

def _gelu(x):
    return jax.nn.gelu(x, approximate=True)

def _silu(x):
    return jax.nn.silu(x)

def _sigmoid(x):
    return jax.nn.sigmoid(x)

def _layernorm(x, axis=-1, eps=1e-05):
    m = jnp.mean(x, axis=axis, keepdims=True)
    v = jnp.var(x, axis=axis, keepdims=True)
    return (x - m) / jnp.sqrt(v + eps)

def _scatter_add(tgt, idx, src, axis=0):
    return tgt.at[idx].add(src)

def _segment_sum(src, seg, n):
    return jax.ops.segment_sum(src, seg, n)
kernel_name = 'mk_adj_ffn_d2_adj_r2_74f5d0'

def setup_inputs(seed: int=0):
    np.random.seed(seed)
    _w = jnp.asarray

    def _rec_inputs():
        import jax
        import jax.numpy as jnp
        _gk = jax.random.key(seed)
        x = -0.001003 + 1 * jax.random.normal(jax.random.fold_in(_gk, 1), (4096, 128), jnp.float32)
        _a = jax.random.bernoulli(jax.random.fold_in(_gk, 2), 0.00390625, (4096, 4096))
        _af = _a.astype(jnp.float32)
        _af = _af * jax.random.uniform(jax.random.fold_in(_gk, 3), (4096, 4096), jnp.float32, 0.05, 0.999999)
        adj = _af
        return (x, adj)
    x, adj = _rec_inputs()

    def _L0_gnn_setup():
        import jax, jax.numpy as jnp
        import numpy as np
        N = 3072
        HID = 128
        T = 350
        DENSITY = 0.05
        key = jax.random.key(seed)
        k1, k2, k3, k4, k5, k6 = jax.random.split(key, 6)
        h = jax.random.normal(k1, (N, HID), dtype=jnp.float32)
        a = jax.random.uniform(k2, (N, N), dtype=jnp.float32)
        mask = jax.random.uniform(k3, (N, N)) < DENSITY
        adj = jnp.where(mask, a, 0.0)
        simlar = jax.random.normal(k4, (N, N), dtype=jnp.float32)
        s = 1.0 / np.sqrt(HID)
        W_proj = jax.random.uniform(k5, (HID, HID), minval=-s, maxval=s, dtype=jnp.float32)
        b_proj = jnp.zeros((HID,), dtype=jnp.float32)
        W_gcn = jax.random.uniform(k6, (HID, HID), minval=-s, maxval=s, dtype=jnp.float32)
        b_gcn = jnp.zeros((HID,), dtype=jnp.float32)
        return {'h': h, 'adj': adj, 'simlar': simlar, 'W_proj': W_proj, 'b_proj': b_proj, 'W_gcn': W_gcn, 'b_gcn': b_gcn}
    _L0_gnn_all = _L0_gnn_setup()
    _L0_gnn_in = {k: v for k, v in _L0_gnn_all.items() if k in ('W_proj', 'b_proj', 'W_gcn', 'b_gcn')}
    del _L0_gnn_all

    def _L0_ffn_setup():
        import jax, jax.numpy as jnp
        import numpy as np
        B, S, D, F, E, K = (8, 1024, 128, 512, 8, 2)
        key = jax.random.key(seed)
        ks = jax.random.split(key, 10)
        s = 0.02
        return {'x': jax.random.normal(ks[0], (B, S, D), dtype=jnp.float32), 'Wr': jax.random.normal(ks[1], (D, E), dtype=jnp.float32) * s, 'W1s': jax.random.normal(ks[2], (D, F), dtype=jnp.float32) * s, 'b1s': jnp.zeros((F,), dtype=jnp.float32), 'W2s': jax.random.normal(ks[3], (F, D), dtype=jnp.float32) * s, 'b2s': jnp.zeros((D,), dtype=jnp.float32), 'W1p': jax.random.normal(ks[4], (E, D, F), dtype=jnp.float32) * s, 'b1p': jnp.zeros((E, F), dtype=jnp.float32), 'W2p': jax.random.normal(ks[5], (E, F, D), dtype=jnp.float32) * s, 'b2p': jnp.zeros((E, D), dtype=jnp.float32)}
    _L0_ffn_all = _L0_ffn_setup()
    _L0_ffn_in = {k: v for k, v in _L0_ffn_all.items() if k in ('Wr', 'W1s', 'b1s', 'W2s', 'b2s', 'W1p', 'b1p', 'W2p', 'b2p')}
    del _L0_ffn_all

    def _L1_gnn_setup():
        import jax, jax.numpy as jnp
        import numpy as np
        N, IN_FEAT, OUT_FEAT, H = (2048, 128, 128, 8)
        D = OUT_FEAT // H
        ADJ_DENSITY = 0.05
        key = jax.random.key(seed)
        kx, kw, kb, ka, kadj = jax.random.split(key, 5)
        x = jax.random.normal(kx, (N, IN_FEAT), dtype=jnp.float32)
        W = jax.random.normal(kw, (OUT_FEAT, IN_FEAT), dtype=jnp.float32) * (1.0 / np.sqrt(IN_FEAT))
        b = jax.random.normal(kb, (OUT_FEAT,), dtype=jnp.float32) * 0.01
        a = jax.random.normal(ka, (H, 2 * D), dtype=jnp.float32)
        adj_matrix = jax.random.bernoulli(kadj, ADJ_DENSITY, (N, N)).astype(jnp.float32)
        return {'x': x, 'W': W, 'b': b, 'a': a, 'adj_matrix': adj_matrix}
    _L1_gnn_all = _L1_gnn_setup()
    _L1_gnn_in = {k: v for k, v in _L1_gnn_all.items() if k in ('W', 'b', 'a')}
    del _L1_gnn_all

    def _L1_ffn_setup():
        import jax, jax.numpy as jnp
        import numpy as np
        N_EXPERTS = 8
        TOP_K = 2
        key = jax.random.key(seed)
        ks = jax.random.split(key, 5)
        B, T, C, E, H = (8, 1024, 128, 8, 341)
        scale = 1.0 / np.sqrt(C)
        return {'x': jax.random.normal(ks[0], (B, T, C), dtype=jnp.float32), 'router_w': jax.random.normal(ks[1], (E, C), dtype=jnp.float32) * scale, 'w1': jax.random.normal(ks[2], (E, H, C), dtype=jnp.float32) * scale, 'w2': jax.random.normal(ks[3], (E, C, H), dtype=jnp.float32) * (1.0 / np.sqrt(H)), 'w3': jax.random.normal(ks[4], (E, H, C), dtype=jnp.float32) * scale}
    _L1_ffn_all = _L1_ffn_setup()
    _L1_ffn_in = {k: v for k, v in _L1_ffn_all.items() if k in ('router_w', 'w1', 'w2', 'w3')}
    del _L1_ffn_all
    return {'x': x, 'adj': adj, 'L0_gnn_W_proj': _L0_gnn_in['W_proj'], 'L0_gnn_b_proj': _L0_gnn_in['b_proj'], 'L0_gnn_W_gcn': _L0_gnn_in['W_gcn'], 'L0_gnn_b_gcn': _L0_gnn_in['b_gcn'], 'L0_ffn_Wr': _L0_ffn_in['Wr'], 'L0_ffn_W1s': _L0_ffn_in['W1s'], 'L0_ffn_b1s': _L0_ffn_in['b1s'], 'L0_ffn_W2s': _L0_ffn_in['W2s'], 'L0_ffn_b2s': _L0_ffn_in['b2s'], 'L0_ffn_W1p': _L0_ffn_in['W1p'], 'L0_ffn_b1p': _L0_ffn_in['b1p'], 'L0_ffn_W2p': _L0_ffn_in['W2p'], 'L0_ffn_b2p': _L0_ffn_in['b2p'], 'L1_gnn_W': _L1_gnn_in['W'], 'L1_gnn_b': _L1_gnn_in['b'], 'L1_gnn_a': _L1_gnn_in['a'], 'L1_ffn_router_w': _L1_ffn_in['router_w'], 'L1_ffn_w1': _L1_ffn_in['w1'], 'L1_ffn_w2': _L1_ffn_in['w2'], 'L1_ffn_w3': _L1_ffn_in['w3']}

def reference(x, adj, L0_gnn_W_proj, L0_gnn_b_proj, L0_gnn_W_gcn, L0_gnn_b_gcn, L0_ffn_Wr, L0_ffn_W1s, L0_ffn_b1s, L0_ffn_W2s, L0_ffn_b2s, L0_ffn_W1p, L0_ffn_b1p, L0_ffn_W2p, L0_ffn_b2p, L1_gnn_W, L1_gnn_b, L1_gnn_a, L1_ffn_router_w, L1_ffn_w1, L1_ffn_w2, L1_ffn_w3):
    import jax
    import jax.numpy as jnp

    def _L0_gnn_ref(h, adj, simlar, W_proj, b_proj, W_gcn, b_gcn):
        import jax, jax.numpy as jnp
        import numpy as np
        N = 3072
        HID = 128
        T = 350
        DENSITY = 0.05
        sim = jnp.tanh(adj * simlar)
        filt = sim * (adj > 0).astype(sim.dtype)
        vals, idx = jax.lax.top_k(filt, T)
        nnz = jnp.sum(filt != 0, axis=1)
        keep = jnp.arange(T)[None, :] < nnz[:, None]
        rows = jnp.arange(filt.shape[0])[:, None]
        new_adj = jnp.zeros_like(filt).at[rows, idx].set(jnp.where(keep, vals, 0.0))
        h2 = jnp.tanh(h @ W_proj + b_proj)
        feat = jax.nn.relu(new_adj @ (h2 @ W_gcn) + b_gcn)
        return feat

    def _L0_ffn_ref(x, Wr, W1s, b1s, W2s, b2s, W1p, b1p, W2p, b2p):
        import jax, jax.numpy as jnp
        import numpy as np
        B, S, D, F, E, K = (8, 1024, 128, 512, 8, 2)
        gelu = lambda t: jax.nn.gelu(t, approximate=False)
        shared = gelu(x @ W1s + b1s) @ W2s + b2s
        rw = jax.nn.softmax(x @ Wr, axis=-1)
        topw, topi = jax.lax.top_k(rw, K)
        topw = topw / jnp.sum(topw, axis=-1, keepdims=True)
        mask = jnp.sum(jax.nn.one_hot(topi, E, dtype=topw.dtype) * topw[..., None], axis=-2)
        h = gelu(jnp.einsum('bsd,edf->bsef', x, W1p) + b1p)
        priv = jnp.einsum('bsef,efd->bsed', h, W2p) + b2p
        routed = jnp.einsum('bsed,bse->bsd', priv, mask)
        return shared + routed

    def _L1_gnn_ref(x, W, b, a, adj_matrix):
        import jax, jax.numpy as jnp
        import numpy as np
        N, IN_FEAT, OUT_FEAT, H = (2048, 128, 128, 8)
        D = OUT_FEAT // H
        ADJ_DENSITY = 0.05
        num_nodes = x.shape[0]
        num_heads = a.shape[0]
        half = a.shape[1] // 2
        node_feats = (x @ W.T + b).reshape(num_nodes, num_heads, half)
        logit_parent = (node_feats * a[None, :, :half]).sum(axis=-1)
        logit_child = (node_feats * a[None, :, half:]).sum(axis=-1)
        attn_logits = logit_parent[:, None, :] + logit_child[None, :, :]
        attn_logits = jax.nn.leaky_relu(attn_logits, 0.2)
        attn_logits = jnp.where(jnp.abs(adj_matrix)[..., None] != 0.0, attn_logits, 0.0)
        attn_probs = jax.nn.softmax(attn_logits, axis=1)
        out = jnp.einsum('ijh,jhc->ihc', attn_probs, node_feats)
        return out.reshape(num_nodes, -1)

    def _L1_ffn_ref(x, router_w, w1, w2, w3):
        import jax, jax.numpy as jnp
        import numpy as np
        N_EXPERTS = 8
        TOP_K = 2
        B, T, C = x.shape
        flat = x.reshape(-1, C)
        logits = flat @ router_w.T
        probs = jax.nn.softmax(logits, axis=-1)
        topk_probs, topk_idx = jax.lax.top_k(probs, TOP_K)
        topk_probs = topk_probs / (jnp.sum(topk_probs, axis=-1, keepdims=True) + 1e-09)
        onehot = jax.nn.one_hot(topk_idx, N_EXPERTS, dtype=flat.dtype)
        gates = jnp.einsum('nk,nke->ne', topk_probs, onehot)
        h1 = jnp.einsum('nc,ehc->neh', flat, w1)
        h3 = jnp.einsum('nc,ehc->neh', flat, w3)
        h = jax.nn.silu(h1) * h3
        y = jnp.einsum('neh,ech->nec', h, w2)
        out = jnp.einsum('ne,nec->nc', gates, y)
        return out.reshape(B, T, C)
    x = x + _L0_gnn_ref(_layernorm(x, axis=-1), adj, adj, L0_gnn_W_proj, L0_gnn_b_proj, L0_gnn_W_gcn, L0_gnn_b_gcn)
    x = x + _L0_ffn_ref(_layernorm(x, axis=-1)[None], L0_ffn_Wr, L0_ffn_W1s, L0_ffn_b1s, L0_ffn_W2s, L0_ffn_b2s, L0_ffn_W1p, L0_ffn_b1p, L0_ffn_W2p, L0_ffn_b2p)[0]
    x = x + _L1_gnn_ref(_layernorm(x, axis=-1), L1_gnn_W, L1_gnn_b, L1_gnn_a, adj)
    x = x + _L1_ffn_ref(_layernorm(x, axis=-1)[None], L1_ffn_router_w, L1_ffn_w1, L1_ffn_w2, L1_ffn_w3)[0]
    return x

_drawn_inputs = setup_inputs


def setup_inputs(seed=0):
    import zlib

    import numpy as np

    out = dict(_drawn_inputs(seed))
    spreads = {'L0_gnn_b_proj': (0.0, 0.1),
     'L0_gnn_b_gcn': (0.0, 0.1),
     'L0_ffn_b1s': (0.0, 0.1),
     'L0_ffn_b2s': (0.0, 0.1),
     'L0_ffn_b1p': (0.0, 0.1),
     'L0_ffn_b2p': (0.0, 0.1)}
    factors = {}
    for name, (base, spread) in spreads.items():
        noise = np.random.default_rng([zlib.crc32(name.encode()), seed]).standard_normal(out[name].shape)
        drawn = base * np.exp(spread * noise) if base else spread * noise
        out[name] = jnp.asarray(drawn.astype(out[name].dtype))
    for name, factor in factors.items():
        out[name] = (out[name] * factor).astype(out[name].dtype)
    return out
```

```python
import concourse.bass as bass
from concourse import mybir
from contextlib import ExitStack

F32 = mybir.dt.float32
BF16 = mybir.dt.bfloat16
ALU = mybir.AluOpType
ACT = mybir.ActivationFunctionType
AX = mybir.AxisListType

P = 128
N = 4096
W = 512
CHUNKS = N // W
TILES = N // P
HEADS = 8
HD = 16
EPS = 1e-5
COLS = HD + 1
PART = 3 * COLS
SELW = 240


class Scope:

    def __init__(self, nc, stage):
        self.nc, self.stage, self.stack = nc, stage, ExitStack()

    def __enter__(self):
        self.stack.__enter__()
        return self

    def __exit__(self, *a):
        return self.stack.__exit__(*a)

    def sbuf(self, name, shape, dt=F32):
        return self.stack.enter_context(self.nc.sbuf_tensor(f"{self.stage}_{name}", shape, dt))

    def psum(self, name, shape, dt=F32):
        return self.stack.enter_context(self.nc.psum_tensor(f"{self.stage}_{name}", shape, dt))

    def sem(self, name):
        return self.stack.enter_context(self.nc.semaphore(f"{self.stage}_{name}"))


def layer_norm(nc, stage, x_dram, xn_dram):
    with Scope(nc, stage) as s:
        x = s.sbuf("x", [P, N])
        centred = s.sbuf("centred", [P, N])
        square = s.sbuf("square", [P, N])
        rstd = s.sbuf("rstd", [P, N])
        mean_of = s.sbuf("mean_of", [P, P])
        mean_ps = s.psum("mean_ps", [P, 4, W])
        var_ps = s.psum("var_ps", [P, 4, W])
        x_in, const_ready, mean_ready, centred_ready, square_ready, var_ready = map(
            s.sem, ("x_in", "const_ready", "mean_ready", "centred_ready", "square_ready", "var_ready"))
        var_taken, inv_ready, rstd_ready, xn_ready, xn_out = map(
            s.sem, ("var_taken", "inv_ready", "rstd_ready", "xn_ready", "xn_out"))

        with nc.Block() as block:

            @block.sync
            def _(sp):
                sp.dma_start(x[:, :], x_dram).then_inc(x_in, 16)
                sp.wait_ge(xn_ready, CHUNKS)
                sp.dma_start(xn_dram, x[:, :]).then_inc(xn_out, 16)
                sp.wait_ge(xn_out, 16)

            @block.tensor
            def _(pe):
                pe.wait_ge(x_in, 16)
                pe.wait_ge(const_ready, 1)

                for c in range(CHUNKS):
                    if c >= 4:
                        pe.wait_ge(centred_ready, c - 3)
                    nc.tensor.matmul(mean_ps[:, c % 4, :], mean_of[:, :], x[:, c * W:(c + 1) * W],
                                     start=True, stop=True).then_inc(mean_ready, 1)
                for c in range(CHUNKS):
                    pe.wait_ge(square_ready, c + 1)
                    if c >= 4:
                        pe.wait_ge(var_taken, c - 3)
                    nc.tensor.matmul(var_ps[:, c % 4, :], mean_of[:, :], square[:, c * W:(c + 1) * W],
                                     start=True, stop=True).then_inc(var_ready, 1)

            @block.scalar
            def _(act):
                for c in range(CHUNKS):
                    cs = slice(c * W, (c + 1) * W)
                    act.wait_ge(centred_ready, c + 1)
                    nc.scalar.activation(square[:, cs], centred[:, cs], ACT.Square).then_inc(square_ready, 1)
                for c in range(CHUNKS):
                    cs = slice(c * W, (c + 1) * W)
                    act.wait_ge(inv_ready, c + 1)
                    nc.scalar.activation(rstd[:, cs], rstd[:, cs], ACT.Sqrt).then_inc(rstd_ready, 1)

            @block.vector
            def _(dve):
                nc.vector.memset(mean_of[:, :], 1.0 / P).then_inc(const_ready, 1)
                for c in range(CHUNKS):
                    cs = slice(c * W, (c + 1) * W)
                    dve.wait_ge(mean_ready, c + 1)
                    nc.vector.tensor_tensor(centred[:, cs], x[:, cs], mean_ps[:, c % 4, :],
                                            ALU.subtract).then_inc(centred_ready, 1)
                for c in range(CHUNKS):
                    cs = slice(c * W, (c + 1) * W)
                    dve.wait_ge(var_ready, c + 1)
                    nc.vector.tensor_scalar(rstd[:, cs], var_ps[:, c % 4, :], EPS, None,
                                            ALU.add).then_inc(var_taken, 1)
                for c in range(CHUNKS):
                    cs = slice(c * W, (c + 1) * W)
                    dve.wait_ge(var_taken, c + 1)
                    nc.vector.reciprocal(rstd[:, cs], rstd[:, cs]).then_inc(inv_ready, 1)
                for c in range(CHUNKS):
                    cs = slice(c * W, (c + 1) * W)
                    dve.wait_ge(rstd_ready, c + 1)
                    nc.vector.tensor_tensor(x[:, cs], centred[:, cs], rstd[:, cs],
                                            ALU.mult).then_inc(xn_ready, 1)


def filtered_graph(nc, x_dram, xn_dram, adj_dram, w_proj, b_proj, w_gcn, b_gcn, x_out, absent_dram):
    UNIT = 4
    UNITS = TILES // UNIT
    RING = 4
    with Scope(nc, "graph") as s:
        xn = s.sbuf("xn", [P, N])
        hidden = s.sbuf("hidden", [P, N])
        x = s.sbuf("x", [P, N])
        g = s.sbuf("g", [P, TILES, P])
        wp, wg = s.sbuf("wp", [P, P]), s.sbuf("wg", [P, P])
        bp, bg = s.sbuf("bp", [P, 1]), s.sbuf("bg", [P, 1])
        ones = s.sbuf("ones", [P, P], BF16)
        adj = s.sbuf("adj", [P, RING, UNIT, W])
        sim = s.sbuf("sim", [P, 2, UNIT, W])
        absent = s.sbuf("absent", [P, 2, UNIT, W], BF16)
        feat = s.sbuf("feat", [P, 2, W])
        counts = s.sbuf("counts", [1, N])
        head_ps = s.psum("head_ps", [P, 4, W])
        feat_ps = s.psum("feat_ps", [P, 2, W])
        count_ps = s.psum("count_ps", [P, 2, W])
        loaded, const_ready, hid_mm, hid_ready, g_mm, g_ready = map(
            s.sem, ("loaded", "const_ready", "hid_mm", "hid_ready", "g_mm", "g_ready"))
        adj_in = [s.sem(f"adj_in{r}") for r in range(RING)]
        square_ready = s.sem("square_ready")
        mask_ready = s.sem("mask_ready")
        sim_ready = s.sem("sim_ready")
        sim_used = s.sem("sim_used")
        mask_used = s.sem("mask_used")
        feat_ready = s.sem("feat_ready")
        counts_ready = s.sem("counts_ready")
        x_ready = s.sem("x_ready")
        stored, pool_turn = s.sem("stored"), s.sem("pool_turn")

        with nc.Block() as block:

            @block.sync
            def _(sp):
                for dst, src in ((xn[:, :], xn_dram), (wp[:, :], w_proj), (wg[:, :], w_gcn),
                                 (bp[:, :], b_proj), (bg[:, :], b_gcn), (x[:, :], x_dram)):
                    sp.dma_start(dst, src).then_inc(loaded, 16)
                with sp.Fori(0, CHUNKS) as c:
                    for k in range(UNITS):
                        sp.wait_ge(square_ready, c * UNITS + (k + 1))
                        sp.wait_ge(mask_ready, c * UNITS + (k + 1))
                        sp.dma_start(adj[:, k % RING, :, :],
                                     adj_dram[c, :, k * UNIT:(k + 1) * UNIT, :]).then_inc(adj_in[k % RING], 16)
                sp.wait_ge(x_ready, CHUNKS + 2)
                sp.dma_start(x_out, x[:, :]).then_inc(stored, 16)
                sp.wait_ge(counts_ready, CHUNKS + 2)
                sp.dma_start(absent_dram, counts[:, :]).then_inc(stored, 16)
                sp.wait_ge(stored, 32)

            @block.tensor
            def _(pe):
                pe.wait_ge(loaded, 6 * 16)
                for c in range(CHUNKS):
                    if c >= 4:
                        pe.wait_ge(hid_ready, c - 3)
                    nc.tensor.matmul(head_ps[:, c % 4, :], wp[:, :], xn[:, c * W:(c + 1) * W],
                                     start=True, stop=True).then_inc(hid_mm, 1)
                pe.wait_ge(hid_ready, CHUNKS)
                for c in range(CHUNKS):
                    if c >= 4:
                        pe.wait_ge(g_ready, c - 3)
                    for t in range(4):
                        j = c * 4 + t
                        last = nc.tensor.matmul(head_ps[:, c % 4, t * P:(t + 1) * P],
                                                hidden[:, j * P:(j + 1) * P], wg[:, :],
                                                start=True, stop=True)
                    last.then_inc(g_mm, 1)
                pe.wait_ge(g_ready, CHUNKS)
                pe.wait_ge(const_ready, 1)
                with pe.Fori(0, CHUNKS // 2) as c2:
                    for cc in range(2):
                        c = c2 * 2 + cc
                        pe.wait_ge(feat_ready, c + 1)
                        pe.wait_ge(counts_ready, c + 1)
                        for k in range(UNITS):
                            pe.wait_ge(sim_ready, c * UNITS + (k + 1))
                            for u in range(UNIT):
                                j = k * UNIT + u
                                last = nc.tensor.matmul(feat_ps[:, cc, :], g[:, j, :], sim[:, k % 2, u, :],
                                                        start=j == 0, stop=j == TILES - 1)
                            last.then_inc(sim_used, 1)
                            pe.wait_ge(mask_ready, c * UNITS + (k + 1 + RING))
                            for u in range(UNIT):
                                j = k * UNIT + u
                                last = nc.tensor.matmul(count_ps[:, cc, :], ones[:, :], absent[:, k % 2, u, :],
                                                        start=j == 0, stop=j == TILES - 1)
                            last.then_inc(mask_used, 1)

            @block.scalar
            def _(act):
                act.sem_inc(feat_ready, 2)
                act.wait_ge(loaded, 6 * 16)
                for c in range(CHUNKS):
                    act.wait_ge(hid_mm, c + 1)
                    nc.scalar.activation(hidden[:, c * W:(c + 1) * W], head_ps[:, c % 4, :], ACT.Tanh,
                                         bias=bp[:, 0:1]).then_inc(hid_ready, 1)
                with act.Fori(0, CHUNKS // 2) as c2:
                    for cc in range(2):
                        c = c2 * 2 + cc
                        for k in range(UNITS):
                            act.wait_ge(square_ready, c * UNITS + (k + 1 + RING))
                            nc.scalar.activation(sim[:, k % 2, :, :], sim[:, k % 2, :, :],
                                                 ACT.Tanh).then_inc(sim_ready, 1)
                        act.wait_ge(sim_used, c * UNITS + (UNITS + 2))
                        act.wait_ge(x_ready, c + 1)
                        nc.scalar.activation(feat[:, cc, :], feat_ps[:, cc, :], ACT.Relu,
                                             bias=bg[:, 0:1]).then_inc(feat_ready, 1)

            @block.gpsimd
            def _(pool):
                pool.sem_inc(mask_ready, RING)
                with pool.Fori(0, CHUNKS) as c:
                    for k in range(UNITS):
                        pool.wait_ge(adj_in[k % RING], c * (UNITS // RING * 16) + (k // RING + 1) * 16)
                        pool.wait_ge(mask_used, c * UNITS + (k + 1))
                        pool.sem_inc(pool_turn, 1)
                        nc.gpsimd.tensor_scalar(absent[:, k % 2, :, :], adj[:, k % RING, :, :], 0.0, None,
                                                ALU.is_equal).then_inc(mask_ready, 1)

            @block.vector
            def _(dve):
                nc.vector.memset(ones[:, :], 1.0).then_inc(const_ready, 1)
                dve.sem_inc(square_ready, RING)
                dve.sem_inc(sim_used, 2)
                dve.sem_inc(mask_used, 2)
                dve.sem_inc(counts_ready, 2)
                dve.sem_inc(x_ready, 2)
                for c in range(CHUNKS):
                    dve.wait_ge(g_mm, c + 1)
                    nc.vector.tensor_copy(g[:, 4 * c:4 * c + 4, :],
                                          head_ps[:, c % 4, :].rearrange("p (t d) -> p t d", t=4)).then_inc(g_ready, 1)
                dve.wait_ge(loaded, 6 * 16)
                with dve.Fori(0, CHUNKS // 2) as c2:
                    for cc in range(2):
                        c = c2 * 2 + cc
                        cs = bass.ds(c * W, W)
                        for k in range(UNITS):
                            dve.wait_ge(adj_in[k % RING], c * (UNITS // RING * 16) + (k // RING + 1) * 16)
                            dve.wait_ge(sim_used, c * UNITS + (k + 1))
                            nc.vector.scalar_tensor_tensor(
                                out=sim[:, k % 2, :, :], in0=adj[:, k % RING, :, :], scalar=0.0,
                                in1=adj[:, k % RING, :, :], op0=ALU.max, op1=ALU.mult).then_inc(square_ready, 1)
                        dve.wait_ge(mask_used, c * UNITS + (UNITS + 2))
                        nc.vector.tensor_scalar(counts[0:1, cs], count_ps[0:1, cc, :], 1.0, None,
                                                ALU.mult).then_inc(counts_ready, 1)
                        dve.wait_ge(feat_ready, c + 3)
                        nc.vector.tensor_tensor(x[:, cs], feat[:, cc, :], x[:, cs],
                                                ALU.add).then_inc(x_ready, 1)


def route(nc, stage, xn_dram, w_router, identity_dram, gates_dram, guard):
    E = 8
    with Scope(nc, stage) as s:
        xn = s.sbuf("xn", [P, N])
        wr = s.sbuf("wr", [P, E])
        ident = s.sbuf("ident", [P, P])
        rank = s.sbuf("rank", [P, TILES, E])
        rank_i = s.sbuf("rank_i", [P, TILES, E], mybir.dt.int32)
        prob, left, hit, pick1, pick2 = (s.sbuf(n, [P, TILES, E]) for n in ("prob", "left", "hit", "pick1", "pick2"))
        top, total, best1, best2 = (s.sbuf(n, [P, TILES]) for n in ("top", "total", "best1", "best2"))
        gates_t = s.sbuf("gates_t", [E, N])
        logit_ps = s.psum("logit_ps", [P, TILES, E])
        gate_ps = s.psum("gate_ps", [E, 4, W])
        loaded, ranked, logits, shifted, powers, step, gates_mm, gates_ready, stored = map(
            s.sem, ("loaded", "ranked", "logits", "shifted", "powers", "step", "gates_mm", "gates_ready", "stored"))

        with nc.Block() as block:

            @block.sync
            def _(sp):
                for dst, src in ((xn[:, :], xn_dram), (wr[:, :], w_router), (ident[:, :], identity_dram)):
                    sp.dma_start(dst, src).then_inc(loaded, 16)
                sp.wait_ge(gates_ready, CHUNKS)
                sp.dma_start(gates_dram, gates_t[:, :]).then_inc(stored, 16)
                sp.wait_ge(stored, 16)

            @block.tensor
            def _(pe):
                pe.wait_ge(loaded, 48)
                for t in range(TILES):
                    last = nc.tensor.matmul(logit_ps[:, t, :], xn[:, t * P:(t + 1) * P], wr[:, :],
                                            start=True, stop=True)
                last.then_inc(logits, 1)
                pe.wait_ge(step, (24 if guard else 23))
                for c in range(CHUNKS):
                    if c >= 4:
                        pe.wait_ge(gates_ready, c - 3)
                    for t in range(4):
                        last = nc.tensor.transpose(gate_ps[:, c % 4, t * P:(t + 1) * P],
                                                   prob[:, c * 4 + t, :], ident[:, :])
                    last.then_inc(gates_mm, 1)

            @block.scalar
            def _(act):
                act.wait_ge(shifted, 1)
                nc.scalar.activation(prob[:, :, :], prob[:, :, :], ACT.Exp).then_inc(powers, 1)

            @block.gpsimd
            def _(pool):
                nc.gpsimd.iota(rank_i[:, :, :], [[0, TILES], [-1, E]], base=E, channel_multiplier=0).then_inc(ranked, 1)

            @block.vector
            def _(dve):
                steps = 0

                def done(ins):
                    nonlocal steps
                    steps += 1
                    ins.then_inc(step, 1)
                    dve.wait_ge(step, steps)

                def wide(a):
                    return a[:, :].rearrange("p (t o) -> p t o", o=1).broadcast_to([P, TILES, E])

                dve.wait_ge(logits, 1)
                done(nc.vector.tensor_reduce(top[:, :], logit_ps[:, :, :], AX.X, ALU.max))
                nc.vector.tensor_tensor(prob[:, :, :], logit_ps[:, :, :], wide(top), ALU.subtract).then_inc(shifted, 1)
                dve.wait_ge(ranked, 1)
                done(nc.vector.tensor_copy(rank[:, :, :], rank_i[:, :, :]))
                dve.wait_ge(powers, 1)
                done(nc.vector.tensor_reduce(total[:, :], prob[:, :, :], AX.X, ALU.add))
                done(nc.vector.reciprocal(total[:, :], total[:, :]))
                done(nc.vector.tensor_tensor(prob[:, :, :], prob[:, :, :], wide(total), ALU.mult))
                done(nc.vector.tensor_copy(left[:, :, :], prob[:, :, :]))
                for best, pick in ((best1, pick1), (best2, pick2)):
                    done(nc.vector.tensor_reduce(best[:, :], left[:, :, :], AX.X, ALU.max))
                    done(nc.vector.tensor_tensor(hit[:, :, :], left[:, :, :], wide(best), ALU.is_equal))
                    done(nc.vector.tensor_tensor(hit[:, :, :], hit[:, :, :], rank[:, :, :], ALU.mult))
                    done(nc.vector.tensor_reduce(top[:, :], hit[:, :, :], AX.X, ALU.max))
                    done(nc.vector.tensor_tensor(pick[:, :, :], hit[:, :, :], wide(top), ALU.is_equal))
                    done(nc.vector.scalar_tensor_tensor(
                        out=left[:, :, :], in0=pick[:, :, :], scalar=-2.0, in1=left[:, :, :],
                        op0=ALU.mult, op1=ALU.add))
                done(nc.vector.tensor_tensor(total[:, :], best1[:, :], best2[:, :], ALU.add))
                if guard:
                    done(nc.vector.tensor_scalar(total[:, :], total[:, :], guard, None, ALU.add))
                done(nc.vector.reciprocal(total[:, :], total[:, :]))
                done(nc.vector.tensor_tensor(pick1[:, :, :], pick1[:, :, :], pick2[:, :, :], ALU.add))
                done(nc.vector.tensor_tensor(prob[:, :, :], prob[:, :, :], pick1[:, :, :], ALU.mult))
                done(nc.vector.tensor_tensor(prob[:, :, :], prob[:, :, :], wide(total), ALU.mult))
                for c in range(CHUNKS):
                    dve.wait_ge(gates_mm, c + 1)
                    nc.vector.tensor_copy(gates_t[:, c * W:(c + 1) * W], gate_ps[:, c % 4, :]).then_inc(gates_ready, 1)


def experts(nc, stage, x_dram, xn_dram, gates_dram, w_up, w_down, bias_up, bias_down, shared, widths, x_out):
    BLOCKS = len(widths)
    HID = sum(widths)
    EXPERTS = 9 if shared else 8
    UPS = 1 if shared else 2
    starts = [sum(widths[:b]) for b in range(BLOCKS)]
    PER = 2 * EXPERTS
    with Scope(nc, stage) as s:
        x = s.sbuf("x", [P, N])
        up = s.sbuf("up", [P, UPS, EXPERTS, HID])
        down = s.sbuf("down", [P, EXPERTS, BLOCKS, P])
        bup = s.sbuf("bup", [P, EXPERTS, BLOCKS])
        bdown = s.sbuf("bdown", [P, EXPERTS])
        xn = s.sbuf("xn", [P, 2, W])
        gates = s.sbuf("gates", [P, 2, 8, W])
        hid = s.sbuf("hid", [P, 2, BLOCKS, W])
        part = s.sbuf("part", [P, 2, W])
        up_ps = [s.psum(f"up_ps{i}", [P, BLOCKS, W]) for i in range(UPS)]
        y_ps = s.psum("y_ps", [P, 2, W])
        loaded = s.sem("loaded")
        xn_in = [s.sem(f"xn_in{i}") for i in range(2)]
        gates_in = [s.sem(f"gates_in{i}") for i in range(2)]
        xn_used = s.sem("xn_used")
        up_mm = s.sem("up_mm")
        act_ready = s.sem("act_ready")
        hid_ready = s.sem("hid_ready")
        y_mm = s.sem("y_mm")
        y_taken = s.sem("y_taken")
        summed = s.sem("summed")
        stored = s.sem("stored")
        hidden_done = act_ready if shared else hid_ready

        with nc.Block() as block:

            @block.sync
            def _(sp):
                sp.dma_start(up[:, :, :, :], w_up).then_inc(loaded, 16)
                sp.dma_start(down[:, :, :, :], w_down).then_inc(loaded, 16)
                sp.dma_start(x[:, :], x_dram).then_inc(loaded, 16)
                if shared:
                    sp.dma_start(bup[:, :, :], bias_up).then_inc(loaded, 16)
                    sp.dma_start(bdown[:, :], bias_down).then_inc(loaded, 16)
                with sp.Fori(0, CHUNKS // 2) as c2:
                    for cc in range(2):
                        c = c2 * 2 + cc
                        sp.wait_ge(xn_used, c + 1)
                        sp.dma_start(xn[:, cc, :], xn_dram[:, bass.ds(c * W, W)]).then_inc(xn_in[cc], 16)
                        sp.wait_ge(summed, c * EXPERTS + 1)
                        sp.dma_start(gates[:, cc, :, :], gates_dram[:, bass.ds(c * W, W)].rearrange(
                            "(o e) n -> o e n", o=1).broadcast_to([P, 8, W])).then_inc(gates_in[cc], 16)
                sp.wait_ge(summed, CHUNKS * EXPERTS + EXPERTS + 1)
                sp.dma_start(x_out, x[:, :]).then_inc(stored, 16)
                sp.wait_ge(stored, 16)

            @block.tensor
            def _(pe):
                pe.wait_ge(loaded, 16 * (5 if shared else 3))

                def expert_down(c2, q):
                    e = q % EXPERTS
                    pe.wait_ge(y_taken, c2 * PER + (q + 1))
                    for b in range(BLOCKS):
                        pe.wait_ge(hidden_done, c2 * (PER * BLOCKS) + (q * BLOCKS + b + 1 + BLOCKS))
                        last = nc.tensor.matmul(y_ps[:, q % 2, :], down[0:widths[b], e, b, :],
                                                hid[0:widths[b], q % 2, b, :],
                                                start=b == 0, stop=b == BLOCKS - 1)
                    last.then_inc(y_mm, 1)

                with pe.Fori(0, CHUNKS // 2) as c2:
                    for q in range(PER):
                        cc, e = divmod(q, EXPERTS)
                        if e == 0:
                            pe.wait_ge(xn_in[cc], c2 * 16 + 16)
                        for b in range(BLOCKS):
                            n = c2 * (PER * BLOCKS) + (q * BLOCKS + b + 1)
                            pe.wait_ge(act_ready, n)
                            if not shared:
                                pe.wait_ge(hid_ready, n)
                            for i in range(UPS):
                                last = nc.tensor.matmul(up_ps[i][0:widths[b], b, :],
                                                        up[:, i, e, starts[b]:starts[b] + widths[b]],
                                                        xn[:, cc, :], start=True, stop=True)
                            last.then_inc(up_mm, 1)
                        if e == EXPERTS - 1:
                            pe.wait_ge(up_mm, c2 * (PER * BLOCKS) + (q + 1) * BLOCKS)
                            pe.sem_inc(xn_used, 1)
                        if q:
                            expert_down(c2, q - 1)
                    expert_down(c2, PER - 1)

            @block.scalar
            def _(act):
                act.sem_inc(act_ready, BLOCKS)
                act.wait_ge(loaded, 16 * (5 if shared else 3))
                with act.Fori(0, CHUNKS // 2) as c2:
                    for q in range(PER):
                        e = q % EXPERTS
                        act.wait_ge(y_mm, c2 * PER + (q + 1))
                        for b in range(BLOCKS):
                            act.wait_ge(up_mm, c2 * (PER * BLOCKS) + (q * BLOCKS + b + 1))
                            to, src = hid[0:widths[b], q % 2, b, :], up_ps[0][0:widths[b], b, :]
                            if shared:
                                nc.scalar.activation(to, src, ACT.Gelu,
                                                     bias=bup[0:widths[b], e, b:b + 1]).then_inc(act_ready, 1)
                            else:
                                nc.scalar.activation(to, src, ACT.Silu).then_inc(act_ready, 1)

            @block.vector
            def _(dve):
                dve.sem_inc(xn_used, 2)
                dve.sem_inc(hid_ready, BLOCKS)
                dve.sem_inc(y_mm, 2)
                dve.sem_inc(y_taken, 2)
                dve.sem_inc(summed, EXPERTS + 1)
                dve.wait_ge(loaded, 16 * (5 if shared else 3))

                def gather_expert(c2, q):
                    cc, e = divmod(q, EXPERTS)
                    n = c2 * PER + q
                    xs = x[:, bass.ds((c2 * 2 + cc) * W, W)]
                    if e == 0:
                        dve.wait_ge(gates_in[cc], c2 * 16 + 16)
                    dve.wait_ge(y_mm, n + 3)
                    if shared and e == 0:
                        nc.vector.tensor_scalar(part[:, q % 2, :], y_ps[:, q % 2, :], bdown[:, 0:1], None,
                                                ALU.add).then_inc(y_taken, 1)
                    elif shared:
                        nc.vector.scalar_tensor_tensor(
                            out=part[:, q % 2, :], in0=y_ps[:, q % 2, :], scalar=bdown[:, e:e + 1],
                            in1=gates[:, cc, e - 1, :], op0=ALU.add, op1=ALU.mult).then_inc(y_taken, 1)
                    else:
                        nc.vector.tensor_tensor(part[:, q % 2, :], y_ps[:, q % 2, :], gates[:, cc, e, :],
                                                ALU.mult).then_inc(y_taken, 1)
                    dve.wait_ge(y_taken, n + 3)
                    dve.wait_ge(summed, n + (EXPERTS + 1))
                    nc.vector.tensor_tensor(xs, xs, part[:, q % 2, :], ALU.add).then_inc(summed, 1)

                with dve.Fori(0, CHUNKS // 2) as c2:
                    for q in range(PER):
                        if not shared:
                            for b in range(BLOCKS):
                                n = c2 * (PER * BLOCKS) + (q * BLOCKS + b + 1)
                                dve.wait_ge(act_ready, n + BLOCKS)
                                h = hid[0:widths[b], q % 2, b, :]
                                nc.vector.tensor_tensor(h, h, up_ps[1][0:widths[b], b, :],
                                                        ALU.mult).then_inc(hid_ready, 1)
                        if q:
                            gather_expert(c2, q - 1)
                    gather_expert(c2, PER - 1)


def attention(nc, x_dram, xn_dram, adj_dram, absent_dram, w_t, bias, a_parent, a_child,
              head_cols, head_blocks, bands, scales, identity_dram, x_out):
    UNIT = 2
    UNITS = TILES // UNIT
    GROUP = 4
    PAIR = 4 * PART
    RING = 3
    with Scope(nc, "attn") as s:
        vz = s.sbuf("vz", [P, TILES, HEADS // 2, PAIR], BF16)
        feats = s.sbuf("feats", [P, TILES, 3, P], BF16)
        gap = s.sbuf("gap", [P, TILES, HEADS])
        cmax = s.sbuf("cmax", [P, HEADS])
        cmax_col = s.sbuf("cmax_col", [P, 1])
        wt, parent_block = s.sbuf("wt", [P, P]), s.sbuf("parent_block", [P, P])
        parent_rep = s.sbuf("parent_rep", [P, HEADS, P])
        bcol, acol, pcol = s.sbuf("bcol", [P, 1]), s.sbuf("acol", [P, 1]), s.sbuf("pcol", [P, 1])
        heads8 = s.sbuf("heads8", [P, HEADS])
        blocks = s.sbuf("blocks", [P, P])

        with Scope(nc, "nodes") as t:
            xn = t.sbuf("xn", [P, N])
            nf_t = t.sbuf("nf_t", [P, N])
            nf = t.sbuf("nf", [P, TILES, P])
            ident = t.sbuf("ident", [P, P])
            child8 = t.sbuf("child8", [P, HEADS])
            child = t.sbuf("child", [P, TILES, HEADS])
            top8, picked = t.sbuf("top8", [P, HEADS]), t.sbuf("picked", [P, HEADS])
            w_v, w_z = t.sbuf("w_v", [P, TILES, HEADS]), t.sbuf("w_z", [P, TILES, HEADS])
            SLAB = 4
            full, rest = (t.sbuf(n, [P, SLAB, HEADS // 2, COLS]) for n in ("full", "rest"))
            rest_f = t.sbuf("rest_f", [P, TILES, P])
            nf_ps = t.psum("nf_ps", [P, 2, W])
            tr_ps = t.psum("tr_ps", [P, 4, W])
            child_ps = t.psum("child_ps", [P, TILES, HEADS])
            loaded, child_const, nf_mm, nf_ready, tr_mm, tr_ready, child_mm, step, reduced, exps = map(
                t.sem, ("loaded", "child_const", "nf_mm", "nf_ready", "tr_mm", "tr_ready", "child_mm", "step",
                        "reduced", "exps"))
            with nc.Block() as block:

                @block.sync
                def _(sp):
                    for dst, src in ((xn, xn_dram), (wt, w_t), (bcol, bias), (acol, a_child), (pcol, a_parent),
                                     (heads8, head_cols), (blocks, head_blocks), (ident, identity_dram)):
                        sp.dma_start(dst[:, :], src).then_inc(loaded, 16)

                @block.tensor
                def _(pe):
                    pe.wait_ge(loaded, 8 * 16)
                    for c in range(CHUNKS):
                        if c >= 2:
                            pe.wait_ge(nf_ready, c - 1)
                        nc.tensor.matmul(nf_ps[:, c % 2, :], wt[:, :], xn[:, c * W:(c + 1) * W],
                                         start=True, stop=True).then_inc(nf_mm, 1)
                    pe.wait_ge(nf_ready, CHUNKS)
                    for c in range(CHUNKS):
                        if c >= 4:
                            pe.wait_ge(tr_ready, c - 3)
                        for k in range(4):
                            j = c * 4 + k
                            last = nc.tensor.transpose(tr_ps[:, c % 4, k * P:(k + 1) * P],
                                                       nf_t[:, j * P:(j + 1) * P], ident[:, :])
                        last.then_inc(tr_mm, 1)
                    pe.wait_ge(child_const, 1)
                    for j in range(TILES):
                        last = nc.tensor.matmul(child_ps[:, j, :], nf_t[:, j * P:(j + 1) * P], child8[:, :],
                                                start=True, stop=True)
                    last.then_inc(child_mm, 1)

                @block.scalar
                def _(act):
                    act.wait_ge(loaded, 8 * 16)
                    for c in range(CHUNKS):
                        act.wait_ge(nf_mm, c + 1)
                        nc.scalar.activation(nf_t[:, c * W:(c + 1) * W], nf_ps[:, c % 2, :], ACT.Identity,
                                             bias=bcol[:, 0:1]).then_inc(nf_ready, 1)
                    act.wait_ge(step, 3)
                    nc.scalar.activation(w_v[:, :, :], gap[:, :, :], ACT.Exp, scale=-0.2).then_inc(exps, 1)
                    nc.scalar.activation(w_z[:, :, :], gap[:, :, :], ACT.Exp, scale=-1.0).then_inc(exps, 1)

                @block.gpsimd
                def _(pool):
                    pool.wait_ge(step, 2)
                    nc.gpsimd.partition_all_reduce(cmax[:, :], top8[:, :], P, bass.bass_isa.ReduceOp.max).then_inc(reduced, 1)

                @block.vector
                def _(dve):
                    steps = 0

                    def done(ins):
                        nonlocal steps
                        steps += 1
                        ins.then_inc(step, 1)
                        dve.wait_ge(step, steps)

                    dve.wait_ge(loaded, 8 * 16)
                    nc.vector.tensor_scalar(child8[:, :], heads8[:, :], acol[:, 0:1], None,
                                            ALU.mult).then_inc(child_const, 1)
                    for c in range(CHUNKS):
                        dve.wait_ge(tr_mm, c + 1)
                        nc.vector.tensor_copy(nf[:, 4 * c:4 * c + 4, :],
                                              tr_ps[:, c % 4, :].rearrange("p (k d) -> p k d", k=4)).then_inc(tr_ready, 1)
                    dve.wait_ge(child_mm, 1)
                    done(nc.vector.tensor_copy(child[:, :, :], child_ps[:, :, :]))
                    done(nc.vector.tensor_reduce(top8[:, :], child[:, :, :].rearrange("p t h -> p h t"), AX.X, ALU.max))
                    dve.wait_ge(reduced, 1)
                    done(nc.vector.tensor_tensor(
                        gap[:, :, :], cmax[:, :].rearrange("p (o h) -> p o h", o=1).broadcast_to([P, TILES, HEADS]),
                        child[:, :, :], ALU.subtract))
                    done(nc.vector.tensor_tensor(picked[:, :], cmax[:, :], heads8[:, :], ALU.mult))
                    done(nc.vector.tensor_reduce(cmax_col[:, :], picked[:, :], AX.X, ALU.add))
                    done(nc.vector.tensor_scalar(parent_block[:, :], blocks[:, :], pcol[:, 0:1], None, ALU.mult))
                    done(nc.vector.tensor_scalar(picked[:, :], heads8[:, :], pcol[:, 0:1], None, ALU.mult))
                    done(nc.vector.tensor_copy(parent_rep[:, :, :], picked[:, :].rearrange(
                        "p (h o) -> p h o", o=1).broadcast_to([P, HEADS, P])))
                    dve.wait_ge(tr_ready, CHUNKS)
                    done(nc.vector.tensor_copy(feats[:, :, 0, :], nf[:, :, :]))
                    done(nc.vector.tensor_tensor(rest_f[:, :, :], nf[:, :, :], feats[:, :, 0, :], ALU.subtract))
                    done(nc.vector.tensor_copy(feats[:, :, 1, :], rest_f[:, :, :]))
                    done(nc.vector.tensor_tensor(rest_f[:, :, :], rest_f[:, :, :], feats[:, :, 1, :], ALU.subtract))
                    done(nc.vector.tensor_copy(feats[:, :, 2, :], rest_f[:, :, :]))
                    dve.wait_ge(exps, 2)
                    base = steps
                    PER = 4 * 7
                    with dve.Fori(0, TILES // SLAB) as slab:
                        n = 0

                        def next_step(ins):
                            nonlocal n
                            n += 1
                            ins.then_inc(step, 1)
                            dve.wait_ge(step, slab * PER + (base + n))

                        rows = bass.ds(slab * SLAB, SLAB)
                        for weight, odd, at in ((w_v, 0, 0), (w_z, 0, PART), (w_z, 1, 2 * PART), (w_v, 1, 3 * PART)):
                            wh = weight[:, rows, odd::2]
                            fh = nf[:, rows, :].rearrange("p t (a b d) -> p t a b d", b=2, d=HD)[:, :, :, odd, :]
                            next_step(nc.vector.tensor_tensor(
                                full[:, :, :, 0:HD], fh, wh.rearrange("p t (a o) -> p t a o", o=1).broadcast_to(
                                    [P, SLAB, HEADS // 2, HD]), ALU.mult))
                            next_step(nc.vector.tensor_scalar(full[:, :, :, HD], wh, 1.0, None, ALU.mult))
                            for part in range(3):
                                to = vz[:, rows, :, at + part * COLS:at + (part + 1) * COLS]
                                next_step(nc.vector.tensor_scalar(to, (full if part == 0 else rest)[:, :, :, :], 1.0, None,
                                                                  ALU.mult))
                                if part < 2:
                                    next_step(nc.vector.tensor_tensor(
                                        rest[:, :, :, :], (full if part == 0 else rest)[:, :, :, :], to, ALU.subtract))

        with Scope(nc, "rows") as t:
            band = t.sbuf("band", [P, 6, SELW])
            xn, x, absent = t.sbuf("xn", [P, W]), t.sbuf("x", [P, W]), t.sbuf("absent", [P, W])
            nf_c = t.sbuf("nf_c", [P, W])
            adj = t.sbuf("adj", [P, 2, UNIT, W])
            holes = t.sbuf("holes", [P, 2, UNIT, W], BF16)
            edges = t.sbuf("edges", [P, TILES, W], BF16)
            picked = t.sbuf("picked", [P, RING, GROUP, W], BF16)
            u = t.sbuf("u", [P, HEADS, W])
            rho = t.sbuf("rho", [P, 2, W])
            scale_vz = t.sbuf("scale_vz", [P, 2])
            sums = t.sbuf("sums", [P, GROUP, W])
            zsums = t.sbuf("zsums", [P, 2, W])
            total = t.sbuf("total", [P, 2, 2, W])
            q_ps = t.psum("q_ps", [P, W])
            sel_ps = t.psum("sel_ps", [P, GROUP, W])
            hole_ps = t.psum("hole_ps", [P, W])
            pair_ps = t.psum("pair_ps", [P, 2, W])
            high, low, gamma, eps = (sums[:, i, :] for i in range(GROUP))
            const_in, chunk_in, x_in, stored = map(t.sem, ("const_in", "chunk_in", "x_in", "stored"))
            adj_in = [t.sem(f"adj_in{i}") for i in range(2)]
            holes_ready = t.sem("holes_ready")
            holes_used = t.sem("holes_used")
            edges_ready, picked_ready, q_mm, q_taken = map(t.sem, ("edges_ready", "picked_ready", "q_mm", "q_taken"))
            step_mm = t.sem("step_mm")
            rho_ready = t.sem("rho_ready")
            sums_ready, zsums_ready, tot_mm, tot_ready, final, x_ready = map(
                t.sem, ("sums_ready", "zsums_ready", "tot_mm", "tot_ready", "final", "x_ready"))
            exps_ready, pool_turn = t.sem("exps_ready"), t.sem("pool_turn")
            QS = 2 + HEADS
            FINAL = 10

            with nc.Block() as block:

                @block.sync
                def _(sp):
                    sp.dma_start(band[:, :, :], bands).then_inc(const_in, 16)
                    sp.dma_start(scale_vz[:, :], scales).then_inc(const_in, 16)
                    with sp.Fori(0, CHUNKS) as c:
                        cs = bass.ds(c * W, W)
                        sp.wait_ge(x_ready, c + 1)
                        sp.dma_start(xn[:, :], xn_dram[:, cs]).then_inc(chunk_in, 16)
                        sp.wait_ge(stored, c * 16 + 16)
                        sp.dma_start(x[:, :], x_dram[:, cs]).then_inc(x_in, 16)
                        sp.wait_ge(x_in, c * 32 + 16)
                        sp.dma_start(absent[:, :], absent_dram[:, cs].broadcast_to([P, W])).then_inc(x_in, 16)
                        for k in range(UNITS):
                            sp.wait_ge(holes_ready, c * UNITS + (k + 1))
                            sp.dma_start(adj[:, k % 2, :, :],
                                         adj_dram[c, :, k * UNIT:(k + 1) * UNIT, :]).then_inc(adj_in[k % 2], 16)
                        sp.wait_ge(x_ready, c + 1 + 1)
                        sp.dma_start(x_out[:, cs], x[:, :]).then_inc(stored, 16)
                    sp.wait_ge(stored, CHUNKS * 16 + 16)

                @block.tensor
                def _(pe):
                    pe.wait_ge(const_in, 32)
                    with pe.Fori(0, CHUNKS) as c:
                        pe.wait_ge(chunk_in, c * 16 + 16)
                        pe.wait_ge(q_taken, c * QS + 1)
                        nc.tensor.matmul(q_ps[:, :], wt[:, :], xn[:, :], start=True, stop=True).then_inc(q_mm, 1)
                        for h in range(HEADS):
                            pe.wait_ge(q_taken, c * QS + (h + 1) + 1)
                            nc.tensor.matmul(q_ps[:, :], parent_rep[:, h, :], nf_c[:, :],
                                             start=True, stop=True).then_inc(q_mm, 1)
                        for g in range(2):
                            n = c * 2 + g
                            if g == 0:
                                pe.wait_ge(x_ready, c + 1)
                            pe.wait_ge(tot_ready, n + 1)
                            pe.wait_ge(sums_ready, n * GROUP + 1)
                            for j in range(TILES):
                                first, final_ = j == 0, j == TILES - 1
                                if g == 0:
                                    k = j // UNIT
                                    pe.wait_ge(holes_ready, c * UNITS + (k + 3))
                                    for part in range(3):
                                        last = nc.tensor.matmul(hole_ps[:, :], feats[:, j, part, :],
                                                                holes[:, k % 2, j % UNIT, :],
                                                                start=first and part == 0, stop=final_ and part == 2)
                                    if j % UNIT == UNIT - 1:
                                        last.then_inc(holes_used, 1)
                                    pe.wait_ge(edges_ready, c * UNITS + (k + 3))
                                for pr in range(2):
                                    nc.tensor.matmul(pair_ps[0:2 * PART, pr, :],
                                                     vz[:, j, 2 * g + pr, PART:3 * PART], edges[:, j, :],
                                                     start=first, stop=final_)
                                pe.wait_ge(picked_ready, n * TILES + (j + 1) + 1)
                                for i in range(GROUP):
                                    at = (i % 2) * 2 * PART
                                    last = nc.tensor.matmul(sel_ps[0:2 * PART, i, :],
                                                            vz[:, j, 2 * g + i // 2, at:at + 2 * PART],
                                                            picked[:, j % RING, i, :],
                                                            start=first, stop=final_)
                                last.then_inc(step_mm, 1)
                            pe.wait_ge(zsums_ready, n + 1)
                            pe.wait_ge(sums_ready, n * GROUP + GROUP + 1)
                            for nd in range(2):
                                for i in range(GROUP):
                                    at = (HEADS - 1 - (GROUP * g + i)) * HD
                                    nc.tensor.matmul(pair_ps[:, nd, :],
                                                     band[0:2 * PART, 2 * (i % 2) + nd, at:at + P],
                                                     sums[0:2 * PART, i, :], start=i == 0, stop=False)
                                for pr in range(2):
                                    at = (HEADS - 1 - (GROUP * g + 2 * pr)) * HD
                                    last = nc.tensor.matmul(pair_ps[:, nd, :],
                                                            band[0:2 * PART, 4 + nd, at:at + P],
                                                            zsums[0:2 * PART, pr, :], start=False, stop=pr == 1)
                                last.then_inc(tot_mm, 1)
                        pe.wait_ge(q_taken, c * QS + (HEADS + 1) + 1)
                        nc.tensor.matmul(q_ps[:, :], parent_block[:, :], nf_c[:, :],
                                         start=True, stop=True).then_inc(q_mm, 1)

                @block.gpsimd
                def _(pool):
                    pool.sem_inc(holes_ready, 2)
                    with pool.Fori(0, CHUNKS) as c:
                        for k in range(UNITS):
                            pool.wait_ge(adj_in[k % 2], c * (UNITS // 2 * 16) + (k // 2 + 1) * 16)
                            pool.wait_ge(holes_used, c * UNITS + (k + 1))
                            pool.wait_ge(edges_ready, c * UNITS + (k + 1))
                            pool.sem_inc(pool_turn, 1)
                            nc.gpsimd.tensor_scalar(holes[:, k % 2, :, :], adj[:, k % 2, :, :], 0.0, None,
                                                    ALU.is_equal).then_inc(holes_ready, 1)

                @block.scalar
                def _(act):
                    act.sem_inc(edges_ready, 2)
                    act.wait_ge(const_in, 32)
                    with act.Fori(0, CHUNKS) as c:
                        act.wait_ge(q_mm, c * QS + 1)
                        nc.scalar.activation(nf_c[:, :], q_ps[:, :], ACT.Identity, bias=bcol[:, 0:1]).then_inc(q_taken, 1)
                        act.wait_ge(picked_ready, c * (2 * TILES) + 1)
                        for h in range(HEADS):
                            act.wait_ge(q_mm, c * QS + (h + 2))
                            nc.scalar.activation(u[:, h, :], q_ps[:, :], ACT.Relu,
                                                 bias=cmax[:, h:h + 1]).then_inc(q_taken, 1)
                        for k in range(UNITS):
                            act.wait_ge(step_mm, c * (2 * TILES) + (k + 1) * UNIT)
                            act.wait_ge(holes_ready, c * UNITS + (k + 3))
                            nc.scalar.activation(edges[:, k * UNIT:(k + 1) * UNIT, :], holes[:, k % 2, :, :],
                                                 ACT.Copy, bias=1.0, scale=-1.0).then_inc(edges_ready, 1)
                        for g in range(2):
                            n = c * 2 + g
                            act.wait_ge(q_taken, c * QS + (HEADS + 1) + 1)
                            for i in range(GROUP):
                                act.wait_ge(sums_ready, n * GROUP + max(i - 1, 0) + 1)
                                nc.scalar.activation(rho[:, i % 2, :], u[:, GROUP * g + i, :], ACT.Exp,
                                                     scale=scale_vz[:, i % 2:i % 2 + 1]).then_inc(rho_ready, 1)
                                if i == 1:
                                    act.wait_ge(step_mm, n * TILES + 2 * TILES)
                                    act.wait_ge(tot_mm, n * 2 + 1)
                                    nc.scalar.copy(zsums[0:2 * PART, :, :],
                                                   pair_ps[0:2 * PART, :, :]).then_inc(zsums_ready, 1)
                            act.wait_ge(tot_mm, n * 2 + 2 + 1)
                            act.wait_ge(x_ready, c + 1)
                            nc.scalar.copy(total[:, g, :, :], pair_ps[:, :, :]).then_inc(tot_ready, 1)
                        act.wait_ge(final, c * FINAL + 2)
                        nc.scalar.activation(gamma, low, ACT.Exp, scale=0.2).then_inc(exps_ready, 1)
                        nc.scalar.activation(eps, high, ACT.Exp, scale=-1.0).then_inc(exps_ready, 1)

                @block.vector
                def _(dve):
                    for one in (x_ready, q_taken, sums_ready, tot_ready, tot_mm, picked_ready):
                        dve.sem_inc(one, 1)
                    dve.sem_inc(stored, 16)
                    dve.sem_inc(holes_used, 2)
                    dve.sem_inc(step_mm, TILES)
                    with dve.Fori(0, CHUNKS) as c:
                        for g in range(2):
                            n = c * 2 + g
                            dve.wait_ge(q_taken, c * QS + (1 + GROUP + GROUP * g) + 1)
                            for j in range(TILES):
                                if g == 0 and j % UNIT == 0:
                                    dve.wait_ge(edges_ready, c * UNITS + (j // UNIT + 3))
                                dve.wait_ge(step_mm, n * TILES + (j + TILES - RING + 1))
                                for i in range(GROUP):
                                    h = GROUP * g + i
                                    last = nc.vector.scalar_tensor_tensor(
                                        out=picked[:, j % RING, i, :], in0=u[:, h, :], scalar=gap[:, j, h:h + 1],
                                        in1=edges[:, j, :], op0=ALU.is_lt, op1=ALU.mult)
                                last.then_inc(picked_ready, 1)
                            dve.wait_ge(step_mm, n * TILES + 2 * TILES)
                            dve.wait_ge(tot_mm, n * 2 + 1)
                            for i in range(GROUP):
                                dve.wait_ge(rho_ready, n * GROUP + (i + 1))
                                nc.vector.tensor_tensor(sums[0:2 * PART, i, :], sel_ps[0:2 * PART, i, :],
                                                        rho[0:2 * PART, i % 2, :], ALU.mult).then_inc(sums_ready, 1)
                        steps = 0

                        def done(ins):
                            nonlocal steps
                            steps += 1
                            ins.then_inc(final, 1)
                            dve.wait_ge(final, c * FINAL + steps)

                        dve.wait_ge(tot_mm, c * 4 + 4 + 1)
                        dve.wait_ge(q_mm, c * QS + QS)
                        done(nc.vector.tensor_scalar(high, q_ps[:, :], cmax_col[:, 0:1], 0.0, ALU.add, ALU.max))
                        done(nc.vector.tensor_scalar(low, q_ps[:, :], cmax_col[:, 0:1], 0.0, ALU.add, ALU.min))
                        dve.sem_inc(q_taken, 1)
                        dve.wait_ge(tot_ready, c * 2 + 2 + 1)
                        done(nc.vector.tensor_tensor(total[:, 0, :, :], total[:, 0, :, :], total[:, 1, :, :], ALU.add))
                        dve.wait_ge(exps_ready, c * 2 + 2)
                        for nd in range(2):
                            done(nc.vector.tensor_tensor(total[:, 0, nd, :], total[:, 0, nd, :], gamma, ALU.mult))
                        dve.wait_ge(x_in, c * 32 + 32)
                        done(nc.vector.tensor_tensor(high, hole_ps[:, :], eps, ALU.mult))
                        done(nc.vector.tensor_tensor(low, absent[:, :], eps, ALU.mult))
                        done(nc.vector.tensor_tensor(total[:, 0, :, :], total[:, 0, :, :], sums[:, 0:2, :], ALU.add))
                        done(nc.vector.reciprocal(total[:, 0, 1, :], total[:, 0, 1, :]))
                        done(nc.vector.tensor_tensor(total[:, 0, 0, :], total[:, 0, 0, :], total[:, 0, 1, :], ALU.mult))
                        dve.wait_ge(x_ready, c + 1)
                        nc.vector.tensor_tensor(x[:, :], x[:, :], total[:, 0, 0, :], ALU.add).then_inc(x_ready, 1)
                        assert steps == FINAL


def network(nc, a, out):
    def scratch(name, shape):
        return nc.dram_tensor(name, shape, F32, kind="Internal").ap()

    x1, x2, x3 = (scratch(f"x{i}", [P, N]) for i in (1, 2, 3))
    xn = [scratch(f"xn{i}", [P, N]) for i in range(4)]
    gates = [scratch(f"gates{i}", [8, N]) for i in range(2)]
    absent = scratch("absent", [1, N])

    layer_norm(nc, "norm0", a["x_t"], xn[0])
    filtered_graph(nc, a["x_t"], xn[0], a["adj"], a["w_proj"], a["b_proj"], a["w_gcn"], a["b_gcn"], x1, absent)
    layer_norm(nc, "norm1", x1, xn[1])
    route(nc, "route0", xn[1], a["w_router0"], a["identity"], gates[0], None)
    experts(nc, "ffn0", x1, xn[1], gates[0], a["up0"], a["down0"], a["bias_up0"], a["bias_down0"],
            True, [P] * 4, x2)
    layer_norm(nc, "norm2", x2, xn[2])
    attention(nc, x2, xn[2], a["adj"], absent, a["w_attn"], a["b_attn"], a["a_parent"], a["a_child"],
              a["head_cols"], a["head_blocks"], a["bands"], a["scales"], a["identity"], x3)
    layer_norm(nc, "norm3", x3, xn[3])
    route(nc, "route1", xn[3], a["w_router1"], a["identity"], gates[1], 1e-9)
    experts(nc, "ffn1", x3, xn[3], gates[1], a["up1"], a["down1"], None, None, False, [P, P, 85], out)


def kernel(**inputs):
    import numpy as np
    import concourse.bacc as bacc
    from concourse.bass_utils import run_bass_kernel_spmd as run

    v = {k: np.asarray(t) for k, t in inputs.items()}
    heads = np.arange(P) // HD
    bands = np.zeros((P, 6, SELW), np.float32)
    for part in range(3):
        for blk in range(2):
            r = blk * PART + part * COLS
            for kind in range(3):
                sign = 1.0 if kind == 2 or (kind == 0) == (blk == 0) else -1.0
                at = P - HD + (HD if kind == 2 and blk == 1 else 0)
                for d in range(HD):
                    bands[r + d, 2 * kind, at + d] = sign
                    bands[r + HD, 2 * kind + 1, at + d] = sign
    scales = np.zeros((P, 2), np.float32)
    scales[0:PART, 0] = -0.8
    scales[PART:2 * PART, 1] = -0.8

    def pad_rows(w, rows):
        return np.concatenate([w, np.zeros((rows - w.shape[0],) + w.shape[1:], w.dtype)], 0)

    hid1 = v["L1_ffn_w1"].shape[1]
    up0 = np.concatenate([v["L0_ffn_W1s"][None], v["L0_ffn_W1p"]], 0)
    down0 = np.concatenate([v["L0_ffn_W2s"][None], v["L0_ffn_W2p"]], 0)
    b_up0 = np.concatenate([v["L0_ffn_b1s"][None], v["L0_ffn_b1p"]], 0)
    b_down0 = np.concatenate([v["L0_ffn_b2s"][None], v["L0_ffn_b2p"]], 0)
    down1 = np.stack([pad_rows(w.T, 3 * P) for w in v["L1_ffn_w2"]])
    arrays = {
        "x_t": v["x"].T,
        "adj": v["adj"].T.reshape(TILES, P, CHUNKS, W).transpose(2, 1, 0, 3),
        "w_proj": v["L0_gnn_W_proj"], "b_proj": v["L0_gnn_b_proj"][:, None],
        "w_gcn": v["L0_gnn_W_gcn"], "b_gcn": v["L0_gnn_b_gcn"][:, None],
        "w_router0": v["L0_ffn_Wr"],
        "up0": up0.transpose(1, 0, 2)[:, None], "down0": down0.reshape(9, 4, P, P).transpose(2, 0, 1, 3),
        "bias_up0": b_up0.reshape(9, 4, P).transpose(2, 0, 1), "bias_down0": b_down0.T,
        "w_attn": v["L1_gnn_W"].T, "b_attn": v["L1_gnn_b"][:, None],
        "a_parent": v["L1_gnn_a"][:, :HD].reshape(P, 1), "a_child": v["L1_gnn_a"][:, HD:].reshape(P, 1),
        "head_cols": (heads[:, None] == np.arange(HEADS)[None]).astype(np.float32),
        "head_blocks": (heads[:, None] == heads[None]).astype(np.float32),
        "bands": bands, "scales": scales, "identity": np.eye(P, dtype=np.float32),
        "w_router1": v["L1_ffn_router_w"].T,
        "up1": np.stack([v["L1_ffn_w1"], v["L1_ffn_w3"]]).transpose(3, 0, 1, 2),
        "down1": down1.reshape(8, 3, P, P).transpose(2, 0, 1, 3),
    }
    nc = bacc.Bacc("TRN2", target_bir_lowering=False, num_devices=1)
    data, a = {}, {}
    for name, t in arrays.items():
        data[name] = np.ascontiguousarray(t)
        a[name] = nc.dram_tensor(name, data[name].shape, mybir.dt.from_np(data[name].dtype),
                                 kind="ExternalInput").ap()
    out = nc.dram_tensor("out_t", [P, N], F32, kind="ExternalOutput").ap()
    network(nc, a, out)
    r = run(nc, [data], core_ids=[0])
    return np.ascontiguousarray(r.results[0]["out_t"].T)
```

```python
import concourse.bass as bass
from concourse import mybir
from contextlib import ExitStack

F32 = mybir.dt.float32
BF16 = mybir.dt.bfloat16
ALU = mybir.AluOpType
ACT = mybir.ActivationFunctionType
AX = mybir.AxisListType

P = 128
N = 4096
W = 512
CHUNKS = N // W
TILES = N // P
HEADS = 8
HD = 16
EPS = 1e-5
COLS = HD + 1
PART = 3 * COLS
SELW = 240


class Scope:

    def __init__(self, nc, stage):
        self.nc, self.stage, self.stack = nc, stage, ExitStack()

    def __enter__(self):
        self.stack.__enter__()
        return self

    def __exit__(self, *a):
        return self.stack.__exit__(*a)

    def sbuf(self, name, shape, dt=F32):
        return self.stack.enter_context(self.nc.sbuf_tensor(f"{self.stage}_{name}", shape, dt))

    def psum(self, name, shape, dt=F32):
        return self.stack.enter_context(self.nc.psum_tensor(f"{self.stage}_{name}", shape, dt))

    def sem(self, name):
        return self.stack.enter_context(self.nc.semaphore(f"{self.stage}_{name}"))


def layer_norm(nc, stage, x_dram, xn_dram, row_of):
    with Scope(nc, stage) as s:
        x = s.sbuf("x", [P, N])
        centred = s.sbuf("centred", [P, N])
        square = s.sbuf("square", [P, N])
        mean_of = s.sbuf("mean_of", [P, P])
        into_row = s.sbuf("into_row", [P, CHUNKS, CHUNKS])
        from_row = s.sbuf("from_row", [CHUNKS, CHUNKS, P])
        rstd = s.sbuf("rstd", [CHUNKS, W])
        wide_ps = s.psum("wide_ps", [P, 4, W])
        var_ps = s.psum("var_ps", [CHUNKS, W])
        x_in = [s.sem(f"x_in{h}") for h in range(2)]
        rows_in, const_ready, mean_ready, centred_ready, square_ready, var_ready = map(
            s.sem, ("rows_in", "const_ready", "mean_ready", "centred_ready", "square_ready", "var_ready"))
        rstd_steps, rstd_ready, wide_ready, xn_ready, xn_out = map(
            s.sem, ("rstd_steps", "rstd_ready", "wide_ready", "xn_ready", "xn_out"))
        zeroed = s.sem("zeroed")
        HALF = N // 2

        with nc.Block() as block:

            @block.sync
            def _(sp):
                for h in range(2):
                    sp.dma_start(x[:, h * HALF:(h + 1) * HALF],
                                 x_dram[:, h * HALF:(h + 1) * HALF]).then_inc(x_in[h], 16)
                sp.dma_start(from_row[:, :, :], row_of).then_inc(rows_in, 16)
                for h in range(2):
                    sp.wait_ge(xn_ready, (h + 1) * CHUNKS // 2)
                    sp.dma_start(xn_dram[:, h * HALF:(h + 1) * HALF],
                                 x[:, h * HALF:(h + 1) * HALF]).then_inc(xn_out, 16)
                sp.wait_ge(xn_out, 32)

            @block.tensor
            def _(pe):
                pe.wait_ge(const_ready, 1 + CHUNKS)
                for c in range(CHUNKS + 2):
                    if c < CHUNKS:
                        if c % 4 == 0:
                            pe.wait_ge(x_in[c // 4], 16)
                        if c >= 4:
                            pe.wait_ge(centred_ready, c - 3)
                        nc.tensor.matmul(wide_ps[:, c % 4, :], mean_of[:, :], x[:, c * W:(c + 1) * W],
                                         start=True, stop=True).then_inc(mean_ready, 1)
                    if c >= 2:
                        b = c - 2
                        pe.wait_ge(square_ready, b + 1)
                        nc.tensor.matmul(var_ps[:, :], into_row[:, b, :], square[:, b * W:(b + 1) * W],
                                         start=b == 0, stop=b == CHUNKS - 1).then_inc(var_ready, 1)
                pe.wait_ge(rows_in, 16)
                pe.wait_ge(rstd_ready, 1)
                for c in range(CHUNKS):
                    if c >= 4:
                        pe.wait_ge(xn_ready, c - 3)
                    nc.tensor.matmul(wide_ps[:, c % 4, :], from_row[:, c, :], rstd[:, :],
                                     start=True, stop=True).then_inc(wide_ready, 1)

            @block.scalar
            def _(act):
                for c in range(CHUNKS):
                    cs = slice(c * W, (c + 1) * W)
                    act.wait_ge(centred_ready, c + 1)
                    nc.scalar.activation(square[:, cs], centred[:, cs], ACT.Square).then_inc(square_ready, 1)
                act.wait_ge(rstd_steps, 2)
                nc.scalar.activation(rstd[:, :], rstd[:, :], ACT.Sqrt).then_inc(rstd_ready, 1)

            @block.vector
            def _(dve):
                nc.vector.memset(mean_of[:, :], 1.0 / P).then_inc(const_ready, 1)
                nc.vector.memset(into_row[:, :, :], 0.0).then_inc(zeroed, 1)
                dve.wait_ge(zeroed, 1)
                for c in range(CHUNKS):
                    nc.vector.memset(into_row[:, c, c:c + 1], 1.0 / P).then_inc(const_ready, 1)
                for c in range(CHUNKS):
                    cs = slice(c * W, (c + 1) * W)
                    dve.wait_ge(mean_ready, c + 1)
                    nc.vector.tensor_tensor(centred[:, cs], x[:, cs], wide_ps[:, c % 4, :],
                                            ALU.subtract).then_inc(centred_ready, 1)
                dve.wait_ge(var_ready, CHUNKS)
                nc.vector.tensor_scalar(rstd[:, :], var_ps[:, :], EPS, None, ALU.add).then_inc(rstd_steps, 1)
                dve.wait_ge(rstd_steps, 1)
                nc.vector.reciprocal(rstd[:, :], rstd[:, :]).then_inc(rstd_steps, 1)
                for c in range(CHUNKS):
                    cs = slice(c * W, (c + 1) * W)
                    dve.wait_ge(wide_ready, c + 1)
                    nc.vector.tensor_tensor(x[:, cs], centred[:, cs], wide_ps[:, c % 4, :],
                                            ALU.mult).then_inc(xn_ready, 1)


def filtered_graph(nc, x_dram, xn_dram, adj_dram, w_proj, b_proj, w_gcn, b_gcn, x_out, absent_dram):
    UNIT = 4
    UNITS = TILES // UNIT
    RING = 4
    with Scope(nc, "graph") as s:
        xn = s.sbuf("xn", [P, N])
        hidden = s.sbuf("hidden", [P, N])
        x = s.sbuf("x", [P, N])
        g = s.sbuf("g", [P, TILES, P])
        wp, wg = s.sbuf("wp", [P, P]), s.sbuf("wg", [P, P])
        bp, bg = s.sbuf("bp", [P, 1]), s.sbuf("bg", [P, 1])
        ones = s.sbuf("ones", [P, P], BF16)
        adj = s.sbuf("adj", [P, RING, UNIT, W])
        sim = s.sbuf("sim", [P, 2, UNIT, W])
        absent = s.sbuf("absent", [P, 2, UNIT, W], BF16)
        feat = s.sbuf("feat", [P, 2, W])
        counts = s.sbuf("counts", [1, N])
        head_ps = s.psum("head_ps", [P, 4, W])
        feat_ps = s.psum("feat_ps", [P, 2, W])
        count_ps = s.psum("count_ps", [P, 2, W])
        loaded, const_ready, hid_mm, hid_ready, g_mm, g_ready = map(
            s.sem, ("loaded", "const_ready", "hid_mm", "hid_ready", "g_mm", "g_ready"))
        adj_in = [s.sem(f"adj_in{r}") for r in range(RING)]
        square_ready = s.sem("square_ready")
        mask_ready = s.sem("mask_ready")
        sim_ready = s.sem("sim_ready")
        sim_used = s.sem("sim_used")
        mask_used = s.sem("mask_used")
        feat_ready = s.sem("feat_ready")
        counts_ready = s.sem("counts_ready")
        x_ready = s.sem("x_ready")
        stored, pool_turn = s.sem("stored"), s.sem("pool_turn")

        with nc.Block() as block:

            @block.sync
            def _(sp):
                for dst, src in ((xn[:, :], xn_dram), (wp[:, :], w_proj), (wg[:, :], w_gcn),
                                 (bp[:, :], b_proj), (bg[:, :], b_gcn), (x[:, :], x_dram)):
                    sp.dma_start(dst, src).then_inc(loaded, 16)
                with sp.Fori(0, CHUNKS) as c:
                    for k in range(UNITS):
                        sp.wait_ge(square_ready, c * UNITS + (k + 1))
                        sp.wait_ge(mask_ready, c * UNITS + (k + 1))
                        sp.dma_start(adj[:, k % RING, :, :],
                                     adj_dram[c, :, k * UNIT:(k + 1) * UNIT, :]).then_inc(adj_in[k % RING], 16)
                sp.wait_ge(x_ready, CHUNKS + 2)
                sp.dma_start(x_out, x[:, :]).then_inc(stored, 16)
                sp.wait_ge(counts_ready, CHUNKS + 2)
                sp.dma_start(absent_dram, counts[:, :]).then_inc(stored, 16)
                sp.wait_ge(stored, 32)

            @block.tensor
            def _(pe):
                pe.wait_ge(loaded, 6 * 16)
                for c in range(CHUNKS):
                    if c >= 4:
                        pe.wait_ge(hid_ready, c - 3)
                    nc.tensor.matmul(head_ps[:, c % 4, :], wp[:, :], xn[:, c * W:(c + 1) * W],
                                     start=True, stop=True).then_inc(hid_mm, 1)
                pe.wait_ge(hid_ready, CHUNKS)
                for c in range(CHUNKS):
                    if c >= 4:
                        pe.wait_ge(g_ready, c - 3)
                    for t in range(4):
                        j = c * 4 + t
                        last = nc.tensor.matmul(head_ps[:, c % 4, t * P:(t + 1) * P],
                                                hidden[:, j * P:(j + 1) * P], wg[:, :],
                                                start=True, stop=True)
                    last.then_inc(g_mm, 1)
                pe.wait_ge(g_ready, CHUNKS)
                pe.wait_ge(const_ready, 1)
                with pe.Fori(0, CHUNKS // 2) as c2:
                    for cc in range(2):
                        c = c2 * 2 + cc
                        pe.wait_ge(feat_ready, c + 1)
                        pe.wait_ge(counts_ready, c + 1)
                        for k in range(UNITS):
                            pe.wait_ge(sim_ready, c * UNITS + (k + 1))
                            for u in range(UNIT):
                                j = k * UNIT + u
                                last = nc.tensor.matmul(feat_ps[:, cc, :], g[:, j, :], sim[:, k % 2, u, :],
                                                        start=j == 0, stop=j == TILES - 1)
                            last.then_inc(sim_used, 1)
                            pe.wait_ge(mask_ready, c * UNITS + (k + 1 + RING))
                            for u in range(UNIT):
                                j = k * UNIT + u
                                last = nc.tensor.matmul(count_ps[:, cc, :], ones[:, :], absent[:, k % 2, u, :],
                                                        start=j == 0, stop=j == TILES - 1)
                            last.then_inc(mask_used, 1)

            @block.scalar
            def _(act):
                act.sem_inc(feat_ready, 2)
                act.wait_ge(loaded, 6 * 16)
                for c in range(CHUNKS):
                    act.wait_ge(hid_mm, c + 1)
                    nc.scalar.activation(hidden[:, c * W:(c + 1) * W], head_ps[:, c % 4, :], ACT.Tanh,
                                         bias=bp[:, 0:1]).then_inc(hid_ready, 1)
                with act.Fori(0, CHUNKS // 2) as c2:
                    for cc in range(2):
                        c = c2 * 2 + cc
                        for k in range(UNITS):
                            act.wait_ge(square_ready, c * UNITS + (k + 1 + RING))
                            nc.scalar.activation(sim[:, k % 2, :, :], sim[:, k % 2, :, :],
                                                 ACT.Tanh).then_inc(sim_ready, 1)
                        act.wait_ge(sim_used, c * UNITS + (UNITS + 2))
                        act.wait_ge(x_ready, c + 1)
                        nc.scalar.activation(feat[:, cc, :], feat_ps[:, cc, :], ACT.Relu,
                                             bias=bg[:, 0:1]).then_inc(feat_ready, 1)

            @block.gpsimd
            def _(pool):
                pool.sem_inc(mask_ready, RING)
                with pool.Fori(0, CHUNKS) as c:
                    for k in range(UNITS):
                        pool.wait_ge(adj_in[k % RING], c * (UNITS // RING * 16) + (k // RING + 1) * 16)
                        pool.wait_ge(mask_used, c * UNITS + (k + 1))
                        pool.sem_inc(pool_turn, 1)
                        nc.gpsimd.tensor_scalar(absent[:, k % 2, :, :], adj[:, k % RING, :, :], 0.0, None,
                                                ALU.is_equal).then_inc(mask_ready, 1)

            @block.vector
            def _(dve):
                nc.vector.memset(ones[:, :], 1.0).then_inc(const_ready, 1)
                dve.sem_inc(square_ready, RING)
                dve.sem_inc(sim_used, 2)
                dve.sem_inc(mask_used, 2)
                dve.sem_inc(counts_ready, 2)
                dve.sem_inc(x_ready, 2)
                for c in range(CHUNKS):
                    dve.wait_ge(g_mm, c + 1)
                    nc.vector.tensor_copy(g[:, 4 * c:4 * c + 4, :],
                                          head_ps[:, c % 4, :].rearrange("p (t d) -> p t d", t=4)).then_inc(g_ready, 1)
                dve.wait_ge(loaded, 6 * 16)
                with dve.Fori(0, CHUNKS // 2) as c2:
                    for cc in range(2):
                        c = c2 * 2 + cc
                        cs = bass.ds(c * W, W)
                        for k in range(UNITS):
                            dve.wait_ge(adj_in[k % RING], c * (UNITS // RING * 16) + (k // RING + 1) * 16)
                            dve.wait_ge(sim_used, c * UNITS + (k + 1))
                            nc.vector.scalar_tensor_tensor(
                                out=sim[:, k % 2, :, :], in0=adj[:, k % RING, :, :], scalar=0.0,
                                in1=adj[:, k % RING, :, :], op0=ALU.max, op1=ALU.mult).then_inc(square_ready, 1)
                        dve.wait_ge(mask_used, c * UNITS + (UNITS + 2))
                        nc.vector.tensor_scalar(counts[0:1, cs], count_ps[0:1, cc, :], 1.0, None,
                                                ALU.mult).then_inc(counts_ready, 1)
                        dve.wait_ge(feat_ready, c + 3)
                        nc.vector.tensor_tensor(x[:, cs], feat[:, cc, :], x[:, cs],
                                                ALU.add).then_inc(x_ready, 1)


def route(nc, stage, xn_dram, w_router, identity_dram, gates_dram, guard):
    E = 8
    with Scope(nc, stage) as s:
        xn = s.sbuf("xn", [P, N])
        wr = s.sbuf("wr", [P, E])
        ident = s.sbuf("ident", [P, P])
        rank = s.sbuf("rank", [P, TILES, E])
        rank_i = s.sbuf("rank_i", [P, TILES, E], mybir.dt.int32)
        prob, left, hit, pick1, pick2 = (s.sbuf(n, [P, TILES, E]) for n in ("prob", "left", "hit", "pick1", "pick2"))
        top, total, best1, best2 = (s.sbuf(n, [P, TILES]) for n in ("top", "total", "best1", "best2"))
        gates_t = s.sbuf("gates_t", [E, N])
        logit_ps = s.psum("logit_ps", [P, TILES, E])
        gate_ps = s.psum("gate_ps", [E, 4, W])
        loaded, ranked, logits, shifted, powers, step, gates_mm, gates_ready, stored = map(
            s.sem, ("loaded", "ranked", "logits", "shifted", "powers", "step", "gates_mm", "gates_ready", "stored"))

        with nc.Block() as block:

            @block.sync
            def _(sp):
                for dst, src in ((xn[:, :], xn_dram), (wr[:, :], w_router), (ident[:, :], identity_dram)):
                    sp.dma_start(dst, src).then_inc(loaded, 16)
                sp.wait_ge(gates_ready, CHUNKS)
                sp.dma_start(gates_dram, gates_t[:, :]).then_inc(stored, 16)
                sp.wait_ge(stored, 16)

            @block.tensor
            def _(pe):
                pe.wait_ge(loaded, 48)
                for t in range(TILES):
                    last = nc.tensor.matmul(logit_ps[:, t, :], xn[:, t * P:(t + 1) * P], wr[:, :],
                                            start=True, stop=True)
                last.then_inc(logits, 1)
                pe.wait_ge(step, (24 if guard else 23))
                for c in range(CHUNKS):
                    if c >= 4:
                        pe.wait_ge(gates_ready, c - 3)
                    for t in range(4):
                        last = nc.tensor.transpose(gate_ps[:, c % 4, t * P:(t + 1) * P],
                                                   prob[:, c * 4 + t, :], ident[:, :])
                    last.then_inc(gates_mm, 1)

            @block.scalar
            def _(act):
                act.wait_ge(shifted, 1)
                nc.scalar.activation(prob[:, :, :], prob[:, :, :], ACT.Exp).then_inc(powers, 1)

            @block.gpsimd
            def _(pool):
                nc.gpsimd.iota(rank_i[:, :, :], [[0, TILES], [-1, E]], base=E, channel_multiplier=0).then_inc(ranked, 1)

            @block.vector
            def _(dve):
                steps = 0

                def done(ins):
                    nonlocal steps
                    steps += 1
                    ins.then_inc(step, 1)
                    dve.wait_ge(step, steps)

                def wide(a):
                    return a[:, :].rearrange("p (t o) -> p t o", o=1).broadcast_to([P, TILES, E])

                dve.wait_ge(logits, 1)
                done(nc.vector.tensor_reduce(top[:, :], logit_ps[:, :, :], AX.X, ALU.max))
                nc.vector.tensor_tensor(prob[:, :, :], logit_ps[:, :, :], wide(top), ALU.subtract).then_inc(shifted, 1)
                dve.wait_ge(ranked, 1)
                done(nc.vector.tensor_copy(rank[:, :, :], rank_i[:, :, :]))
                dve.wait_ge(powers, 1)
                done(nc.vector.tensor_reduce(total[:, :], prob[:, :, :], AX.X, ALU.add))
                done(nc.vector.reciprocal(total[:, :], total[:, :]))
                done(nc.vector.tensor_tensor(prob[:, :, :], prob[:, :, :], wide(total), ALU.mult))
                done(nc.vector.tensor_copy(left[:, :, :], prob[:, :, :]))
                for best, pick in ((best1, pick1), (best2, pick2)):
                    done(nc.vector.tensor_reduce(best[:, :], left[:, :, :], AX.X, ALU.max))
                    done(nc.vector.tensor_tensor(hit[:, :, :], left[:, :, :], wide(best), ALU.is_equal))
                    done(nc.vector.tensor_tensor(hit[:, :, :], hit[:, :, :], rank[:, :, :], ALU.mult))
                    done(nc.vector.tensor_reduce(top[:, :], hit[:, :, :], AX.X, ALU.max))
                    done(nc.vector.tensor_tensor(pick[:, :, :], hit[:, :, :], wide(top), ALU.is_equal))
                    done(nc.vector.scalar_tensor_tensor(
                        out=left[:, :, :], in0=pick[:, :, :], scalar=-2.0, in1=left[:, :, :],
                        op0=ALU.mult, op1=ALU.add))
                done(nc.vector.tensor_tensor(total[:, :], best1[:, :], best2[:, :], ALU.add))
                if guard:
                    done(nc.vector.tensor_scalar(total[:, :], total[:, :], guard, None, ALU.add))
                done(nc.vector.reciprocal(total[:, :], total[:, :]))
                done(nc.vector.tensor_tensor(pick1[:, :, :], pick1[:, :, :], pick2[:, :, :], ALU.add))
                done(nc.vector.tensor_tensor(prob[:, :, :], prob[:, :, :], pick1[:, :, :], ALU.mult))
                done(nc.vector.tensor_tensor(prob[:, :, :], prob[:, :, :], wide(total), ALU.mult))
                for c in range(CHUNKS):
                    dve.wait_ge(gates_mm, c + 1)
                    nc.vector.tensor_copy(gates_t[:, c * W:(c + 1) * W], gate_ps[:, c % 4, :]).then_inc(gates_ready, 1)


def experts(nc, stage, x_dram, xn_dram, gates_dram, w_up, w_down, bias_up, bias_down, shared, widths, x_out):
    BLOCKS = len(widths)
    HID = sum(widths)
    EXPERTS = 9 if shared else 8
    UPS = 1 if shared else 2
    starts = [sum(widths[:b]) for b in range(BLOCKS)]
    PER = 2 * EXPERTS
    with Scope(nc, stage) as s:
        x = s.sbuf("x", [P, N])
        up = s.sbuf("up", [P, UPS, EXPERTS, HID])
        down = s.sbuf("down", [P, EXPERTS, BLOCKS, P])
        bup = s.sbuf("bup", [P, EXPERTS, BLOCKS])
        bdown = s.sbuf("bdown", [P, EXPERTS])
        xn = s.sbuf("xn", [P, 2, W])
        gates = s.sbuf("gates", [P, 2, 8, W])
        hid = s.sbuf("hid", [P, 2, BLOCKS, W])
        part = s.sbuf("part", [P, 2, W])
        up_ps = [s.psum(f"up_ps{i}", [P, BLOCKS, W]) for i in range(UPS)]
        y_ps = s.psum("y_ps", [P, 2, W])
        loaded = s.sem("loaded")
        xn_in = [s.sem(f"xn_in{i}") for i in range(2)]
        gates_in = [s.sem(f"gates_in{i}") for i in range(2)]
        xn_used = s.sem("xn_used")
        up_mm = s.sem("up_mm")
        act_ready = s.sem("act_ready")
        hid_ready = s.sem("hid_ready")
        y_mm = s.sem("y_mm")
        y_taken = s.sem("y_taken")
        summed = s.sem("summed")
        stored = s.sem("stored")
        hidden_done = act_ready if shared else hid_ready

        with nc.Block() as block:

            @block.sync
            def _(sp):
                sp.dma_start(up[:, :, :, :], w_up).then_inc(loaded, 16)
                sp.dma_start(down[:, :, :, :], w_down).then_inc(loaded, 16)
                sp.dma_start(x[:, :], x_dram).then_inc(loaded, 16)
                if shared:
                    sp.dma_start(bup[:, :, :], bias_up).then_inc(loaded, 16)
                    sp.dma_start(bdown[:, :], bias_down).then_inc(loaded, 16)
                with sp.Fori(0, CHUNKS // 2) as c2:
                    for cc in range(2):
                        c = c2 * 2 + cc
                        sp.wait_ge(xn_used, c + 1)
                        sp.dma_start(xn[:, cc, :], xn_dram[:, bass.ds(c * W, W)]).then_inc(xn_in[cc], 16)
                        sp.wait_ge(summed, c * EXPERTS + 1)
                        sp.dma_start(gates[:, cc, :, :], gates_dram[:, bass.ds(c * W, W)].rearrange(
                            "(o e) n -> o e n", o=1).broadcast_to([P, 8, W])).then_inc(gates_in[cc], 16)
                sp.wait_ge(summed, CHUNKS * EXPERTS + EXPERTS + 1)
                sp.dma_start(x_out, x[:, :]).then_inc(stored, 16)
                sp.wait_ge(stored, 16)

            @block.tensor
            def _(pe):
                pe.wait_ge(loaded, 16 * (5 if shared else 3))

                def expert_down(c2, q):
                    e = q % EXPERTS
                    pe.wait_ge(y_taken, c2 * PER + (q + 1))
                    for b in range(BLOCKS):
                        pe.wait_ge(hidden_done, c2 * (PER * BLOCKS) + (q * BLOCKS + b + 1 + BLOCKS))
                        last = nc.tensor.matmul(y_ps[:, q % 2, :], down[0:widths[b], e, b, :],
                                                hid[0:widths[b], q % 2, b, :],
                                                start=b == 0, stop=b == BLOCKS - 1)
                    last.then_inc(y_mm, 1)

                with pe.Fori(0, CHUNKS // 2) as c2:
                    for q in range(PER):
                        cc, e = divmod(q, EXPERTS)
                        if e == 0:
                            pe.wait_ge(xn_in[cc], c2 * 16 + 16)
                        for b in range(BLOCKS):
                            n = c2 * (PER * BLOCKS) + (q * BLOCKS + b + 1)
                            pe.wait_ge(act_ready, n)
                            if not shared:
                                pe.wait_ge(hid_ready, n)
                            for i in range(UPS):
                                last = nc.tensor.matmul(up_ps[i][0:widths[b], b, :],
                                                        up[:, i, e, starts[b]:starts[b] + widths[b]],
                                                        xn[:, cc, :], start=True, stop=True)
                            last.then_inc(up_mm, 1)
                        if e == EXPERTS - 1:
                            pe.wait_ge(up_mm, c2 * (PER * BLOCKS) + (q + 1) * BLOCKS)
                            pe.sem_inc(xn_used, 1)
                        if q:
                            expert_down(c2, q - 1)
                    expert_down(c2, PER - 1)

            @block.scalar
            def _(act):
                act.sem_inc(act_ready, BLOCKS)
                act.wait_ge(loaded, 16 * (5 if shared else 3))
                with act.Fori(0, CHUNKS // 2) as c2:
                    for q in range(PER):
                        e = q % EXPERTS
                        act.wait_ge(y_mm, c2 * PER + (q + 1))
                        for b in range(BLOCKS):
                            act.wait_ge(up_mm, c2 * (PER * BLOCKS) + (q * BLOCKS + b + 1))
                            to, src = hid[0:widths[b], q % 2, b, :], up_ps[0][0:widths[b], b, :]
                            if shared:
                                nc.scalar.activation(to, src, ACT.Gelu,
                                                     bias=bup[0:widths[b], e, b:b + 1]).then_inc(act_ready, 1)
                            else:
                                nc.scalar.activation(to, src, ACT.Silu).then_inc(act_ready, 1)

            @block.vector
            def _(dve):
                dve.sem_inc(xn_used, 2)
                dve.sem_inc(hid_ready, BLOCKS)
                dve.sem_inc(y_mm, 2)
                dve.sem_inc(y_taken, 2)
                dve.sem_inc(summed, EXPERTS + 1)
                dve.wait_ge(loaded, 16 * (5 if shared else 3))

                def gather_expert(c2, q):
                    cc, e = divmod(q, EXPERTS)
                    n = c2 * PER + q
                    xs = x[:, bass.ds((c2 * 2 + cc) * W, W)]
                    if e == 0:
                        dve.wait_ge(gates_in[cc], c2 * 16 + 16)
                    dve.wait_ge(y_mm, n + 3)
                    if shared and e == 0:
                        nc.vector.tensor_scalar(part[:, q % 2, :], y_ps[:, q % 2, :], bdown[:, 0:1], None,
                                                ALU.add).then_inc(y_taken, 1)
                    elif shared:
                        nc.vector.scalar_tensor_tensor(
                            out=part[:, q % 2, :], in0=y_ps[:, q % 2, :], scalar=bdown[:, e:e + 1],
                            in1=gates[:, cc, e - 1, :], op0=ALU.add, op1=ALU.mult).then_inc(y_taken, 1)
                    else:
                        nc.vector.tensor_tensor(part[:, q % 2, :], y_ps[:, q % 2, :], gates[:, cc, e, :],
                                                ALU.mult).then_inc(y_taken, 1)
                    dve.wait_ge(y_taken, n + 3)
                    dve.wait_ge(summed, n + (EXPERTS + 1))
                    nc.vector.tensor_tensor(xs, xs, part[:, q % 2, :], ALU.add).then_inc(summed, 1)

                with dve.Fori(0, CHUNKS // 2) as c2:
                    for q in range(PER):
                        if not shared:
                            for b in range(BLOCKS):
                                n = c2 * (PER * BLOCKS) + (q * BLOCKS + b + 1)
                                dve.wait_ge(act_ready, n + BLOCKS)
                                h = hid[0:widths[b], q % 2, b, :]
                                nc.vector.tensor_tensor(h, h, up_ps[1][0:widths[b], b, :],
                                                        ALU.mult).then_inc(hid_ready, 1)
                        if q:
                            gather_expert(c2, q - 1)
                    gather_expert(c2, PER - 1)


def attention(nc, x_dram, xn_dram, adj_dram, absent_dram, w_t, bias, a_parent, a_child,
              head_cols, head_blocks, bands, scales, identity_dram, x_out):
    UNIT = 2
    UNITS = TILES // UNIT
    GROUP = 4
    PAIR = 4 * PART
    RING = 4
    with Scope(nc, "attn") as s:
        vz = s.sbuf("vz", [P, TILES, HEADS // 2, PAIR], BF16)
        feats = s.sbuf("feats", [P, TILES, 3, P], BF16)
        gap = s.sbuf("gap", [P, TILES, HEADS])
        cmax = s.sbuf("cmax", [P, HEADS])
        cmax_col = s.sbuf("cmax_col", [P, 1])
        wt, parent_block = s.sbuf("wt", [P, P]), s.sbuf("parent_block", [P, P])
        parent_rep = s.sbuf("parent_rep", [P, HEADS, P])
        bcol, acol, pcol = s.sbuf("bcol", [P, 1]), s.sbuf("acol", [P, 1]), s.sbuf("pcol", [P, 1])
        heads8 = s.sbuf("heads8", [P, HEADS])
        blocks = s.sbuf("blocks", [P, P])

        with Scope(nc, "nodes") as t:
            xn = t.sbuf("xn", [P, N])
            nf_t = t.sbuf("nf_t", [P, N])
            nf = t.sbuf("nf", [P, TILES, P])
            ident = t.sbuf("ident", [P, P])
            child8 = t.sbuf("child8", [P, HEADS])
            child = t.sbuf("child", [P, TILES, HEADS])
            top8, picked = t.sbuf("top8", [P, HEADS]), t.sbuf("picked", [P, HEADS])
            w_v, w_z = t.sbuf("w_v", [P, TILES, HEADS]), t.sbuf("w_z", [P, TILES, HEADS])
            SLAB = 4
            full, rest = (t.sbuf(n, [P, SLAB, HEADS // 2, COLS]) for n in ("full", "rest"))
            rest_f = t.sbuf("rest_f", [P, TILES, P])
            nf_ps = t.psum("nf_ps", [P, 2, W])
            tr_ps = t.psum("tr_ps", [P, 4, W])
            child_ps = t.psum("child_ps", [P, TILES, HEADS])
            loaded, child_const, nf_mm, nf_ready, tr_mm, tr_ready, child_mm, step, reduced, exps = map(
                t.sem, ("loaded", "child_const", "nf_mm", "nf_ready", "tr_mm", "tr_ready", "child_mm", "step",
                        "reduced", "exps"))
            with nc.Block() as block:

                @block.sync
                def _(sp):
                    for dst, src in ((xn, xn_dram), (wt, w_t), (bcol, bias), (acol, a_child), (pcol, a_parent),
                                     (heads8, head_cols), (blocks, head_blocks), (ident, identity_dram)):
                        sp.dma_start(dst[:, :], src).then_inc(loaded, 16)

                @block.tensor
                def _(pe):
                    pe.wait_ge(loaded, 8 * 16)
                    for c in range(CHUNKS):
                        if c >= 2:
                            pe.wait_ge(nf_ready, c - 1)
                        nc.tensor.matmul(nf_ps[:, c % 2, :], wt[:, :], xn[:, c * W:(c + 1) * W],
                                         start=True, stop=True).then_inc(nf_mm, 1)
                    pe.wait_ge(nf_ready, CHUNKS)
                    for c in range(CHUNKS):
                        if c >= 4:
                            pe.wait_ge(tr_ready, c - 3)
                        for k in range(4):
                            j = c * 4 + k
                            last = nc.tensor.transpose(tr_ps[:, c % 4, k * P:(k + 1) * P],
                                                       nf_t[:, j * P:(j + 1) * P], ident[:, :])
                        last.then_inc(tr_mm, 1)
                    pe.wait_ge(child_const, 1)
                    for j in range(TILES):
                        last = nc.tensor.matmul(child_ps[:, j, :], nf_t[:, j * P:(j + 1) * P], child8[:, :],
                                                start=True, stop=True)
                    last.then_inc(child_mm, 1)

                @block.scalar
                def _(act):
                    act.wait_ge(loaded, 8 * 16)
                    for c in range(CHUNKS):
                        act.wait_ge(nf_mm, c + 1)
                        nc.scalar.activation(nf_t[:, c * W:(c + 1) * W], nf_ps[:, c % 2, :], ACT.Identity,
                                             bias=bcol[:, 0:1]).then_inc(nf_ready, 1)
                    act.wait_ge(step, 3)
                    nc.scalar.activation(w_v[:, :, :], gap[:, :, :], ACT.Exp, scale=-0.2).then_inc(exps, 1)
                    nc.scalar.activation(w_z[:, :, :], gap[:, :, :], ACT.Exp, scale=-1.0).then_inc(exps, 1)

                @block.gpsimd
                def _(pool):
                    pool.wait_ge(step, 2)
                    nc.gpsimd.partition_all_reduce(cmax[:, :], top8[:, :], P, bass.bass_isa.ReduceOp.max).then_inc(reduced, 1)

                @block.vector
                def _(dve):
                    steps = 0

                    def done(ins):
                        nonlocal steps
                        steps += 1
                        ins.then_inc(step, 1)
                        dve.wait_ge(step, steps)

                    dve.wait_ge(loaded, 8 * 16)
                    nc.vector.tensor_scalar(child8[:, :], heads8[:, :], acol[:, 0:1], None,
                                            ALU.mult).then_inc(child_const, 1)
                    for c in range(CHUNKS):
                        dve.wait_ge(tr_mm, c + 1)
                        nc.vector.tensor_copy(nf[:, 4 * c:4 * c + 4, :],
                                              tr_ps[:, c % 4, :].rearrange("p (k d) -> p k d", k=4)).then_inc(tr_ready, 1)
                    dve.wait_ge(child_mm, 1)
                    done(nc.vector.tensor_copy(child[:, :, :], child_ps[:, :, :]))
                    done(nc.vector.tensor_reduce(top8[:, :], child[:, :, :].rearrange("p t h -> p h t"), AX.X, ALU.max))
                    dve.wait_ge(reduced, 1)
                    done(nc.vector.tensor_tensor(
                        gap[:, :, :], cmax[:, :].rearrange("p (o h) -> p o h", o=1).broadcast_to([P, TILES, HEADS]),
                        child[:, :, :], ALU.subtract))
                    done(nc.vector.tensor_tensor(picked[:, :], cmax[:, :], heads8[:, :], ALU.mult))
                    done(nc.vector.tensor_reduce(cmax_col[:, :], picked[:, :], AX.X, ALU.add))
                    done(nc.vector.tensor_scalar(parent_block[:, :], blocks[:, :], pcol[:, 0:1], None, ALU.mult))
                    done(nc.vector.tensor_scalar(picked[:, :], heads8[:, :], pcol[:, 0:1], None, ALU.mult))
                    done(nc.vector.tensor_copy(parent_rep[:, :, :], picked[:, :].rearrange(
                        "p (h o) -> p h o", o=1).broadcast_to([P, HEADS, P])))
                    dve.wait_ge(tr_ready, CHUNKS)
                    done(nc.vector.tensor_copy(feats[:, :, 0, :], nf[:, :, :]))
                    done(nc.vector.tensor_tensor(rest_f[:, :, :], nf[:, :, :], feats[:, :, 0, :], ALU.subtract))
                    done(nc.vector.tensor_copy(feats[:, :, 1, :], rest_f[:, :, :]))
                    done(nc.vector.tensor_tensor(rest_f[:, :, :], rest_f[:, :, :], feats[:, :, 1, :], ALU.subtract))
                    done(nc.vector.tensor_copy(feats[:, :, 2, :], rest_f[:, :, :]))
                    dve.wait_ge(exps, 2)
                    base = steps
                    PER = 4 * 7
                    with dve.Fori(0, TILES // SLAB) as slab:
                        n = 0

                        def next_step(ins):
                            nonlocal n
                            n += 1
                            ins.then_inc(step, 1)
                            dve.wait_ge(step, slab * PER + (base + n))

                        rows = bass.ds(slab * SLAB, SLAB)
                        for weight, odd, at in ((w_v, 0, 0), (w_z, 0, PART), (w_z, 1, 2 * PART), (w_v, 1, 3 * PART)):
                            wh = weight[:, rows, odd::2]
                            fh = nf[:, rows, :].rearrange("p t (a b d) -> p t a b d", b=2, d=HD)[:, :, :, odd, :]
                            next_step(nc.vector.tensor_tensor(
                                full[:, :, :, 0:HD], fh, wh.rearrange("p t (a o) -> p t a o", o=1).broadcast_to(
                                    [P, SLAB, HEADS // 2, HD]), ALU.mult))
                            next_step(nc.vector.tensor_scalar(full[:, :, :, HD], wh, 1.0, None, ALU.mult))
                            for part in range(3):
                                to = vz[:, rows, :, at + part * COLS:at + (part + 1) * COLS]
                                next_step(nc.vector.tensor_scalar(to, (full if part == 0 else rest)[:, :, :, :], 1.0, None,
                                                                  ALU.mult))
                                if part < 2:
                                    next_step(nc.vector.tensor_tensor(
                                        rest[:, :, :, :], (full if part == 0 else rest)[:, :, :, :], to, ALU.subtract))

        EVENTS = 14
        TAIL_NUM, TAIL_DEN, P_FEAT, U_LATE, NUM, DEN, FEATS, U_EARLY = 1, 2, 3, 4, 8, 9, 10, 11
        HOLE_AT = {3 + tile * 15 // 8: tile for tile in range(TILES)}
        RAW = 2

        def by_act(g, j):
            return 3 if g == 0 or j % 2 else 2

        BIG = 2.0 ** 64

        def event(c, e):
            return c * EVENTS + (3 + e)

        with Scope(nc, "rows") as t:
            band = t.sbuf("band", [P, 6, SELW])
            xn, x, absent = t.sbuf("xn", [P, W]), t.sbuf("x", [P, W]), t.sbuf("absent", [P, W])
            nf_c = t.sbuf("nf_c", [P, W])
            adj = t.sbuf("adj", [P, 2, UNIT, W])
            holes = t.sbuf("holes", [P, 2, UNIT, W], BF16)
            edges = t.sbuf("edges", [P, TILES, W], BF16)
            raw = t.sbuf("raw", [P, RAW, 3, W], BF16)
            picked = t.sbuf("picked", [P, RING, GROUP, W], BF16)
            u = t.sbuf("u", [P, HEADS, W])
            rho = t.sbuf("rho", [P, 2, W])
            scale_vz = t.sbuf("scale_vz", [P, 2])
            big_gap = t.sbuf("big_gap", [P, TILES, HEADS])
            sums = t.sbuf("sums", [P, GROUP, W])
            zsums = t.sbuf("zsums", [P, 2, W])
            hole_sum = t.sbuf("hole_sum", [P, W])
            scales_i = t.sbuf("scales_i", [P, 2, W])
            total = t.sbuf("total", [P, 2, W])
            misc_ps = t.psum("misc_ps", [P, W])
            sel_ps = t.psum("sel_ps", [P, GROUP, W])
            hole_ps = t.psum("hole_ps", [P, W])
            pair_ps = t.psum("pair_ps", [P, 2, W])
            const_in, chunk_in, x_in, big_ready, pool_turn = map(
                t.sem, ("const_in", "chunk_in", "x_in", "big_ready", "pool_turn"))
            adj_in = [t.sem(f"adj_in{i}") for i in range(2)]
            stored = t.sem("stored")
            holes_ready = t.sem("holes_ready")
            holes_used = t.sem("holes_used")
            edges_ready = t.sem("edges_ready")
            raw_ready = t.sem("raw_ready")
            picked_ready = t.sem("picked_ready")
            step_mm = t.sem("step_mm")
            misc_mm = t.sem("misc_mm")
            misc_taken = t.sem("misc_taken")
            rho_ready = t.sem("rho_ready")
            sums_ready = t.sem("sums_ready")
            zsums_ready = t.sem("zsums_ready")
            hole_taken = t.sem("hole_taken")
            bounds_ready, scales_ready = t.sem("bounds_ready"), t.sem("scales_ready")
            final = t.sem("final")
            x_ready = t.sem("x_ready")
            FINAL = 7

            def u_taken(c, g):
                if g == 1:
                    return event(c, NUM)
                return event(c, TAIL_NUM) if not isinstance(c, int) else 1 + 5

            def each_chunk(eng, run, after):
                run(0, False)
                with eng.Fori(1, CHUNKS) as c:
                    run(c, True)
                after(CHUNKS)

            with nc.Block() as block:

                @block.sync
                def _(sp):
                    def load_adj(chunk, c, k):
                        sp.wait_ge(edges_ready, c * UNITS + (k + 1))
                        sp.dma_start(adj[:, k % 2, :, :], adj_dram[chunk, :, (k % UNITS) * UNIT:(k % UNITS + 1) * UNIT, :]
                                     ).then_inc(adj_in[k % 2], 16)

                    def load_last(c):
                        cs = bass.ds((c - 1) * W, W)
                        sp.wait_ge(stored, c * 16)
                        sp.dma_start(x[:, :], x_dram[:, cs]).then_inc(x_in, 16)
                        sp.wait_ge(x_in, c * 32 - 16)
                        sp.dma_start(absent[:, :], absent_dram[:, cs].broadcast_to([P, W])).then_inc(x_in, 16)

                    def store_last(c):
                        sp.wait_ge(x_ready, c + 1)
                        sp.dma_start(x_out[:, bass.ds((c - 1) * W, W)], x[:, :]).then_inc(stored, 16)

                    def run(c, tail):
                        following = (c + 1) % CHUNKS
                        sp.wait_ge(misc_mm, event(c, -2))
                        sp.dma_start(xn[:, :], xn_dram[:, bass.ds(following * W, W)]).then_inc(chunk_in, 16)
                        for k in range(2, UNITS):
                            load_adj(c, c, k)
                            if k == 3 and tail:
                                load_last(c)
                        load_adj(following, c, UNITS)
                        load_adj(following, c, UNITS + 1)
                        if tail:
                            store_last(c)

                    def after(c):
                        load_last(c)
                        store_last(c)
                        sp.wait_ge(stored, CHUNKS * 16 + 16)
                        for i in range(2):
                            sp.wait_ge(adj_in[i], (CHUNKS * UNITS // 2 + 1) * 16)
                        sp.wait_ge(chunk_in, (CHUNKS + 1) * 16)

                    sp.dma_start(band[:, :, :], bands).then_inc(const_in, 16)
                    sp.dma_start(scale_vz[:, :], scales).then_inc(const_in, 16)
                    sp.dma_start(xn[:, :], xn_dram[:, 0:W]).then_inc(chunk_in, 16)
                    load_adj(0, 0, 0)
                    load_adj(0, 0, 1)
                    each_chunk(sp, run, after)

                @block.tensor
                def _(pe):
                    def through_misc(number, w, rhs):
                        pe.wait_ge(misc_taken, number)
                        nc.tensor.matmul(misc_ps[:, :], w, rhs, start=True, stop=True).then_inc(misc_mm, 1)

                    def gather(c, e, g, nd, at):
                        if at == 0:
                            pe.wait_ge(misc_taken, event(c, e))
                        for i in ((0, 1), (2, 3), (4, 5))[at]:
                            if i < GROUP:
                                off = (HEADS - 1 - (GROUP * g + i)) * HD
                                w, rhs = band[0:2 * PART, 2 * (i % 2) + nd, off:off + P], sums[0:2 * PART, i, :]
                            else:
                                off = (HEADS - 1 - (GROUP * g + 2 * (i - GROUP))) * HD
                                w, rhs = band[0:2 * PART, 4 + nd, off:off + P], zsums[0:2 * PART, i - GROUP, :]
                            last = nc.tensor.matmul(misc_ps[:, :], w, rhs, start=i == 0, stop=i == 5)
                        if at == 2:
                            last.then_inc(misc_mm, 1)

                    def gather_when_ready(c, n, e, g, at, nd):
                        if at == 0 and nd == 0:
                            pe.wait_ge(sums_ready, n * GROUP + (GROUP + 2))
                            pe.wait_ge(zsums_ready, n + 2)
                        gather(c, e, g, nd, at)

                    def run(c, tail):
                        for g in range(2):
                            n = c * 2 + g
                            for j in range(TILES):
                                first, final_ = j == 0, j == TILES - 1
                                if first:
                                    pe.wait_ge(zsums_ready, n + 1)
                                k = j // UNIT
                                if g * TILES + j in HOLE_AT:
                                    tile = HOLE_AT[g * TILES + j]
                                    kb = tile // UNIT
                                    if tile == 0:
                                        pe.wait_ge(hole_taken, c + 1)
                                    pe.wait_ge(holes_ready, c * UNITS + (kb + 1 + UNITS))
                                    for part in range(3):
                                        last = nc.tensor.matmul(
                                            hole_ps[:, :], feats[:, tile, part, :],
                                            holes[:, kb % 2, tile % UNIT, :],
                                            start=tile == 0 and part == 0, stop=tile == TILES - 1 and part == 2)
                                    if tile % UNIT == UNIT - 1:
                                        last.then_inc(holes_used, 1)
                                if g == 0:
                                    pe.wait_ge(edges_ready, c * UNITS + (k + 3))
                                for pr in range(2):
                                    nc.tensor.matmul(pair_ps[0:2 * PART, pr, :],
                                                     vz[:, j, 2 * g + pr, PART:3 * PART], edges[:, j, :],
                                                     start=first, stop=final_)
                                if first:
                                    pe.wait_ge(sums_ready, n * GROUP + 2)
                                pe.wait_ge(picked_ready, n * TILES + (j + 1 + RAW))
                                for i in range(GROUP):
                                    at = (i % 2) * 2 * PART
                                    last = nc.tensor.matmul(sel_ps[0:2 * PART, i, :],
                                                            vz[:, j, 2 * g + i // 2, at:at + 2 * PART],
                                                            picked[:, j % RING, i, :],
                                                            start=first, stop=final_)
                                last.then_inc(step_mm, 1)
                                if g == 1 or tail:
                                    e = NUM if g == 1 else TAIL_NUM
                                    if j in (3, 4, 5):
                                        gather_when_ready(c, n - 1, e, 1 - g, j - 3, 0)
                                    if j in (8, 9, 10):
                                        gather_when_ready(c, n - 1, e + 1, 1 - g, j - 8, 1)
                                if j == 13:
                                    if g == 0:
                                        through_misc(event(c, P_FEAT), parent_block[:, :], nf_c[:, :])
                                    else:
                                        pe.wait_ge(chunk_in, c * 16 + 32)
                                        through_misc(event(c, FEATS), wt[:, :], xn[:, :])
                                if j in (16, 19, 22, 25):
                                    i = (j - 16) // 3
                                    through_misc(event(c, (U_LATE, U_EARLY)[g] + i),
                                                 parent_rep[:, GROUP * (1 - g) + i, :], nf_c[:, :])

                    def after(c):
                        for nd in range(2):
                            for at in range(3):
                                gather_when_ready(c, c * 2 - 1, TAIL_NUM + nd, 1, at, nd)

                    pe.wait_ge(const_in, 32)
                    pe.wait_ge(chunk_in, 16)
                    through_misc(1, wt[:, :], xn[:, :])
                    for i in range(GROUP):
                        through_misc(2 + i, parent_rep[:, i, :], nf_c[:, :])
                    each_chunk(pe, run, after)

                @block.gpsimd
                def _(pool):
                    pool.sem_inc(holes_ready, UNITS)
                    with pool.Fori(0, CHUNKS) as c:
                        for k in range(UNITS):
                            pool.wait_ge(edges_ready, c * UNITS + (k + 3))
                            pool.wait_ge(holes_used, c * UNITS + (k + 1))
                            pool.sem_inc(pool_turn, 1)
                            nc.gpsimd.tensor_scalar(holes[:, k % 2, :, :],
                                                    edges[:, k * UNIT:(k + 1) * UNIT, :], 0.0, None,
                                                    ALU.is_equal).then_inc(holes_ready, 1)

                @block.scalar
                def _(act):
                    def take_feats(number):
                        act.wait_ge(misc_mm, number)
                        nc.scalar.activation(nf_c[:, :], misc_ps[:, :], ACT.Identity,
                                             bias=bcol[:, 0:1]).then_inc(misc_taken, 1)

                    def take_u(number, h):
                        act.wait_ge(misc_mm, number)
                        nc.scalar.activation(u[:, h, :], misc_ps[:, :], ACT.Relu,
                                             bias=cmax[:, h:h + 1]).then_inc(misc_taken, 1)

                    def make_rho(n, g, i):
                        act.wait_ge(sums_ready, n * GROUP + (i + 1))
                        nc.scalar.activation(rho[:, i % 2, :], u[:, GROUP * g + i, :], ACT.Exp,
                                             scale=scale_vz[:, i % 2:i % 2 + 1]).then_inc(rho_ready, 1)

                    def close_group(c, n, g):
                        act.wait_ge(step_mm, n * TILES + 2 * TILES)
                        act.wait_ge(misc_mm, event(c, DEN if g == 1 else TAIL_DEN))
                        if g == 0:
                            act.wait_ge(x_ready, c + 1)
                        else:
                            act.wait_ge(holes_used, c * UNITS + (UNITS + 2))
                            nc.scalar.copy(hole_sum[:, :], hole_ps[:, :]).then_inc(hole_taken, 1)
                        nc.scalar.copy(zsums[0:2 * PART, :, :],
                                       pair_ps[0:2 * PART, :, :]).then_inc(zsums_ready, 1)
                        make_rho(n, g, 2)
                        make_rho(n, g, 3)

                    def run(c, tail):
                        for g in range(2):
                            n = c * 2 + g
                            act.wait_ge(misc_taken, u_taken(c, g))
                            for j in range(TILES):
                                act.wait_ge(picked_ready, n * TILES + (j + 1))
                                for i in range(by_act(g, j)):
                                    h = GROUP * (g + 1) - by_act(g, j) + i
                                    last = nc.scalar.activation(raw[:, j % RAW, i, :], u[:, h, :], ACT.Relu,
                                                                bias=big_gap[:, j, h:h + 1], scale=-BIG)
                                last.then_inc(raw_ready, 1)
                                if j == 1:
                                    if g == 1:
                                        close_group(c, n - 1, 0)
                                    elif tail:
                                        close_group(c - 1, n - 1, 1)
                                if g == 1 and j in (8, 13):
                                    nd = (j - 8) // 5
                                    act.wait_ge(misc_mm, event(c, NUM + nd))
                                    nc.scalar.copy(total[:, nd, :], misc_ps[:, :]).then_inc(misc_taken, 1)
                                if g == 1 and j == 16:
                                    take_feats(event(c, FEATS))
                                if j in (19, 22, 25, 28):
                                    i = (j - 19) // 3
                                    take_u(event(c, (U_LATE, U_EARLY)[g] + i), GROUP * (1 - g) + i)
                                if g == 0 and j == 20:
                                    act.wait_ge(bounds_ready, c + 1)
                                    act.wait_ge(misc_taken, event(c, P_FEAT + 1))
                                    nc.scalar.activation(scales_i[:, 0, :], scales_i[:, 0, :], ACT.Exp,
                                                         scale=0.2).then_inc(scales_ready, 1)
                                    nc.scalar.activation(scales_i[:, 1, :], scales_i[:, 1, :], ACT.Exp,
                                                         scale=-1.0).then_inc(scales_ready, 1)
                                if j in (29, 30):
                                    make_rho(n, g, j - 29)

                    def after(c):
                        close_group(c - 1, c * 2 - 1, 1)

                    act.wait_ge(const_in, 32)
                    act.wait_ge(big_ready, 1)
                    take_feats(1)
                    for i in range(GROUP):
                        take_u(2 + i, i)
                    each_chunk(act, run, after)

                @block.vector
                def _(dve):
                    def make_edges(c, k):
                        dve.wait_ge(adj_in[k % 2], c * (UNITS // 2 * 16) + (k // 2 + 1) * 16)
                        dve.wait_ge(step_mm, c * (2 * TILES) + (k + 1) * UNIT)
                        dve.wait_ge(holes_ready, c * UNITS + (k + 1))
                        nc.vector.tensor_scalar(edges[:, k * UNIT:(k + 1) * UNIT, :], adj[:, k % 2, :, :],
                                                0.0, None, ALU.not_equal).then_inc(edges_ready, 1)

                    def take_sums(c, n, g):
                        dve.wait_ge(step_mm, n * TILES + 2 * TILES)
                        dve.wait_ge(misc_mm, event(c, DEN if g == 1 else TAIL_DEN))
                        for i in range(GROUP):
                            dve.wait_ge(rho_ready, n * GROUP + (i + 1))
                            nc.vector.tensor_tensor(sums[0:2 * PART, i, :], sel_ps[0:2 * PART, i, :],
                                                    rho[0:2 * PART, i % 2, :], ALU.mult).then_inc(sums_ready, 1)

                    def finish(c, part):
                        done = (c - 1) * FINAL
                        both = zsums[:, :, :]
                        if part in (0, 1):
                            if part == 0:
                                dve.wait_ge(misc_taken, event(c - 1, DEN + 1))
                            dve.wait_ge(misc_mm, event(c, TAIL_NUM + part))
                            nc.vector.tensor_tensor(total[:, part, :], total[:, part, :], misc_ps[:, :],
                                                    ALU.add).then_inc(misc_taken, 1)
                        elif part == 2:
                            dve.wait_ge(misc_taken, event(c, TAIL_DEN + 1))
                            dve.wait_ge(scales_ready, c * 2)
                            dve.wait_ge(x_in, c * 32)
                            for nd in range(2):
                                nc.vector.tensor_tensor(total[:, nd, :], total[:, nd, :], scales_i[:, 0, :],
                                                        ALU.mult).then_inc(final, 1)
                            nc.vector.tensor_tensor(both[:, 1, :], absent[:, :], scales_i[:, 1, :],
                                                    ALU.mult).then_inc(final, 1)
                        elif part == 3:
                            dve.wait_ge(hole_taken, c + 1)
                            nc.vector.tensor_tensor(both[:, 0, :], hole_sum[:, :], scales_i[:, 1, :],
                                                    ALU.mult).then_inc(final, 1)
                        elif part == 4:
                            dve.wait_ge(final, done + 4)
                            nc.vector.tensor_tensor(total[:, :, :], total[:, :, :], both, ALU.add).then_inc(final, 1)
                        elif part == 5:
                            dve.wait_ge(final, done + 5)
                            nc.vector.reciprocal(total[:, 1, :], total[:, 1, :]).then_inc(final, 1)
                        elif part == 6:
                            dve.wait_ge(final, done + 6)
                            nc.vector.tensor_tensor(total[:, 0, :], total[:, 0, :], total[:, 1, :],
                                                    ALU.mult).then_inc(final, 1)
                        else:
                            dve.wait_ge(final, done + 7)
                            nc.vector.tensor_tensor(x[:, :], x[:, :], total[:, 0, :], ALU.add).then_inc(x_ready, 1)

                    def run(c, tail):
                        for g in range(2):
                            n = c * 2 + g
                            dve.wait_ge(misc_taken, u_taken(c, g))
                            for j in range(TILES):
                                if g == 0 and j % UNIT == 0:
                                    if j == 0:
                                        make_edges(c, 0)
                                    if j // UNIT + 1 < UNITS:
                                        make_edges(c, j // UNIT + 1)
                                    dve.wait_ge(edges_ready, c * UNITS + (j // UNIT + 3))
                                dve.wait_ge(step_mm, n * TILES + (j + TILES - RING + 1))
                                mine = GROUP - by_act(g, j)
                                for i in range(mine):
                                    h = GROUP * g + i
                                    nc.vector.scalar_tensor_tensor(
                                        out=picked[:, j % RING, i, :], in0=u[:, h, :], scalar=gap[:, j, h:h + 1],
                                        in1=edges[:, j, :], op0=ALU.is_lt, op1=ALU.mult)
                                dve.wait_ge(raw_ready, n * TILES + (j + 1))
                                nc.vector.tensor_tensor(
                                    picked[:, j % RING, mine:GROUP, :], raw[:, j % RAW, 0:by_act(g, j), :],
                                    edges[:, j:j + 1, :].broadcast_to([P, by_act(g, j), W]),
                                    ALU.min).then_inc(picked_ready, 1)
                                if j == 1:
                                    if g == 1:
                                        take_sums(c, n - 1, 0)
                                    elif tail:
                                        take_sums(c - 1, n - 1, 1)
                                if g == 0 and tail and j in (8, 13, 14, 15, 17, 18, 19, 21):
                                    finish(c, (8, 13, 14, 15, 17, 18, 19, 21).index(j))
                                if g == 0 and j == 16:
                                    if tail:
                                        dve.wait_ge(final, (c - 1) * FINAL + 4)
                                    dve.wait_ge(misc_mm, event(c, P_FEAT))
                                    nc.vector.tensor_scalar(scales_i[:, 0, :], misc_ps[:, :], cmax_col[:, 0:1], 0.0,
                                                            ALU.add, ALU.min).then_inc(bounds_ready, 1)
                                    nc.vector.tensor_scalar(scales_i[:, 1, :], misc_ps[:, :], cmax_col[:, 0:1], 0.0,
                                                            ALU.add, ALU.max).then_inc(misc_taken, 1)

                    def after(c):
                        take_sums(c - 1, c * 2 - 1, 1)
                        for part in range(8):
                            finish(c, part)

                    for one, start in ((x_ready, 1), (hole_taken, 1), (misc_taken, 1), (zsums_ready, 1), (sums_ready, 2),
                                       (picked_ready, RAW), (stored, 16), (holes_used, 2), (edges_ready, 2),
                                       (step_mm, TILES)):
                        dve.sem_inc(one, start)
                    nc.vector.tensor_scalar(big_gap[:, :, :], gap[:, :, :], BIG, None, ALU.mult).then_inc(big_ready, 1)
                    each_chunk(dve, run, after)


def network(nc, a, out):
    def scratch(name, shape):
        return nc.dram_tensor(name, shape, F32, kind="Internal").ap()

    x1, x2, x3 = (scratch(f"x{i}", [P, N]) for i in (1, 2, 3))
    xn = [scratch(f"xn{i}", [P, N]) for i in range(4)]
    gates = [scratch(f"gates{i}", [8, N]) for i in range(2)]
    absent = scratch("absent", [1, N])

    layer_norm(nc, "norm0", a["x_t"], xn[0], a["row_of"])
    filtered_graph(nc, a["x_t"], xn[0], a["adj"], a["w_proj"], a["b_proj"], a["w_gcn"], a["b_gcn"], x1, absent)
    layer_norm(nc, "norm1", x1, xn[1], a["row_of"])
    route(nc, "route0", xn[1], a["w_router0"], a["identity"], gates[0], None)
    experts(nc, "ffn0", x1, xn[1], gates[0], a["up0"], a["down0"], a["bias_up0"], a["bias_down0"],
            True, [P] * 4, x2)
    layer_norm(nc, "norm2", x2, xn[2], a["row_of"])
    attention(nc, x2, xn[2], a["adj"], absent, a["w_attn"], a["b_attn"], a["a_parent"], a["a_child"],
              a["head_cols"], a["head_blocks"], a["bands"], a["scales"], a["identity"], x3)
    layer_norm(nc, "norm3", x3, xn[3], a["row_of"])
    route(nc, "route1", xn[3], a["w_router1"], a["identity"], gates[1], 1e-9)
    experts(nc, "ffn1", x3, xn[3], gates[1], a["up1"], a["down1"], None, None, False, [P, P, 85], out)


def kernel(**inputs):
    import numpy as np
    import concourse.bacc as bacc
    from concourse.bass_utils import run_bass_kernel_spmd as run

    v = {k: np.asarray(t) for k, t in inputs.items()}
    heads = np.arange(P) // HD
    bands = np.zeros((P, 6, SELW), np.float32)
    for part in range(3):
        for blk in range(2):
            r = blk * PART + part * COLS
            for kind in range(3):
                sign = 1.0 if kind == 2 or (kind == 0) == (blk == 0) else -1.0
                at = P - HD + (HD if kind == 2 and blk == 1 else 0)
                for d in range(HD):
                    bands[r + d, 2 * kind, at + d] = sign
                    bands[r + HD, 2 * kind + 1, at + d] = sign
    scales = np.zeros((P, 2), np.float32)
    scales[0:PART, 0] = -0.8
    scales[PART:2 * PART, 1] = -0.8

    def pad_rows(w, rows):
        return np.concatenate([w, np.zeros((rows - w.shape[0],) + w.shape[1:], w.dtype)], 0)

    hid1 = v["L1_ffn_w1"].shape[1]
    up0 = np.concatenate([v["L0_ffn_W1s"][None], v["L0_ffn_W1p"]], 0)
    down0 = np.concatenate([v["L0_ffn_W2s"][None], v["L0_ffn_W2p"]], 0)
    b_up0 = np.concatenate([v["L0_ffn_b1s"][None], v["L0_ffn_b1p"]], 0)
    b_down0 = np.concatenate([v["L0_ffn_b2s"][None], v["L0_ffn_b2p"]], 0)
    down1 = np.stack([pad_rows(w.T, 3 * P) for w in v["L1_ffn_w2"]])
    arrays = {
        "x_t": v["x"].T,
        "adj": v["adj"].T.reshape(TILES, P, CHUNKS, W).transpose(2, 1, 0, 3),
        "w_proj": v["L0_gnn_W_proj"], "b_proj": v["L0_gnn_b_proj"][:, None],
        "w_gcn": v["L0_gnn_W_gcn"], "b_gcn": v["L0_gnn_b_gcn"][:, None],
        "w_router0": v["L0_ffn_Wr"],
        "up0": up0.transpose(1, 0, 2)[:, None], "down0": down0.reshape(9, 4, P, P).transpose(2, 0, 1, 3),
        "bias_up0": b_up0.reshape(9, 4, P).transpose(2, 0, 1), "bias_down0": b_down0.T,
        "w_attn": v["L1_gnn_W"].T, "b_attn": v["L1_gnn_b"][:, None],
        "a_parent": v["L1_gnn_a"][:, :HD].reshape(P, 1), "a_child": v["L1_gnn_a"][:, HD:].reshape(P, 1),
        "head_cols": (heads[:, None] == np.arange(HEADS)[None]).astype(np.float32),
        "head_blocks": (heads[:, None] == heads[None]).astype(np.float32),
        "bands": bands, "scales": scales, "identity": np.eye(P, dtype=np.float32),
        "row_of": np.repeat(np.eye(CHUNKS, dtype=np.float32)[:, :, None], P, 2),
        "w_router1": v["L1_ffn_router_w"].T,
        "up1": np.stack([v["L1_ffn_w1"], v["L1_ffn_w3"]]).transpose(3, 0, 1, 2),
        "down1": down1.reshape(8, 3, P, P).transpose(2, 0, 1, 3),
    }
    nc = bacc.Bacc("TRN2", target_bir_lowering=False, num_devices=1)
    data, a = {}, {}
    for name, t in arrays.items():
        data[name] = np.ascontiguousarray(t)
        a[name] = nc.dram_tensor(name, data[name].shape, mybir.dt.from_np(data[name].dtype),
                                 kind="ExternalInput").ap()
    out = nc.dram_tensor("out_t", [P, N], F32, kind="ExternalOutput").ap()
    network(nc, a, out)
    r = run(nc, [data], core_ids=[0])
    return np.ascontiguousarray(r.results[0]["out_t"].T)
```

```python
import concourse.bass as bass
from concourse import mybir
from contextlib import ExitStack

F32 = mybir.dt.float32
BF16 = mybir.dt.bfloat16
F32R = mybir.dt.float32r
ALU = mybir.AluOpType
ACT = mybir.ActivationFunctionType
AX = mybir.AxisListType

P = 128
N = 4096
W = 512
CHUNKS = N // W
TILES = N // P
HEADS = 8
HD = 16
EPS = 1e-5
COLS = HD + 1
PART = 3 * COLS
PASSES = ((0, 0), (0, 1), (1, 0))
SELW = 240


class Scope:

    def __init__(self, nc, stage):
        self.nc, self.stage, self.stack, self.sems = nc, stage, ExitStack(), []

    def __enter__(self):
        self.stack.__enter__()
        return self

    def __exit__(self, *a):
        return self.stack.__exit__(*a)

    def sbuf(self, name, shape, dt=F32):
        return self.stack.enter_context(self.nc.sbuf_tensor(f"{self.stage}_{name}", shape, dt))

    def psum(self, name, shape, dt=F32):
        return self.stack.enter_context(self.nc.psum_tensor(f"{self.stage}_{name}", shape, dt))

    def sem(self, name):
        self.sems.append(self.stack.enter_context(self.nc.semaphore(f"{self.stage}_{name}")))
        return self.sems[-1]

    def clear_sems(self):
        with self.nc.Block() as block:

            @block.gpsimd
            def _(pool):
                for one in self.sems:
                    pool.sem_clear(one)


def layer_norm(nc, stage, x, xn, row_of, x_from=None, x_to=None, xn_to=None, ahead=()):
    with Scope(nc, stage) as s:
        centred = xn
        square = s.sbuf("square", [P, N])
        mean_of = s.sbuf("mean_of", [P, P])
        into_row = s.sbuf("into_row", [P, CHUNKS, CHUNKS])
        from_row = s.sbuf("from_row", [CHUNKS, CHUNKS, P])
        rstd = s.sbuf("rstd", [CHUNKS, W])
        wide_ps = s.psum("wide_ps", [P, 4, W])
        var_ps = s.psum("var_ps", [CHUNKS, W])
        x_in = [s.sem(f"x_in{h}") for h in range(2)]
        rows_in, const_ready, mean_ready, centred_ready, square_ready, var_ready = map(
            s.sem, ("rows_in", "const_ready", "mean_ready", "centred_ready", "square_ready", "var_ready"))
        rstd_steps, rstd_ready, wide_ready, xn_ready, xn_out = map(
            s.sem, ("rstd_steps", "rstd_ready", "wide_ready", "xn_ready", "xn_out"))
        zeroed, x_out = s.sem("zeroed"), s.sem("x_out")
        HALF = N // 2

        with nc.Block() as block:

            @block.sync
            def _(sp):
                if x_from is not None:
                    for h in range(2):
                        sp.dma_start(x[:, h * HALF:(h + 1) * HALF],
                                     x_from[:, h * HALF:(h + 1) * HALF]).then_inc(x_in[h], 16)
                sp.dma_start(from_row[:, :, :], row_of).then_inc(rows_in, 16)
                if x_to is not None:
                    sp.dma_start(x_to, x[:, :]).then_inc(x_out, 16)
                for dst, src, sem in ahead:
                    sp.dma_start(dst, src).then_inc(sem, 16)
                if xn_to is not None:
                    for h in range(2):
                        sp.wait_ge(xn_ready, (h + 1) * CHUNKS // 2)
                        sp.dma_start(xn_to[:, h * HALF:(h + 1) * HALF],
                                     xn[:, h * HALF:(h + 1) * HALF]).then_inc(xn_out, 16)
                    sp.wait_ge(xn_out, 32)
                if x_to is not None:
                    sp.wait_ge(x_out, 16)

            @block.tensor
            def _(pe):
                pe.wait_ge(const_ready, 1 + CHUNKS)
                for c in range(CHUNKS + 2):
                    if c < CHUNKS:
                        if c % 4 == 0 and x_from is not None:
                            pe.wait_ge(x_in[c // 4], 16)
                        if c >= 4:
                            pe.wait_ge(centred_ready, c - 3)
                        nc.tensor.matmul(wide_ps[:, c % 4, :], mean_of[:, :], x[:, c * W:(c + 1) * W],
                                         start=True, stop=True).then_inc(mean_ready, 1)
                    if c >= 2:
                        b = c - 2
                        pe.wait_ge(square_ready, b + 1)
                        nc.tensor.matmul(var_ps[:, :], into_row[:, b, :], square[:, b * W:(b + 1) * W],
                                         start=b == 0, stop=b == CHUNKS - 1).then_inc(var_ready, 1)
                pe.wait_ge(rows_in, 16)
                pe.wait_ge(rstd_ready, 1)
                for c in range(CHUNKS):
                    if c >= 4:
                        pe.wait_ge(xn_ready, c - 3)
                    nc.tensor.matmul(wide_ps[:, c % 4, :], from_row[:, c, :], rstd[:, :],
                                     start=True, stop=True).then_inc(wide_ready, 1)

            @block.scalar
            def _(act):
                for c in range(CHUNKS):
                    cs = slice(c * W, (c + 1) * W)
                    act.wait_ge(centred_ready, c + 1)
                    nc.scalar.activation(square[:, cs], centred[:, cs], ACT.Square).then_inc(square_ready, 1)
                act.wait_ge(rstd_steps, 2)
                nc.scalar.activation(rstd[:, :], rstd[:, :], ACT.Sqrt).then_inc(rstd_ready, 1)

            @block.vector
            def _(dve):
                nc.vector.memset(mean_of[:, :], 1.0 / P).then_inc(const_ready, 1)
                nc.vector.memset(into_row[:, :, :], 0.0).then_inc(zeroed, 1)
                dve.wait_ge(zeroed, 1)
                for c in range(CHUNKS):
                    nc.vector.memset(into_row[:, c, c:c + 1], 1.0 / P).then_inc(const_ready, 1)
                for c in range(CHUNKS):
                    cs = slice(c * W, (c + 1) * W)
                    dve.wait_ge(mean_ready, c + 1)
                    nc.vector.tensor_tensor(centred[:, cs], x[:, cs], wide_ps[:, c % 4, :],
                                            ALU.subtract).then_inc(centred_ready, 1)
                dve.wait_ge(var_ready, CHUNKS)
                nc.vector.tensor_scalar(rstd[:, :], var_ps[:, :], EPS, None, ALU.add).then_inc(rstd_steps, 1)
                dve.wait_ge(rstd_steps, 1)
                nc.vector.reciprocal(rstd[:, :], rstd[:, :]).then_inc(rstd_steps, 1)
                for c in range(CHUNKS):
                    cs = slice(c * W, (c + 1) * W)
                    dve.wait_ge(wide_ready, c + 1)
                    nc.vector.tensor_tensor(xn[:, cs], centred[:, cs], wide_ps[:, c % 4, :],
                                            ALU.mult).then_inc(xn_ready, 1)
        s.clear_sems()


def filtered_graph(nc, x, xn, x_dram, adj_dram, w_proj, b_proj, w_gcn, b_gcn, absent_dram,
                   adj_rows, identity_dram):
    UNIT = 4
    UNITS = TILES // UNIT
    RING = 4
    with Scope(nc, "graph") as s:
        hidden = s.sbuf("hidden", [P, N])
        g = s.sbuf("g", [P, TILES, P])
        wp, wg = s.sbuf("wp", [P, P]), s.sbuf("wg", [P, P])
        bp, bg = s.sbuf("bp", [P, 1]), s.sbuf("bg", [P, 1])
        ones = s.sbuf("ones", [P, P], BF16)
        adj = s.sbuf("adj", [P, RING, UNIT, W])
        sim = s.sbuf("sim", [P, 2, UNIT, W])
        absent = s.sbuf("absent", [P, 2, UNIT, W], BF16)
        feat = s.sbuf("feat", [P, 2, W])
        counts = s.sbuf("counts", [1, N])
        head_ps = s.psum("head_ps", [P, 4, W])
        feat_ps = s.psum("feat_ps", [P, 2, W])
        count_ps = s.psum("count_ps", [P, 2, W])
        loaded, const_ready, hid_mm, hid_ready, g_mm, g_ready = map(
            s.sem, ("loaded", "const_ready", "hid_mm", "hid_ready", "g_mm", "g_ready"))
        adj_in = [s.sem(f"adj_in{r}") for r in range(RING)]
        square_ready = s.sem("square_ready")
        mask_ready = s.sem("mask_ready")
        sim_ready = s.sem("sim_ready")
        sim_used = s.sem("sim_used")
        mask_used = s.sem("mask_used")
        feat_ready = s.sem("feat_ready")
        counts_ready = s.sem("counts_ready")
        x_ready = s.sem("x_ready")
        stored = s.sem("stored")

        def each_chunk(eng, run):
            run(0, 0, False)
            with eng.Fori(0, CHUNKS // 2 - 1) as c2:
                run(c2 * 2 + 1, 1, True)
                run(c2 * 2 + 2, 0, True)
            run(CHUNKS - 1, 1, True)

        with nc.Block() as block:

            @block.sync
            def _(sp):
                for dst, src in ((wp[:, :], w_proj), (wg[:, :], w_gcn), (bp[:, :], b_proj), (bg[:, :], b_gcn)):
                    sp.dma_start(dst, src).then_inc(loaded, 16)
                with sp.Fori(0, CHUNKS) as c:
                    for k in range(UNITS):
                        sp.wait_ge(square_ready, c * UNITS + (k + 1))
                        sp.wait_ge(mask_ready, c * UNITS + (k + 1))
                        sp.dma_start(adj[:, k % RING, :, :],
                                     adj_dram[c, :, k * UNIT:(k + 1) * UNIT, :]).then_inc(adj_in[k % RING], 16)
                sp.wait_ge(counts_ready, CHUNKS + 2)
                sp.dma_start(absent_dram, counts[:, :]).then_inc(stored, 16)
                sp.wait_ge(stored, 16)

            @block.tensor
            def _(pe):
                pe.wait_ge(loaded, 4 * 16)
                for c in range(CHUNKS):
                    if c >= 4:
                        pe.wait_ge(hid_ready, c - 3)
                    nc.tensor.matmul(head_ps[:, c % 4, :], wp[:, :], xn[:, c * W:(c + 1) * W],
                                     start=True, stop=True).then_inc(hid_mm, 1)
                pe.wait_ge(hid_ready, CHUNKS)
                for c in range(CHUNKS):
                    if c >= 4:
                        pe.wait_ge(g_ready, c - 3)
                    for t in range(4):
                        j = c * 4 + t
                        last = nc.tensor.matmul(head_ps[:, c % 4, t * P:(t + 1) * P],
                                                hidden[:, j * P:(j + 1) * P], wg[:, :],
                                                start=True, stop=True)
                    last.then_inc(g_mm, 1)
                pe.wait_ge(g_ready, CHUNKS)
                pe.wait_ge(const_ready, 1)

                def run(c, cc, tail):
                    pe.wait_ge(feat_ready, c + 1)
                    pe.wait_ge(counts_ready, c + 1)
                    for k in range(UNITS):
                        pe.wait_ge(sim_ready, c * UNITS + (k + 1))
                        for u in range(UNIT):
                            j = k * UNIT + u
                            last = nc.tensor.matmul(feat_ps[:, cc, :], g[:, j, :], sim[:, k % 2, u, :],
                                                    start=j == 0, stop=j == TILES - 1)
                        last.then_inc(sim_used, 1)
                        pe.wait_ge(mask_ready, c * UNITS + (k + 1 + RING))
                        for u in range(UNIT):
                            j = k * UNIT + u
                            last = nc.tensor.matmul(count_ps[:, cc, :], ones[:, :], absent[:, k % 2, u, :],
                                                    start=j == 0, stop=j == TILES - 1)
                        last.then_inc(mask_used, 1)

                each_chunk(pe, run)

            @block.scalar
            def _(act):
                act.sem_inc(feat_ready, 2)
                act.wait_ge(loaded, 4 * 16)
                for c in range(CHUNKS):
                    act.wait_ge(hid_mm, c + 1)
                    nc.scalar.activation(hidden[:, c * W:(c + 1) * W], head_ps[:, c % 4, :], ACT.Tanh,
                                         bias=bp[:, 0:1]).then_inc(hid_ready, 1)

                def take_feat(c, cc):
                    act.wait_ge(sim_used, c * UNITS + (UNITS + 2))
                    act.wait_ge(x_ready, c + 1)
                    nc.scalar.activation(feat[:, cc, :], feat_ps[:, cc, :], ACT.Relu,
                                         bias=bg[:, 0:1]).then_inc(feat_ready, 1)

                def run(c, cc, tail):
                    for k in range(UNITS):
                        act.wait_ge(square_ready, c * UNITS + (k + 1 + RING))
                        nc.scalar.activation(sim[:, k % 2, :, :], sim[:, k % 2, :, :],
                                             ACT.Tanh).then_inc(sim_ready, 1)
                        if k == 1 and tail:
                            take_feat(c - 1, 1 - cc)

                each_chunk(act, run)
                take_feat(CHUNKS - 1, (CHUNKS - 1) % 2)

            @block.vector
            def _(dve):
                nc.vector.memset(ones[:, :], 1.0).then_inc(const_ready, 1)
                dve.sem_inc(square_ready, RING)
                dve.sem_inc(mask_ready, RING)
                dve.sem_inc(sim_used, 2)
                dve.sem_inc(mask_used, 2)
                dve.sem_inc(counts_ready, 2)
                dve.sem_inc(x_ready, 2)
                for c in range(CHUNKS):
                    dve.wait_ge(g_mm, c + 1)
                    nc.vector.tensor_copy(g[:, 4 * c:4 * c + 4, :],
                                          head_ps[:, c % 4, :].rearrange("p (t d) -> p t d", t=4)).then_inc(g_ready, 1)
                dve.wait_ge(loaded, 4 * 16)

                def take_chunk(c, cc):
                    cs = bass.ds(c * W, W)
                    dve.wait_ge(mask_used, c * UNITS + (UNITS + 2))
                    nc.vector.tensor_scalar(counts[0:1, cs], count_ps[0:1, cc, :], 1.0, None,
                                            ALU.mult).then_inc(counts_ready, 1)
                    dve.wait_ge(feat_ready, c + 3)
                    nc.vector.tensor_tensor(x[:, cs], feat[:, cc, :], x[:, cs],
                                            ALU.add).then_inc(x_ready, 1)

                def run(c, cc, tail):
                    for k in range(UNITS):
                        dve.wait_ge(adj_in[k % RING], c * (UNITS // RING * 16) + (k // RING + 1) * 16)
                        dve.wait_ge(sim_used, c * UNITS + (k + 1))
                        nc.vector.scalar_tensor_tensor(
                            out=sim[:, k % 2, :, :], in0=adj[:, k % RING, :, :], scalar=0.0,
                            in1=adj[:, k % RING, :, :], op0=ALU.max, op1=ALU.mult).then_inc(square_ready, 1)
                        dve.wait_ge(mask_used, c * UNITS + (k + 1))
                        nc.vector.tensor_scalar(absent[:, k % 2, :, :], adj[:, k % RING, :, :], 0.0, None,
                                                ALU.is_equal).then_inc(mask_ready, 1)
                        if k == 2 and tail:
                            take_chunk(c - 1, 1 - cc)

                each_chunk(dve, run)
                take_chunk(CHUNKS - 1, (CHUNKS - 1) % 2)

        keep_strongest(nc, s, x_dram, adj_rows, identity_dram, counts, hidden, xn, adj, x, feat, g, bg,
                       head_ps, feat_ps)
        s.clear_sems()


def keep_strongest(nc, s, x_dram, adj_rows, identity_dram, counts, filt, turned, adj, x, feat, g, bg,
                   turn_ps, feat_ps):
    KEEP = 350
    ROUNDS = -(-KEEP // 8)
    SENTINELS = ROUNDS * 8 - KEEP
    WIDE = N + SENTINELS
    left = adj[:, :, :, :].rearrange("p r u w -> p (r u w)")[:, 0:WIDE]
    ident = s.sbuf("keep_ident", [P, P])
    fewest, top8 = s.sbuf("keep_fewest", [1, 1]), s.sbuf("keep_top8", [P, 8])
    flag = s.sbuf("keep_flag", [1, 1], mybir.dt.int32)
    (fewest_ready, flag_ready, ident_in, x_in, row_in, squares, filt_ready, left_ready, picks, kept, turns, turned_ready,
     feat_mm, feat_relu, tile_done, turn) = (s.sem(f"keep_{n}") for n in (
         "fewest_ready", "flag_ready", "ident_in", "x_in", "row_in", "squares", "filt_ready", "left_ready", "picks",
         "kept", "turns", "turned_ready", "feat_mm", "feat_relu", "tile_done", "turn"))
    BANKS = TILES // 4

    with nc.Block() as block:

        def needed(eng):
            eng.wait_ge(flag_ready, 1)
            return eng.value_load(flag[0:1, 0:1]) > 0

        @block.sync
        def _(sp):
            with sp.If(needed(sp)):
                sp.dma_start(ident[:, :], identity_dram).then_inc(ident_in, 16)
                sp.dma_start(x[:, :], x_dram).then_inc(x_in, 16)
                with sp.Fori(0, TILES) as t:
                    sp.wait_ge(tile_done, t + 1)
                    sp.dma_start(filt[:, :], adj_rows[bass.ds(t * P, P), :]).then_inc(row_in, 16)

        @block.vector
        def _(dve):
            nc.vector.tensor_reduce(fewest[:, :], counts[:, :], AX.X, ALU.min).then_inc(fewest_ready, 1)
            dve.wait_ge(fewest_ready, 1)
            nc.vector.tensor_scalar(flag[:, :], fewest[:, :], float(N - KEEP), None,
                                    ALU.is_lt).then_inc(flag_ready, 1)
            with dve.If(needed(dve)):
                dve.sem_inc(tile_done, 1)
                dve.wait_ge(x_in, 16)
                with dve.Fori(0, TILES) as t:
                    dve.wait_ge(row_in, t * 16 + 16)
                    nc.vector.scalar_tensor_tensor(out=left[:, 0:N], in0=filt[:, :], scalar=0.0, in1=filt[:, :],
                                                   op0=ALU.max, op1=ALU.mult)
                    nc.vector.memset(left[:, N:WIDE], 2.0).then_inc(squares, 1)
                    dve.wait_ge(left_ready, t + 1)
                    dve.sem_inc(turn, 1)
                    with dve.Fori(0, ROUNDS) as r:
                        nc.vector.max(top8[:, :], left).then_inc(picks, 1)
                        dve.wait_ge(picks, t * (2 * ROUNDS) + r * 2 + 1)
                        dve.sem_inc(turn, 1)
                        nc.vector.match_replace(left, top8[:, :], left, -1.0).then_inc(picks, 1)
                        dve.wait_ge(picks, t * (2 * ROUNDS) + r * 2 + 2)
                    nc.vector.scalar_tensor_tensor(out=filt[:, :], in0=left[:, 0:N], scalar=0.0, in1=filt[:, :],
                                                   op0=ALU.is_lt, op1=ALU.mult).then_inc(kept, 1)
                    for b in range(BANKS):
                        dve.wait_ge(turns, t * BANKS + (b + 1))
                        nc.vector.tensor_copy(turned[:, b * W:(b + 1) * W],
                                              turn_ps[:, b % 4, :]).then_inc(turned_ready, 1)
                    dve.wait_ge(feat_relu, t + 1)
                    nc.vector.tensor_tensor(x[:, bass.ds(t * P, P)], feat[:, 0, 0:P], x[:, bass.ds(t * P, P)],
                                            ALU.add).then_inc(tile_done, 1)

        @block.scalar
        def _(act):
            with act.If(needed(act)):
                with act.Fori(0, TILES) as t:
                    act.wait_ge(squares, t + 1)
                    nc.scalar.activation(filt[:, :], left[:, 0:N], ACT.Tanh).then_inc(filt_ready, 1)
                    act.wait_ge(filt_ready, t + 1)
                    nc.scalar.copy(left[:, 0:N], filt[:, :]).then_inc(left_ready, 1)
                    act.wait_ge(feat_mm, t + 1)
                    nc.scalar.activation(feat[:, 0, 0:P], feat_ps[:, 0, 0:P], ACT.Relu,
                                         bias=bg[:, 0:1]).then_inc(feat_relu, 1)

        @block.tensor
        def _(pe):
            with pe.If(needed(pe)):
                pe.wait_ge(ident_in, 16)
                with pe.Fori(0, TILES) as t:
                    pe.wait_ge(kept, t + 1)
                    for b in range(BANKS):
                        if b >= 4:
                            pe.wait_ge(turned_ready, t * BANKS + (b - 3))
                        for k in range(4):
                            j = b * 4 + k
                            last = nc.tensor.transpose(turn_ps[:, b % 4, k * P:(k + 1) * P],
                                                       filt[:, j * P:(j + 1) * P], ident[:, :])
                        last.then_inc(turns, 1)
                    pe.wait_ge(turned_ready, t * BANKS + BANKS)
                    for j in range(TILES):
                        last = nc.tensor.matmul(feat_ps[:, 0, 0:P], g[:, j, :], turned[:, j * P:(j + 1) * P],
                                                start=j == 0, stop=j == TILES - 1)
                    last.then_inc(feat_mm, 1)


def route(nc, stage, xn, w_router, identity_dram, gates_dram, guard, weights):
    E = 8
    with Scope(nc, stage) as s:
        wr = s.sbuf("wr", [P, E])
        ident = s.sbuf("ident", [P, P])
        rank = s.sbuf("rank", [P, TILES, E])
        rank_i = s.sbuf("rank_i", [P, TILES, E], mybir.dt.int32)
        prob, left, hit, pick1, pick2 = (s.sbuf(n, [P, TILES, E]) for n in ("prob", "left", "hit", "pick1", "pick2"))
        top, total, best1, best2 = (s.sbuf(n, [P, TILES]) for n in ("top", "total", "best1", "best2"))
        gates_t = s.sbuf("gates_t", [E, N])
        logit_ps = s.psum("logit_ps", [P, TILES, E])
        gate_ps = s.psum("gate_ps", [E, 4, W])
        loaded, ranked, logits, shifted, powers, step, gates_mm, gates_ready, stored = map(
            s.sem, ("loaded", "ranked", "logits", "shifted", "powers", "step", "gates_mm", "gates_ready", "stored"))
        high_ready = s.sem("high_ready")

        with nc.Block() as block:

            @block.sync
            def _(sp):
                for dst, src in ((wr[:, :], w_router), (ident[:, :], identity_dram)):
                    sp.dma_start(dst, src).then_inc(loaded, 16)
                sp.wait_ge(gates_ready, CHUNKS)
                sp.dma_start(gates_dram, gates_t[:, :]).then_inc(stored, 16)
                sp.wait_ge(stored, 16)

            @block.tensor
            def _(pe):
                pe.wait_ge(loaded, 32)
                for t in range(TILES):
                    last = nc.tensor.matmul(logit_ps[:, t, :], xn[:, t * P:(t + 1) * P], wr[:, :],
                                            start=True, stop=True)
                last.then_inc(logits, 1)
                pe.wait_ge(step, (24 if guard else 23))
                for c in range(CHUNKS):
                    if c >= 4:
                        pe.wait_ge(gates_ready, c - 3)
                    for t in range(4):
                        last = nc.tensor.transpose(gate_ps[:, c % 4, t * P:(t + 1) * P],
                                                   prob[:, c * 4 + t, :], ident[:, :])
                    last.then_inc(gates_mm, 1)

            @block.scalar
            def _(act):
                act.wait_ge(weights.loaded, 16 * len(weights.loads))
                for whole, high, _low in weights.splits:
                    nc.scalar.copy(high, whole).then_inc(high_ready, 1)
                act.wait_ge(shifted, 1)
                nc.scalar.activation(prob[:, :, :], prob[:, :, :], ACT.Exp).then_inc(powers, 1)

            @block.gpsimd
            def _(pool):
                nc.gpsimd.iota(rank_i[:, :, :], [[0, TILES], [-1, E]], base=E, channel_multiplier=0).then_inc(ranked, 1)
                pool.wait_ge(weights.loaded, 16 * len(weights.loads))
                for n, (whole, high, low) in enumerate(weights.splits):
                    pool.wait_ge(high_ready, n + 1)
                    nc.gpsimd.tensor_tensor(low, whole, high, ALU.subtract)

            @block.vector
            def _(dve):
                steps = 0

                def done(ins):
                    nonlocal steps
                    steps += 1
                    ins.then_inc(step, 1)
                    dve.wait_ge(step, steps)

                def wide(a):
                    return a[:, :].rearrange("p (t o) -> p t o", o=1).broadcast_to([P, TILES, E])

                dve.wait_ge(logits, 1)
                done(nc.vector.tensor_reduce(top[:, :], logit_ps[:, :, :], AX.X, ALU.max))
                nc.vector.tensor_tensor(prob[:, :, :], logit_ps[:, :, :], wide(top), ALU.subtract).then_inc(shifted, 1)
                dve.wait_ge(ranked, 1)
                done(nc.vector.tensor_copy(rank[:, :, :], rank_i[:, :, :]))
                dve.wait_ge(powers, 1)
                done(nc.vector.tensor_reduce(total[:, :], prob[:, :, :], AX.X, ALU.add))
                done(nc.vector.reciprocal(total[:, :], total[:, :]))
                done(nc.vector.tensor_tensor(prob[:, :, :], prob[:, :, :], wide(total), ALU.mult))
                done(nc.vector.tensor_copy(left[:, :, :], prob[:, :, :]))
                for best, pick in ((best1, pick1), (best2, pick2)):
                    done(nc.vector.tensor_reduce(best[:, :], left[:, :, :], AX.X, ALU.max))
                    done(nc.vector.tensor_tensor(hit[:, :, :], left[:, :, :], wide(best), ALU.is_equal))
                    done(nc.vector.tensor_tensor(hit[:, :, :], hit[:, :, :], rank[:, :, :], ALU.mult))
                    done(nc.vector.tensor_reduce(top[:, :], hit[:, :, :], AX.X, ALU.max))
                    done(nc.vector.tensor_tensor(pick[:, :, :], hit[:, :, :], wide(top), ALU.is_equal))
                    done(nc.vector.scalar_tensor_tensor(
                        out=left[:, :, :], in0=pick[:, :, :], scalar=-2.0, in1=left[:, :, :],
                        op0=ALU.mult, op1=ALU.add))
                done(nc.vector.tensor_tensor(total[:, :], best1[:, :], best2[:, :], ALU.add))
                if guard:
                    done(nc.vector.tensor_scalar(total[:, :], total[:, :], guard, None, ALU.add))
                done(nc.vector.reciprocal(total[:, :], total[:, :]))
                done(nc.vector.tensor_tensor(pick1[:, :, :], pick1[:, :, :], pick2[:, :, :], ALU.add))
                done(nc.vector.tensor_tensor(prob[:, :, :], prob[:, :, :], pick1[:, :, :], ALU.mult))
                done(nc.vector.tensor_tensor(prob[:, :, :], prob[:, :, :], wide(total), ALU.mult))
                for c in range(CHUNKS):
                    dve.wait_ge(gates_mm, c + 1)
                    nc.vector.tensor_copy(gates_t[:, c * W:(c + 1) * W], gate_ps[:, c % 4, :]).then_inc(gates_ready, 1)


class ExpertWeights:

    def __init__(self, s, shared, widths):
        count, blocks = 9 if shared else 8, len(widths)
        self.up = [s.sbuf(f"up_{part}", [P, 1 if shared else 2, count, sum(widths)], F32R) for part in ("high", "low")]
        self.down = [s.sbuf(f"down_{part}", [P, count, blocks, P], F32R) for part in ("high", "low")]
        if shared:
            self.bup, self.bdown = s.sbuf("bup", [P, count, blocks]), s.sbuf("bdown", [P, count])

    def stage(self, s, w_up, w_down, bias_up=None, bias_down=None):
        up, down = s.sbuf("up", self.up[0].shape), s.sbuf("down", self.down[0].shape)
        self.loaded = s.sem("weights_in")
        self.loads = [(up[:, :, :, :], w_up, self.loaded), (down[:, :, :, :], w_down, self.loaded)]
        if bias_up is not None:
            self.loads += [(self.bup[:, :, :], bias_up, self.loaded), (self.bdown[:, :], bias_down, self.loaded)]
        self.splits = [(whole[:, :, :, :], parts[0][:, :, :, :], parts[1][:, :, :, :])
                       for whole, parts in ((up, self.up), (down, self.down))]


def experts(nc, stage, x, xn, gates_dram, weights, shared, widths, x_out=None):
    BLOCKS = len(widths)
    EXPERTS = 9 if shared else 8
    UPS = 1 if shared else 2
    starts = [sum(widths[:b]) for b in range(BLOCKS)]
    PER = 2 * EXPERTS
    with Scope(nc, stage) as s:
        up, down = weights.up, weights.down
        if shared:
            bup, bdown = weights.bup, weights.bdown
        gates = s.sbuf("gates", [P, 2, 8, W])
        hid = s.sbuf("hid", [P, 2, BLOCKS, W])
        hid_part = [s.sbuf(f"hid_{n}", [P, 2, BLOCKS, W], F32R) for n in ("high", "low")]
        xn_part = [s.sbuf(f"xn_{n}", [P, 2, W], F32R) for n in ("high", "low")]
        part = s.sbuf("part", [P, 2, W])
        up_ps = [s.psum(f"up_ps{i}", [P, BLOCKS, W]) for i in range(UPS)]
        y_ps = s.psum("y_ps", [P, 2, W])
        gates_in = [s.sem(f"gates_in{i}") for i in range(2)]
        xn_high, xn_low = s.sem("xn_high"), s.sem("xn_low")
        pool_turn = s.sem("pool_turn")
        up_mm = s.sem("up_mm")
        high_ready, low_ready = s.sem("high_ready"), s.sem("low_ready")
        act_ready = s.sem("act_ready")
        hid_ready = s.sem("hid_ready")
        y_mm = s.sem("y_mm")
        y_taken = s.sem("y_taken")
        summed = s.sem("summed")
        stored = s.sem("stored")

        with nc.Block() as block:

            @block.sync
            def _(sp):
                with sp.Fori(0, CHUNKS // 2) as c2:
                    for cc in range(2):
                        c = c2 * 2 + cc
                        sp.wait_ge(summed, c * EXPERTS + 1)
                        sp.dma_start(gates[:, cc, :, :], gates_dram[:, bass.ds(c * W, W)].rearrange(
                            "(o e) n -> o e n", o=1).broadcast_to([P, 8, W])).then_inc(gates_in[cc], 16)
                if x_out is not None:
                    for h in range(2):
                        cs = slice(0, N - W) if h == 0 else slice(N - W, N)
                        sp.wait_ge(summed, (CHUNKS - 1 + h) * EXPERTS + EXPERTS + 1)
                        sp.dma_start(x_out[:, cs], x[:, cs]).then_inc(stored, 16)
                    sp.wait_ge(stored, 32)

            @block.tensor
            def _(pe):

                def expert_down(c2, q):
                    e = q % EXPERTS
                    pe.wait_ge(y_taken, c2 * PER + (q + 1))
                    for b in range(BLOCKS):
                        pe.wait_ge(low_ready, c2 * (PER * BLOCKS) + (q * BLOCKS + b + 1))
                        for i, (w, m) in enumerate(PASSES):
                            last = nc.tensor.matmul(y_ps[:, q % 2, :], down[w][0:widths[b], e, b, :],
                                                    hid_part[m][0:widths[b], q % 2, b, :],
                                                    start=b == 0 and i == 0, stop=b == BLOCKS - 1 and i == 2)
                    last.then_inc(y_mm, 1)

                with pe.Fori(0, CHUNKS // 2) as c2:
                    for q in range(PER):
                        cc, e = divmod(q, EXPERTS)
                        if e == 0:
                            pe.wait_ge(xn_low, c2 * 2 + (cc + 1))
                        for b in range(BLOCKS):
                            n = c2 * (PER * BLOCKS) + (q * BLOCKS + b + 1)
                            pe.wait_ge(act_ready, n)
                            if not shared:
                                pe.wait_ge(hid_ready, n)
                            for i in range(UPS):
                                for k, (w, m) in enumerate(PASSES):
                                    last = nc.tensor.matmul(up_ps[i][0:widths[b], b, :],
                                                            up[w][:, i, e, starts[b]:starts[b] + widths[b]],
                                                            xn_part[m][:, cc, :], start=k == 0, stop=k == 2)
                            last.then_inc(up_mm, 1)
                        if q:
                            expert_down(c2, q - 1)
                    expert_down(c2, PER - 1)

            @block.scalar
            def _(act):
                act.sem_inc(act_ready, BLOCKS)

                def take_high(c2, q, b):
                    n = c2 * (PER * BLOCKS) + (q * BLOCKS + b + 1)
                    act.wait_ge(act_ready if shared else hid_ready, n + BLOCKS)
                    nc.scalar.copy(hid_part[0][0:widths[b], q % 2, b, :],
                                   hid[0:widths[b], q % 2, b, :]).then_inc(high_ready, 1)

                with act.Fori(0, CHUNKS // 2) as c2:
                    for q in range(PER):
                        e = q % EXPERTS
                        act.wait_ge(y_mm, c2 * PER + (q + 1))
                        for b in range(BLOCKS):
                            act.wait_ge(up_mm, (c2 + 1) * (PER * BLOCKS) + (q * BLOCKS + b + 1))
                            to, src = hid[0:widths[b], q % 2, b, :], up_ps[0][0:widths[b], b, :]
                            if shared:
                                nc.scalar.activation(to, src, ACT.Gelu,
                                                     bias=bup[0:widths[b], e, b:b + 1]).then_inc(act_ready, 1)
                            else:
                                nc.scalar.activation(to, src, ACT.Silu).then_inc(act_ready, 1)
                            if b:
                                take_high(c2, q, b - 1)
                        take_high(c2, q, BLOCKS - 1)

            @block.gpsimd
            def _(pool):
                with pool.Fori(0, CHUNKS // 2) as c2:
                    for cc in range(2):
                        cs = bass.ds((c2 * 2 + cc) * W, W)
                        pool.wait_ge(up_mm, c2 * (PER * BLOCKS) + (cc + 1) * (EXPERTS * BLOCKS))
                        pool.sem_inc(pool_turn, 1)
                        nc.gpsimd.tensor_copy(xn_part[0][:, cc, :], xn[:, cs]).then_inc(xn_high, 1)
                        pool.wait_ge(xn_high, c2 * 2 + (cc + 1))
                        pool.sem_inc(pool_turn, 1)
                        nc.gpsimd.tensor_tensor(xn_part[1][:, cc, :], xn[:, cs], xn_part[0][:, cc, :],
                                                ALU.subtract).then_inc(xn_low, 1)

            @block.vector
            def _(dve):
                dve.sem_inc(hid_ready, BLOCKS)
                dve.sem_inc(y_mm, 2)
                dve.sem_inc(y_taken, 2)
                dve.sem_inc(summed, EXPERTS + 1)
                dve.sem_inc(up_mm, PER * BLOCKS)

                def take_low(c2, q, b):
                    dve.wait_ge(high_ready, c2 * (PER * BLOCKS) + (q * BLOCKS + b + 1))
                    at = (slice(0, widths[b]), q % 2, b, slice(0, W))
                    nc.vector.tensor_tensor(hid_part[1][at], hid[at], hid_part[0][at],
                                            ALU.subtract).then_inc(low_ready, 1)


                def gather_expert(c2, q):
                    cc, e = divmod(q, EXPERTS)
                    n = c2 * PER + q
                    xs = x[:, bass.ds((c2 * 2 + cc) * W, W)]
                    if e == 0:
                        dve.wait_ge(gates_in[cc], c2 * 16 + 16)
                    dve.wait_ge(y_mm, n + 3)
                    if shared and e == 0:
                        nc.vector.tensor_scalar(part[:, q % 2, :], y_ps[:, q % 2, :], bdown[:, 0:1], None,
                                                ALU.add).then_inc(y_taken, 1)
                    elif shared:
                        nc.vector.scalar_tensor_tensor(
                            out=part[:, q % 2, :], in0=y_ps[:, q % 2, :], scalar=bdown[:, e:e + 1],
                            in1=gates[:, cc, e - 1, :], op0=ALU.add, op1=ALU.mult).then_inc(y_taken, 1)
                    else:
                        nc.vector.tensor_tensor(part[:, q % 2, :], y_ps[:, q % 2, :], gates[:, cc, e, :],
                                                ALU.mult).then_inc(y_taken, 1)
                    dve.wait_ge(y_taken, n + 3)
                    dve.wait_ge(summed, n + (EXPERTS + 1))
                    nc.vector.tensor_tensor(xs, xs, part[:, q % 2, :], ALU.add).then_inc(summed, 1)

                with dve.Fori(0, CHUNKS // 2) as c2:
                    for q in range(PER):
                        for b in range(BLOCKS):
                            if not shared:
                                n = c2 * (PER * BLOCKS) + (q * BLOCKS + b + 1)
                                dve.wait_ge(act_ready, n + BLOCKS)
                                h = hid[0:widths[b], q % 2, b, :]
                                nc.vector.tensor_tensor(h, h, up_ps[1][0:widths[b], b, :],
                                                        ALU.mult).then_inc(hid_ready, 1)
                            if b:
                                take_low(c2, q, b - 1)
                        take_low(c2, q, BLOCKS - 1)
                        if q:
                            gather_expert(c2, q - 1)
                    gather_expert(c2, PER - 1)


def attention(nc, x_dram, xn_dram, adj_dram, absent_dram, w_t, bias, a_parent, a_child,
              head_cols, head_blocks, bands, scales, identity_dram, x_out):
    UNIT = 2
    UNITS = TILES // UNIT
    GROUP = 4
    PAIR = 4 * PART
    RING = 4
    with Scope(nc, "attn") as s:
        vz = s.sbuf("vz", [P, TILES, HEADS // 2, PAIR], BF16)
        feats = s.sbuf("feats", [P, TILES, 3, P], BF16)
        gap = s.sbuf("gap", [P, TILES, HEADS])
        cmax = s.sbuf("cmax", [P, HEADS])
        cmax_col = s.sbuf("cmax_col", [P, 1])
        wt, parent_block = s.sbuf("wt", [P, P]), s.sbuf("parent_block", [P, P])
        parent_rep = s.sbuf("parent_rep", [P, HEADS, P])
        bcol, acol, pcol = s.sbuf("bcol", [P, 1]), s.sbuf("acol", [P, 1]), s.sbuf("pcol", [P, 1])
        heads8 = s.sbuf("heads8", [P, HEADS])
        blocks = s.sbuf("blocks", [P, P])

        with Scope(nc, "nodes") as t:
            xn = t.sbuf("xn", [P, N])
            nf_t = t.sbuf("nf_t", [P, N])
            nf = t.sbuf("nf", [P, TILES, P])
            ident = t.sbuf("ident", [P, P])
            child8 = t.sbuf("child8", [P, HEADS])
            child = t.sbuf("child", [P, TILES, HEADS])
            top8, picked = t.sbuf("top8", [P, HEADS]), t.sbuf("picked", [P, HEADS])
            w_v, w_z = t.sbuf("w_v", [P, TILES, HEADS]), t.sbuf("w_z", [P, TILES, HEADS])
            SLAB = 4
            KINDS = ((w_v, 0, 0), (w_z, 0, PART), (w_z, 1, 2 * PART), (w_v, 1, 3 * PART))
            full, rest = (t.sbuf(n, [P, len(KINDS), SLAB, HEADS // 2, COLS]) for n in ("full", "rest"))
            rest_f = t.sbuf("rest_f", [P, TILES, P])
            nf_ps = t.psum("nf_ps", [P, 2, W])
            tr_ps = t.psum("tr_ps", [P, 4, W])
            child_ps = t.psum("child_ps", [P, TILES, HEADS])
            loaded, child_const, nf_mm, nf_ready, tr_mm, tr_ready, child_mm, step, reduced, exps = map(
                t.sem, ("loaded", "child_const", "nf_mm", "nf_ready", "tr_mm", "tr_ready", "child_mm", "step",
                        "reduced", "exps"))
            xn_in = [t.sem(f"xn_in{q}") for q in range(4)]
            feat_cast, feat_rest = t.sem("feat_cast"), t.sem("feat_rest")
            cast = t.sem("cast")
            left = t.sem("left")
            with nc.Block() as block:

                @block.sync
                def _(sp):
                    for dst, src in ((wt, w_t), (bcol, bias), (acol, a_child), (pcol, a_parent),
                                     (heads8, head_cols), (blocks, head_blocks), (ident, identity_dram)):
                        sp.dma_start(dst[:, :], src).then_inc(loaded, 16)
                    for q in range(4):
                        qs = slice(q * 2 * W, (q + 1) * 2 * W)
                        sp.dma_start(xn[:, qs], xn_dram[:, qs]).then_inc(xn_in[q], 16)

                @block.tensor
                def _(pe):
                    pe.wait_ge(loaded, 7 * 16)
                    for c in range(CHUNKS):
                        if c % 2 == 0:
                            pe.wait_ge(xn_in[c // 2], 16)
                        if c >= 2:
                            pe.wait_ge(nf_ready, c - 1)
                        nc.tensor.matmul(nf_ps[:, c % 2, :], wt[:, :], xn[:, c * W:(c + 1) * W],
                                         start=True, stop=True).then_inc(nf_mm, 1)
                    pe.wait_ge(nf_ready, CHUNKS)
                    for c in range(CHUNKS):
                        if c >= 4:
                            pe.wait_ge(tr_ready, c - 3)
                        for k in range(4):
                            j = c * 4 + k
                            last = nc.tensor.transpose(tr_ps[:, c % 4, k * P:(k + 1) * P],
                                                       nf_t[:, j * P:(j + 1) * P], ident[:, :])
                        last.then_inc(tr_mm, 1)
                    pe.wait_ge(child_const, 1)
                    for j in range(TILES):
                        last = nc.tensor.matmul(child_ps[:, j, :], nf_t[:, j * P:(j + 1) * P], child8[:, :],
                                                start=True, stop=True)
                    last.then_inc(child_mm, 1)

                @block.scalar
                def _(act):
                    act.wait_ge(loaded, 7 * 16)
                    for c in range(CHUNKS):
                        act.wait_ge(nf_mm, c + 1)
                        nc.scalar.activation(nf_t[:, c * W:(c + 1) * W], nf_ps[:, c % 2, :], ACT.Identity,
                                             bias=bcol[:, 0:1]).then_inc(nf_ready, 1)
                    act.wait_ge(tr_ready, CHUNKS)
                    for part in range(3):
                        if part:
                            act.wait_ge(feat_rest, part)
                        nc.scalar.copy(feats[:, :, part, :], (rest_f if part else nf)[:, :, :]).then_inc(feat_cast, 1)
                        if part == 1:
                            act.wait_ge(step, 3)
                            nc.scalar.activation(w_v[:, :, :], gap[:, :, :], ACT.Exp, scale=-0.2).then_inc(exps, 1)
                            nc.scalar.activation(w_z[:, :, :], gap[:, :, :], ACT.Exp, scale=-1.0).then_inc(exps, 1)
                    act.wait_ge(exps, 2)
                    with act.Fori(0, TILES // SLAB) as slab:
                        rows = bass.ds(slab * SLAB, SLAB)
                        for k, (weight, odd, _at) in enumerate(KINDS):
                            act.wait_ge(left, slab * 12 + (4 + k + 1))
                            nc.scalar.copy(full[:, k, :, :, HD], weight[:, rows, odd::2]).then_inc(cast, 1)
                        for part in range(3):
                            for k, (_weight, _odd, at) in enumerate(KINDS):
                                act.wait_ge(left, (slab + 1) * 12 + (4 * part + k + 1))
                                if part == 0:
                                    act.wait_ge(cast, slab * 16 + (k + 1))
                                nc.scalar.copy(vz[:, rows, :, at + part * COLS:at + (part + 1) * COLS],
                                               (rest if part else full)[:, k, :, :, :]).then_inc(cast, 1)

                @block.gpsimd
                def _(pool):
                    pool.wait_ge(step, 2)
                    nc.gpsimd.partition_all_reduce(cmax[:, :], top8[:, :], P, bass.bass_isa.ReduceOp.max).then_inc(reduced, 1)

                @block.vector
                def _(dve):
                    steps = 0

                    def done(ins):
                        nonlocal steps
                        steps += 1
                        ins.then_inc(step, 1)
                        dve.wait_ge(step, steps)

                    dve.wait_ge(loaded, 7 * 16)
                    nc.vector.tensor_scalar(child8[:, :], heads8[:, :], acol[:, 0:1], None,
                                            ALU.mult).then_inc(child_const, 1)
                    for c in range(CHUNKS):
                        dve.wait_ge(tr_mm, c + 1)
                        nc.vector.tensor_copy(nf[:, 4 * c:4 * c + 4, :],
                                              tr_ps[:, c % 4, :].rearrange("p (k d) -> p k d", k=4)).then_inc(tr_ready, 1)

                    def rest_of_feats(part):
                        dve.wait_ge(feat_cast, part + 1)
                        if part:
                            dve.wait_ge(feat_rest, part)
                        nc.vector.tensor_tensor(rest_f[:, :, :], (rest_f if part else nf)[:, :, :],
                                                feats[:, :, part, :], ALU.subtract).then_inc(feat_rest, 1)

                    dve.sem_inc(left, 12)
                    dve.wait_ge(child_mm, 1)
                    done(nc.vector.tensor_copy(child[:, :, :], child_ps[:, :, :]))
                    done(nc.vector.tensor_reduce(top8[:, :], child[:, :, :].rearrange("p t h -> p h t"), AX.X, ALU.max))
                    dve.wait_ge(reduced, 1)
                    done(nc.vector.tensor_tensor(
                        gap[:, :, :], cmax[:, :].rearrange("p (o h) -> p o h", o=1).broadcast_to([P, TILES, HEADS]),
                        child[:, :, :], ALU.subtract))
                    rest_of_feats(0)
                    done(nc.vector.tensor_tensor(picked[:, :], cmax[:, :], heads8[:, :], ALU.mult))
                    done(nc.vector.tensor_reduce(cmax_col[:, :], picked[:, :], AX.X, ALU.add))
                    done(nc.vector.tensor_scalar(parent_block[:, :], blocks[:, :], pcol[:, 0:1], None, ALU.mult))
                    done(nc.vector.tensor_scalar(picked[:, :], heads8[:, :], pcol[:, 0:1], None, ALU.mult))
                    done(nc.vector.tensor_copy(parent_rep[:, :, :], picked[:, :].rearrange(
                        "p (h o) -> p h o", o=1).broadcast_to([P, HEADS, P])))
                    rest_of_feats(1)
                    dve.wait_ge(exps, 2)
                    with dve.Fori(0, TILES // SLAB) as slab:
                        rows = bass.ds(slab * SLAB, SLAB)
                        for k, (weight, odd, _at) in enumerate(KINDS):
                            wh = weight[:, rows, odd::2]
                            fh = nf[:, rows, :].rearrange("p t (a b d) -> p t a b d", b=2, d=HD)[:, :, :, odd, :]
                            dve.wait_ge(left, slab * 12 + (4 + k + 1))
                            nc.vector.tensor_tensor(
                                full[:, k, :, :, 0:HD], fh, wh.rearrange("p t (a o) -> p t a o", o=1).broadcast_to(
                                    [P, SLAB, HEADS // 2, HD]), ALU.mult).then_inc(left, 1)
                        for part in range(2):
                            for k, (_weight, _odd, at) in enumerate(KINDS):
                                dve.wait_ge(cast, slab * 16 + (4 * (part + 1) + k + 1))
                                nc.vector.tensor_tensor(
                                    rest[:, k, :, :, :], (rest if part else full)[:, k, :, :, :],
                                    vz[:, rows, :, at + part * COLS:at + (part + 1) * COLS],
                                    ALU.subtract).then_inc(left, 1)

        EVENTS = 14
        TAIL_NUM, TAIL_DEN, P_FEAT, U_LATE, NUM, DEN, FEATS, U_EARLY = 1, 2, 3, 4, 8, 9, 10, 11
        HOLE_AT = {3 + tile * 15 // 8: tile for tile in range(TILES)}
        HOLE_UNIT_AT = {2 + k * 15 // 4: k for k in range(UNITS)}
        EARLY = UNITS // 2
        EDGES_AT = {38 + k * 7 // 2: k for k in range(UNITS)}
        LEAD = 2
        RAW = 2

        def by_act(g, j):
            return 3 if j % 2 or g == 0 and j % 4 else 2

        BIG = 2.0 ** 64

        def event(c, e):
            return c * EVENTS + (3 + e)

        with Scope(nc, "rows") as t:
            band = t.sbuf("band", [P, 6, SELW])
            xn, x, absent = t.sbuf("xn", [P, W]), t.sbuf("x", [P, W]), t.sbuf("absent", [P, W])
            nf_c = t.sbuf("nf_c", [P, W])
            adj = t.sbuf("adj", [P, 2, UNIT, W])
            holes = t.sbuf("holes", [P, 2, UNIT, W], BF16)
            edges = t.sbuf("edges", [P, TILES, W], BF16)
            raw = t.sbuf("raw", [P, RAW, 3, W], BF16)
            picked = t.sbuf("picked", [P, RING, GROUP, W], BF16)
            u = t.sbuf("u", [P, HEADS, W])
            rho = t.sbuf("rho", [P, 2, W])
            scale_vz = t.sbuf("scale_vz", [P, 2])
            big_gap = t.sbuf("big_gap", [P, TILES, HEADS])
            sums = t.sbuf("sums", [P, GROUP, W])
            zsums = t.sbuf("zsums", [P, 2, W])
            hole_sum = t.sbuf("hole_sum", [P, W])
            scales_i = t.sbuf("scales_i", [P, 2, W])
            total = t.sbuf("total", [P, 2, W])
            misc_ps = t.psum("misc_ps", [P, W])
            sel_ps = t.psum("sel_ps", [P, GROUP, W])
            hole_ps = t.psum("hole_ps", [P, W])
            pair_ps = t.psum("pair_ps", [P, 2, W])
            const_in, chunk_in, x_in, big_ready = map(
                t.sem, ("const_in", "chunk_in", "x_in", "big_ready"))
            adj_in = [t.sem(f"adj_in{i}") for i in range(2)]
            stored = t.sem("stored")
            holes_ready = t.sem("holes_ready")
            holes_used = t.sem("holes_used")
            edges_ready = t.sem("edges_ready")
            raw_ready = t.sem("raw_ready")
            picked_ready = t.sem("picked_ready")
            step_mm = t.sem("step_mm")
            pairs_mm = t.sem("pairs_mm")
            misc_mm = t.sem("misc_mm")
            misc_taken = t.sem("misc_taken")
            rho_ready = t.sem("rho_ready")
            sums_ready = t.sem("sums_ready")
            zsums_ready = t.sem("zsums_ready")
            hole_taken = t.sem("hole_taken")
            bounds_ready, scales_ready = t.sem("bounds_ready"), t.sem("scales_ready")
            final = t.sem("final")
            x_ready = t.sem("x_ready")
            FINAL = 10

            def u_taken(c, g):
                if g == 1:
                    return event(c, NUM)
                return event(c, TAIL_NUM) if not isinstance(c, int) else 1 + 5

            def each_chunk(eng, run, after):
                run(0, False)
                with eng.Fori(1, CHUNKS) as c:
                    run(c, True)
                after(CHUNKS)

            with nc.Block() as block:

                @block.sync
                def _(sp):
                    def load_adj(chunk, c, k):
                        sp.wait_ge(edges_ready, c * UNITS + (k + 1))
                        sp.dma_start(adj[:, k % 2, :, :], adj_dram[chunk, :, (k % UNITS) * UNIT:(k % UNITS + 1) * UNIT, :]
                                     ).then_inc(adj_in[k % 2], 16)

                    def load_last(c):
                        cs = bass.ds((c - 1) * W, W)
                        sp.wait_ge(stored, c * 16)
                        sp.dma_start(x[:, :], x_dram[:, cs]).then_inc(x_in, 16)
                        sp.wait_ge(x_in, c * 32 - 16)
                        sp.dma_start(absent[:, :], absent_dram[:, cs].broadcast_to([P, W])).then_inc(x_in, 16)

                    def store_last(c):
                        sp.wait_ge(x_ready, c + 1)
                        sp.dma_start(x_out[:, bass.ds((c - 1) * W, W)], x[:, :]).then_inc(stored, 16)

                    def run(c, tail):
                        following = (c + 1) % CHUNKS
                        sp.wait_ge(misc_mm, event(c, -2))
                        sp.dma_start(xn[:, :], xn_dram[:, bass.ds(following * W, W)]).then_inc(chunk_in, 16)
                        for k in range(EARLY + 2 if tail else 2, UNITS):
                            load_adj(c, c, k)
                            if k == EARLY + 3 and tail:
                                load_last(c)
                        for k in range(UNITS, UNITS + EARLY + 2):
                            load_adj(following, c, k)
                        if tail:
                            store_last(c)

                    def after(c):
                        load_last(c)
                        store_last(c)
                        sp.wait_ge(stored, CHUNKS * 16 + 16)
                        for i in range(2):
                            sp.wait_ge(adj_in[i], (CHUNKS * UNITS // 2 + EARLY // 2 + 1) * 16)
                        sp.wait_ge(chunk_in, (CHUNKS + 1) * 16)

                    sp.dma_start(band[:, :, :], bands).then_inc(const_in, 16)
                    sp.dma_start(scale_vz[:, :], scales).then_inc(const_in, 16)
                    sp.dma_start(xn[:, :], xn_dram[:, 0:W]).then_inc(chunk_in, 16)
                    load_adj(0, 0, 0)
                    load_adj(0, 0, 1)
                    each_chunk(sp, run, after)

                @block.tensor
                def _(pe):
                    def through_misc(number, w, rhs):
                        pe.wait_ge(misc_taken, number)
                        nc.tensor.matmul(misc_ps[:, :], w, rhs, start=True, stop=True).then_inc(misc_mm, 1)

                    def gather(c, e, g, nd, at):
                        if at == 0:
                            pe.wait_ge(misc_taken, event(c, e))
                        for i in ((0, 1), (2, 3), (4, 5))[at]:
                            if i < GROUP:
                                off = (HEADS - 1 - (GROUP * g + i)) * HD
                                w, rhs = band[0:2 * PART, 2 * (i % 2) + nd, off:off + P], sums[0:2 * PART, i, :]
                            else:
                                off = (HEADS - 1 - (GROUP * g + 2 * (i - GROUP))) * HD
                                w, rhs = band[0:2 * PART, 4 + nd, off:off + P], zsums[0:2 * PART, i - GROUP, :]
                            last = nc.tensor.matmul(misc_ps[:, :], w, rhs, start=i == 0, stop=i == 5)
                        if at == 2:
                            last.then_inc(misc_mm, 1)

                    def gather_when_ready(c, n, e, g, at, nd):
                        if at == 0 and nd == 0:
                            pe.wait_ge(sums_ready, n * GROUP + (GROUP + 2))
                            pe.wait_ge(zsums_ready, n + 2)
                        gather(c, e, g, nd, at)

                    def run(c, tail):
                        for g in range(2):
                            n = c * 2 + g
                            for j in range(TILES):
                                first, final_ = j == 0, j == TILES - 1
                                if first:
                                    pe.wait_ge(zsums_ready, n + 1)
                                if g * TILES + j in HOLE_AT:
                                    tile = HOLE_AT[g * TILES + j]
                                    kb = tile // UNIT
                                    if tile == 0:
                                        pe.wait_ge(hole_taken, c + 1)
                                    pe.wait_ge(holes_ready, c * UNITS + (kb + 1 + UNITS))
                                    for part in range(3):
                                        last = nc.tensor.matmul(
                                            hole_ps[:, :], feats[:, tile, part, :],
                                            holes[:, kb % 2, tile % UNIT, :],
                                            start=tile == 0 and part == 0, stop=tile == TILES - 1 and part == 2)
                                    if tile % UNIT == UNIT - 1:
                                        last.then_inc(holes_used, 1)
                                for tile in range(LEAD + 1) if first else (j + LEAD,):
                                    if tile >= TILES:
                                        break
                                    if g == 0:
                                        pe.wait_ge(edges_ready, c * UNITS + (tile // UNIT + 3))
                                    for pr in range(2):
                                        last = nc.tensor.matmul(
                                            pair_ps[0:2 * PART, pr, :], vz[:, tile, 2 * g + pr, PART:3 * PART],
                                            edges[:, tile, :], start=tile == 0, stop=tile == TILES - 1)
                                    if tile == TILES - 1:
                                        last.then_inc(pairs_mm, 1)
                                pe.wait_ge(picked_ready, n * TILES + (j + 1 + RAW))
                                for i in range(GROUP):
                                    at = (i % 2) * 2 * PART
                                    if first and (g == 1 or tail):
                                        pe.wait_ge(sums_ready, n * GROUP + (i - 1))
                                    last = nc.tensor.matmul(sel_ps[0:2 * PART, i, :],
                                                            vz[:, j, 2 * g + i // 2, at:at + 2 * PART],
                                                            picked[:, j % RING, i, :],
                                                            start=first, stop=final_)
                                last.then_inc(step_mm, 1)
                                if g == 1 or tail:
                                    e = NUM if g == 1 else TAIL_NUM
                                    if j in (3, 4, 5):
                                        gather_when_ready(c, n - 1, e, 1 - g, j - 3, 0)
                                    if j in (8, 9, 10):
                                        gather_when_ready(c, n - 1, e + 1, 1 - g, j - 8, 1)
                                if j == 13:
                                    if g == 0:
                                        through_misc(event(c, P_FEAT), parent_block[:, :], nf_c[:, :])
                                    else:
                                        pe.wait_ge(chunk_in, c * 16 + 32)
                                        through_misc(event(c, FEATS), wt[:, :], xn[:, :])
                                if j in (16, 19, 22, 25):
                                    i = (j - 16) // 3
                                    through_misc(event(c, (U_LATE, U_EARLY)[g] + i),
                                                 parent_rep[:, GROUP * (1 - g) + i, :], nf_c[:, :])

                    def after(c):
                        for nd in range(2):
                            for at in range(3):
                                gather_when_ready(c, c * 2 - 1, TAIL_NUM + nd, 1, at, nd)

                    pe.wait_ge(const_in, 32)
                    pe.wait_ge(chunk_in, 16)
                    through_misc(1, wt[:, :], xn[:, :])
                    for i in range(GROUP):
                        through_misc(2 + i, parent_rep[:, i, :], nf_c[:, :])
                    each_chunk(pe, run, after)

                @block.scalar
                def _(act):
                    def take_feats(number):
                        act.wait_ge(misc_mm, number)
                        nc.scalar.activation(nf_c[:, :], misc_ps[:, :], ACT.Identity,
                                             bias=bcol[:, 0:1]).then_inc(misc_taken, 1)

                    def take_u(number, h):
                        act.wait_ge(misc_mm, number)
                        nc.scalar.activation(u[:, h, :], misc_ps[:, :], ACT.Relu,
                                             bias=cmax[:, h:h + 1]).then_inc(misc_taken, 1)

                    def make_rho(n, g, i):
                        act.wait_ge(sums_ready, n * GROUP + (i + 1))
                        nc.scalar.activation(rho[:, i % 2, :], u[:, GROUP * g + i, :], ACT.Exp,
                                             scale=scale_vz[:, i % 2:i % 2 + 1]).then_inc(rho_ready, 1)

                    def take_pairs(c, n, g):
                        act.wait_ge(pairs_mm, n + 1)
                        before = event(c, DEN) if g == 1 else event(c, TAIL_DEN)
                        if not (isinstance(c, int) and c == 0 and g == 0):
                            act.wait_ge(misc_mm, before)
                        if g == 0 and not (isinstance(c, int) and c == 0):
                            act.wait_ge(final, (c - 1) * FINAL + 5)
                        nc.scalar.copy(zsums[0:2 * PART, :, :],
                                       pair_ps[0:2 * PART, :, :]).then_inc(zsums_ready, 1)

                    def close_group(c, n, g):
                        make_rho(n, g, 2)
                        make_rho(n, g, 3)
                        if g == 1:
                            act.wait_ge(holes_used, c * UNITS + (UNITS + 2))
                            nc.scalar.copy(hole_sum[:, :], hole_ps[:, :]).then_inc(hole_taken, 1)

                    def run(c, tail):
                        for g in range(2):
                            n = c * 2 + g
                            act.wait_ge(misc_taken, u_taken(c, g))
                            for j in range(TILES):
                                act.wait_ge(picked_ready, n * TILES + (j + 1))
                                for i in range(by_act(g, j)):
                                    h = GROUP * (g + 1) - by_act(g, j) + i
                                    last = nc.scalar.activation(raw[:, j % RAW, i, :], u[:, h, :], ACT.Relu,
                                                                bias=big_gap[:, j, h:h + 1], scale=-BIG)
                                last.then_inc(raw_ready, 1)
                                if j == 1:
                                    if g == 1:
                                        close_group(c, n - 1, 0)
                                    elif tail:
                                        close_group(c - 1, n - 1, 1)
                                if g == 1 and j in (9, 14):
                                    nd = (j - 9) // 5
                                    if nd == 0 and tail:
                                        act.wait_ge(x_ready, c + 1)
                                    act.wait_ge(misc_mm, event(c, NUM + nd))
                                    nc.scalar.copy(total[:, nd, :], misc_ps[:, :]).then_inc(misc_taken, 1)
                                if g == 1 and j == 16:
                                    take_feats(event(c, FEATS))
                                if j in (19, 22, 25, 28):
                                    i = (j - 19) // 3
                                    take_u(event(c, (U_LATE, U_EARLY)[g] + i), GROUP * (1 - g) + i)
                                if g == 0 and j == 20:
                                    act.wait_ge(bounds_ready, c + 1)
                                    act.wait_ge(misc_taken, event(c, P_FEAT + 1))
                                    nc.scalar.activation(scales_i[:, 0, :], scales_i[:, 0, :], ACT.Exp,
                                                         scale=0.2).then_inc(scales_ready, 1)
                                    nc.scalar.activation(scales_i[:, 1, :], scales_i[:, 1, :], ACT.Exp,
                                                         scale=-1.0).then_inc(scales_ready, 1)
                                if j in (29, 30):
                                    make_rho(n, g, j - 29)
                            take_pairs(c, n, g)

                    def after(c):
                        close_group(c - 1, c * 2 - 1, 1)

                    act.wait_ge(const_in, 32)
                    act.wait_ge(big_ready, 1)
                    take_feats(1)
                    for i in range(GROUP):
                        take_u(2 + i, i)
                    each_chunk(act, run, after)

                @block.vector
                def _(dve):
                    def make_edges(c, k):
                        dve.wait_ge(adj_in[k % 2], c * (UNITS // 2 * 16) + (k // 2 + 1) * 16)
                        dve.wait_ge(step_mm, c * (2 * TILES) + (k + 1) * UNIT)
                        dve.wait_ge(holes_ready, c * UNITS + (k + 1))
                        nc.vector.tensor_scalar(edges[:, k * UNIT:(k + 1) * UNIT, :], adj[:, k % 2, :, :],
                                                0.0, None, ALU.not_equal).then_inc(edges_ready, 1)

                    def take_sums(c, n, g):
                        dve.wait_ge(step_mm, n * TILES + 2 * TILES)
                        dve.wait_ge(misc_mm, event(c, DEN if g == 1 else TAIL_DEN))
                        for i in range(GROUP):
                            dve.wait_ge(rho_ready, n * GROUP + (i + 1))
                            nc.vector.tensor_tensor(sums[0:2 * PART, i, :], sel_ps[0:2 * PART, i, :],
                                                    rho[0:2 * PART, i % 2, :], ALU.mult).then_inc(sums_ready, 1)

                    def finish(c, part):
                        done = (c - 1) * FINAL
                        both = zsums[:, :, :]
                        if part in (0, 1):
                            if part == 0:
                                dve.wait_ge(misc_taken, event(c - 1, DEN + 1))
                            dve.wait_ge(misc_mm, event(c, TAIL_NUM + part))
                            nc.vector.tensor_tensor(total[:, part, :], total[:, part, :], misc_ps[:, :],
                                                    ALU.add).then_inc(misc_taken, 1)
                        elif part == 2:
                            dve.wait_ge(misc_taken, event(c, TAIL_DEN + 1))
                            dve.wait_ge(scales_ready, c * 2)
                            dve.wait_ge(x_in, c * 32)
                            for nd in range(2):
                                nc.vector.tensor_tensor(total[:, nd, :], total[:, nd, :], scales_i[:, 0, :],
                                                        ALU.mult).then_inc(final, 1)
                            nc.vector.tensor_tensor(both[:, 1, :], absent[:, :], scales_i[:, 1, :],
                                                    ALU.mult).then_inc(final, 1)
                        elif part == 3:
                            dve.wait_ge(hole_taken, c + 1)
                            nc.vector.tensor_tensor(both[:, 0, :], hole_sum[:, :], scales_i[:, 1, :],
                                                    ALU.mult).then_inc(final, 1)
                        elif part == 4:
                            dve.wait_ge(final, done + 4)
                            nc.vector.tensor_tensor(total[:, :, :], total[:, :, :], both, ALU.add).then_inc(final, 1)
                        elif part in (5, 6, 7, 8):
                            quarter = slice((part - 5) * (W // 4), (part - 4) * (W // 4))
                            dve.wait_ge(final, done + 5)
                            nc.vector.reciprocal(total[:, 1, quarter], total[:, 1, quarter]).then_inc(final, 1)
                        elif part == 9:
                            dve.wait_ge(final, done + 9)
                            nc.vector.tensor_tensor(total[:, 0, :], total[:, 0, :], total[:, 1, :],
                                                    ALU.mult).then_inc(final, 1)
                        else:
                            dve.wait_ge(final, done + 10)
                            nc.vector.tensor_tensor(x[:, :], x[:, :], total[:, 0, :], ALU.add).then_inc(x_ready, 1)

                    def run(c, tail):
                        for g in range(2):
                            n = c * 2 + g
                            dve.wait_ge(misc_taken, u_taken(c, g))
                            for j in range(TILES):
                                if g == 0 and j % UNIT == 0 and not tail:
                                    if j == 0:
                                        make_edges(c, 0)
                                    if j // UNIT + 1 < UNITS:
                                        make_edges(c, j // UNIT + 1)
                                if g == 0 and tail and 2 * TILES + j in EDGES_AT:
                                    make_edges(c, EDGES_AT[2 * TILES + j])
                                if g == 1 and TILES + j in EDGES_AT:
                                    make_edges(c + 1, EDGES_AT[TILES + j])
                                if g == 0 and j % UNIT == 0:
                                    dve.wait_ge(edges_ready, c * UNITS + (j // UNIT + 3))
                                dve.wait_ge(step_mm, n * TILES + (j + TILES - RING + 1))
                                mine = GROUP - by_act(g, j)
                                for i in range(mine):
                                    h = GROUP * g + i
                                    nc.vector.scalar_tensor_tensor(
                                        out=picked[:, j % RING, i, :], in0=u[:, h, :], scalar=gap[:, j, h:h + 1],
                                        in1=edges[:, j, :], op0=ALU.is_lt, op1=ALU.mult)
                                dve.wait_ge(raw_ready, n * TILES + (j + 1))
                                nc.vector.tensor_tensor(
                                    picked[:, j % RING, mine:GROUP, :], raw[:, j % RAW, 0:by_act(g, j), :],
                                    edges[:, j:j + 1, :].broadcast_to([P, by_act(g, j), W]),
                                    ALU.min).then_inc(picked_ready, 1)
                                if g * TILES + j in HOLE_UNIT_AT:
                                    k = HOLE_UNIT_AT[g * TILES + j]
                                    dve.wait_ge(edges_ready, c * UNITS + (k + 3))
                                    dve.wait_ge(holes_used, c * UNITS + (k + 1))
                                    nc.vector.tensor_scalar(holes[:, k % 2, :, :], edges[:, k * UNIT:(k + 1) * UNIT, :],
                                                            0.0, None, ALU.is_equal).then_inc(holes_ready, 1)
                                if j == 1:
                                    if g == 1:
                                        take_sums(c, n - 1, 0)
                                    elif tail:
                                        take_sums(c - 1, n - 1, 1)
                                if g == 0 and tail and j in (9, 14, 15, 16, 18):
                                    finish(c, (9, 14, 15, 16, 18).index(j))
                                if g == 1 and tail and 3 <= j <= 8:
                                    finish(c, 5 + j - 3)
                                if g == 0 and j == 17:
                                    if tail:
                                        dve.wait_ge(final, (c - 1) * FINAL + 4)
                                    dve.wait_ge(misc_mm, event(c, P_FEAT))
                                    nc.vector.tensor_scalar(scales_i[:, 0, :], misc_ps[:, :], cmax_col[:, 0:1], 0.0,
                                                            ALU.add, ALU.min).then_inc(bounds_ready, 1)
                                    nc.vector.tensor_scalar(scales_i[:, 1, :], misc_ps[:, :], cmax_col[:, 0:1], 0.0,
                                                            ALU.add, ALU.max).then_inc(misc_taken, 1)

                    def after(c):
                        take_sums(c - 1, c * 2 - 1, 1)
                        for part in range(11):
                            finish(c, part)

                    for one, start in ((x_ready, 1), (hole_taken, 1), (misc_taken, 1), (zsums_ready, 1), (sums_ready, 2),
                                       (picked_ready, RAW), (stored, 16), (holes_used, 2), (holes_ready, UNITS), (edges_ready, 2),
                                       (step_mm, TILES)):
                        dve.sem_inc(one, start)
                    nc.vector.tensor_scalar(big_gap[:, :, :], gap[:, :, :], BIG, None, ALU.mult).then_inc(big_ready, 1)
                    each_chunk(dve, run, after)


def network(nc, a, out):
    def scratch(name, shape):
        return nc.dram_tensor(name, shape, F32, kind="Internal").ap()

    x2, x3, xn2 = (scratch(name, [P, N]) for name in ("x2", "x3", "xn2"))
    gates = [scratch(f"gates{i}", [8, N]) for i in range(2)]
    absent = scratch("absent", [1, N])
    widths0, widths1 = [P] * 4, [P, P, 85]

    with Scope(nc, "front") as s:
        x, xn = s.sbuf("x", [P, N]), s.sbuf("xn", [P, N])
        layer_norm(nc, "norm0", x, xn, a["row_of"], x_from=a["x_t"])
        filtered_graph(nc, x, xn, a["x_t"], a["adj"], a["w_proj"], a["b_proj"], a["w_gcn"], a["b_gcn"], absent,
                       a["adj_rows"], a["identity"])
        with Scope(nc, "experts0") as w:
            weights = ExpertWeights(w, True, widths0)
            with Scope(nc, "staged0") as st:
                weights.stage(st, a["up0"], a["down0"], a["bias_up0"], a["bias_down0"])
                layer_norm(nc, "norm1", x, xn, a["row_of"], ahead=weights.loads)
                route(nc, "route0", xn, a["w_router0"], a["identity"], gates[0], None, weights)
            experts(nc, "ffn0", x, xn, gates[0], weights, True, widths0)
        layer_norm(nc, "norm2", x, xn, a["row_of"], x_to=x2, xn_to=xn2)
    attention(nc, x2, xn2, a["adj"], absent, a["w_attn"], a["b_attn"], a["a_parent"], a["a_child"],
              a["head_cols"], a["head_blocks"], a["bands"], a["scales"], a["identity"], x3)
    with Scope(nc, "back") as s:
        x, xn = s.sbuf("x", [P, N]), s.sbuf("xn", [P, N])
        weights = ExpertWeights(s, False, widths1)
        with Scope(nc, "staged1") as st:
            weights.stage(st, a["up1"], a["down1"])
            layer_norm(nc, "norm3", x, xn, a["row_of"], x_from=x3, ahead=weights.loads)
            route(nc, "route1", xn, a["w_router1"], a["identity"], gates[1], 1e-9, weights)
        experts(nc, "ffn1", x, xn, gates[1], weights, False, widths1, x_out=out)


def kernel(**inputs):
    import numpy as np
    import concourse.bacc as bacc
    from concourse.bass_utils import run_bass_kernel_spmd as run

    v = {k: np.asarray(t) for k, t in inputs.items()}
    heads = np.arange(P) // HD
    bands = np.zeros((P, 6, SELW), np.float32)
    for part in range(3):
        for blk in range(2):
            r = blk * PART + part * COLS
            for kind in range(3):
                sign = 1.0 if kind == 2 or (kind == 0) == (blk == 0) else -1.0
                at = P - HD + (HD if kind == 2 and blk == 1 else 0)
                for d in range(HD):
                    bands[r + d, 2 * kind, at + d] = sign
                    bands[r + HD, 2 * kind + 1, at + d] = sign
    scales = np.zeros((P, 2), np.float32)
    scales[0:PART, 0] = -0.8
    scales[PART:2 * PART, 1] = -0.8

    def pad_rows(w, rows):
        return np.concatenate([w, np.zeros((rows - w.shape[0],) + w.shape[1:], w.dtype)], 0)

    hid1 = v["L1_ffn_w1"].shape[1]
    up0 = np.concatenate([v["L0_ffn_W1s"][None], v["L0_ffn_W1p"]], 0)
    down0 = np.concatenate([v["L0_ffn_W2s"][None], v["L0_ffn_W2p"]], 0)
    b_up0 = np.concatenate([v["L0_ffn_b1s"][None], v["L0_ffn_b1p"]], 0)
    b_down0 = np.concatenate([v["L0_ffn_b2s"][None], v["L0_ffn_b2p"]], 0)
    down1 = np.stack([pad_rows(w.T, 3 * P) for w in v["L1_ffn_w2"]])
    arrays = {
        "x_t": v["x"].T,
        "adj": v["adj"].T.reshape(TILES, P, CHUNKS, W).transpose(2, 1, 0, 3),
        "adj_rows": v["adj"],
        "w_proj": v["L0_gnn_W_proj"], "b_proj": v["L0_gnn_b_proj"][:, None],
        "w_gcn": v["L0_gnn_W_gcn"], "b_gcn": v["L0_gnn_b_gcn"][:, None],
        "w_router0": v["L0_ffn_Wr"],
        "up0": up0.transpose(1, 0, 2)[:, None], "down0": down0.reshape(9, 4, P, P).transpose(2, 0, 1, 3),
        "bias_up0": b_up0.reshape(9, 4, P).transpose(2, 0, 1), "bias_down0": b_down0.T,
        "w_attn": v["L1_gnn_W"].T, "b_attn": v["L1_gnn_b"][:, None],
        "a_parent": v["L1_gnn_a"][:, :HD].reshape(P, 1), "a_child": v["L1_gnn_a"][:, HD:].reshape(P, 1),
        "head_cols": (heads[:, None] == np.arange(HEADS)[None]).astype(np.float32),
        "head_blocks": (heads[:, None] == heads[None]).astype(np.float32),
        "bands": bands, "scales": scales, "identity": np.eye(P, dtype=np.float32),
        "row_of": np.repeat(np.eye(CHUNKS, dtype=np.float32)[:, :, None], P, 2),
        "w_router1": v["L1_ffn_router_w"].T,
        "up1": np.stack([v["L1_ffn_w1"], v["L1_ffn_w3"]]).transpose(3, 0, 1, 2),
        "down1": down1.reshape(8, 3, P, P).transpose(2, 0, 1, 3),
    }
    nc = bacc.Bacc("TRN2", target_bir_lowering=False, num_devices=1)
    data, a = {}, {}
    for name, t in arrays.items():
        data[name] = np.ascontiguousarray(t)
        a[name] = nc.dram_tensor(name, data[name].shape, mybir.dt.from_np(data[name].dtype),
                                 kind="ExternalInput").ap()
    out = nc.dram_tensor("out_t", [P, N], F32, kind="ExternalOutput").ap()
    network(nc, a, out)
    r = run(nc, [data], core_ids=[0])
    return np.ascontiguousarray(r.results[0]["out_t"].T)
```
